# Optimizing a Trainium2 kernel written in Bass

```python
import numpy as np
import jax
import jax.numpy as jnp

def _softmax(x, axis=-1):
    return jax.nn.softmax(x, axis=axis)

def _gelu(x):
    return jax.nn.gelu(x, approximate=True)

def _silu(x):
    return jax.nn.silu(x)

def _sigmoid(x):
    return jax.nn.sigmoid(x)

def _layernorm(x, axis=-1, eps=1e-05):
    m = jnp.mean(x, axis=axis, keepdims=True)
    v = jnp.var(x, axis=axis, keepdims=True)
    return (x - m) / jnp.sqrt(v + eps)

def _scatter_add(tgt, idx, src, axis=0):
    return tgt.at[idx].add(src)

def _segment_sum(src, seg, n):
    return jax.ops.segment_sum(src, seg, n)
kernel_name = 'mk_adj_preln_d2_adj_r2_2b82de'

def setup_inputs(seed: int=0):
    np.random.seed(seed)
    _w = jnp.asarray

    def _rec_inputs():
        import jax
        import jax.numpy as jnp
        _gk = jax.random.key(seed)
        x = -0.0005963 + 1.001 * jax.random.normal(jax.random.fold_in(_gk, 1), (2048, 256), jnp.float32)
        _w = (1.0 + jnp.arange(2048, dtype=jnp.float32)) ** (-0.5)
        _w = _w / _w.mean()
        _pij = jnp.clip(0.000976562 * _w[:, None] * _w[None, :], 0.0, 1.0)
        _a = jax.random.uniform(jax.random.fold_in(_gk, 2), (2048, 2048)) < _pij
        _af = _a.astype(jnp.float32)
        adj = _af
        return (x, adj)
    x, adj = _rec_inputs()

    def _L0_gnn_setup():
        import jax, jax.numpy as jnp
        import numpy as np
        N = 3072
        D_IN = 256
        D_OUT = 256
        DENSITY = 0.005
        key = jax.random.key(seed)
        ks = jax.random.split(key, 12)
        x = jax.random.normal(ks[0], (N, D_IN), dtype=jnp.float32)
        adj_a = (jax.random.uniform(ks[1], (N, N)) < DENSITY).astype(jnp.float32)
        adj_b = (jax.random.uniform(ks[2], (N, N)) < DENSITY).astype(jnp.float32)
        W_sa = jax.random.normal(ks[3], (D_IN, D_OUT), dtype=jnp.float32) * (1.414 / np.sqrt(D_IN + D_OUT))
        a_sa = jax.random.normal(ks[4], (1, 2 * D_OUT), dtype=jnp.float32) * (1.414 / np.sqrt(1 + 2 * D_OUT))
        stdv = 1.0 / np.sqrt(D_OUT)
        W_gcnb = jax.random.uniform(ks[5], (D_IN, D_OUT), minval=-stdv, maxval=stdv, dtype=jnp.float32)
        b_gcnb = jax.random.uniform(ks[6], (D_OUT,), minval=-stdv, maxval=stdv, dtype=jnp.float32)
        s = 1.0 / np.sqrt(2 * D_IN)
        Wa = jax.random.uniform(ks[7], (1, 2 * D_IN), minval=-s, maxval=s, dtype=jnp.float32)
        ba = jax.random.uniform(ks[8], (1,), minval=-s, maxval=s, dtype=jnp.float32)
        Wb = jax.random.uniform(ks[9], (1, 2 * D_IN), minval=-s, maxval=s, dtype=jnp.float32)
        bb = jax.random.uniform(ks[10], (1,), minval=-s, maxval=s, dtype=jnp.float32)
        return {'x': x, 'adj_a': adj_a, 'adj_b': adj_b, 'W_sa': W_sa, 'a_sa': a_sa, 'W_gcnb': W_gcnb, 'b_gcnb': b_gcnb, 'Wa': Wa, 'ba': ba, 'Wb': Wb, 'bb': bb}
    _L0_gnn_all = _L0_gnn_setup()
    _L0_gnn_in = {k: v for k, v in _L0_gnn_all.items() if k in ('W_sa', 'a_sa', 'W_gcnb', 'b_gcnb', 'Wa', 'ba', 'Wb', 'bb')}
    del _L0_gnn_all

    def _L1_gnn_setup():
        import jax, jax.numpy as jnp
        import numpy as np
        N = 2048
        DIM_IN = 256
        DIM_Q = 256
        DIM_K = 256
        N_GRAPHS = 32
        key = jax.random.key(seed)
        ks = jax.random.split(key, 9)
        x = jax.random.normal(ks[0], (N, DIM_IN), dtype=jnp.float32)
        b = jax.random.normal(ks[1], (N, N), dtype=jnp.float32)
        edge_encoding = jax.random.normal(ks[2], (N, N), dtype=jnp.float32)
        ptr = jnp.arange(N_GRAPHS + 1, dtype=jnp.int64) * (N // N_GRAPHS)
        s_in = 1.0 / np.sqrt(DIM_IN)
        Wq = jax.random.normal(ks[3], (DIM_Q, DIM_IN), dtype=jnp.float32) * s_in
        bq = jnp.zeros((DIM_Q,), dtype=jnp.float32)
        Wk = jax.random.normal(ks[4], (DIM_K, DIM_IN), dtype=jnp.float32) * s_in
        bk = jnp.zeros((DIM_K,), dtype=jnp.float32)
        Wv = jax.random.normal(ks[5], (DIM_K, DIM_IN), dtype=jnp.float32) * s_in
        bv = jnp.zeros((DIM_K,), dtype=jnp.float32)
        return {'x': x, 'b': b, 'edge_encoding': edge_encoding, 'ptr': ptr, 'Wq': Wq, 'bq': bq, 'Wk': Wk, 'bk': bk, 'Wv': Wv, 'bv': bv}
    _L1_gnn_all = _L1_gnn_setup()
    _L1_gnn_in = {k: v for k, v in _L1_gnn_all.items() if k in ('ptr', 'Wq', 'bq', 'Wk', 'bk', 'Wv', 'bv')}
    del _L1_gnn_all
    return {'x': x, 'adj': adj, 'L0_gnn_W_sa': _L0_gnn_in['W_sa'], 'L0_gnn_a_sa': _L0_gnn_in['a_sa'], 'L0_gnn_W_gcnb': _L0_gnn_in['W_gcnb'], 'L0_gnn_b_gcnb': _L0_gnn_in['b_gcnb'], 'L0_gnn_Wa': _L0_gnn_in['Wa'], 'L0_gnn_ba': _L0_gnn_in['ba'], 'L0_gnn_Wb': _L0_gnn_in['Wb'], 'L0_gnn_bb': _L0_gnn_in['bb'], 'L1_gnn_ptr': _L1_gnn_in['ptr'], 'L1_gnn_Wq': _L1_gnn_in['Wq'], 'L1_gnn_bq': _L1_gnn_in['bq'], 'L1_gnn_Wk': _L1_gnn_in['Wk'], 'L1_gnn_bk': _L1_gnn_in['bk'], 'L1_gnn_Wv': _L1_gnn_in['Wv'], 'L1_gnn_bv': _L1_gnn_in['bv']}

def reference(x, adj, L0_gnn_W_sa, L0_gnn_a_sa, L0_gnn_W_gcnb, L0_gnn_b_gcnb, L0_gnn_Wa, L0_gnn_ba, L0_gnn_Wb, L0_gnn_bb, L1_gnn_ptr, L1_gnn_Wq, L1_gnn_bq, L1_gnn_Wk, L1_gnn_bk, L1_gnn_Wv, L1_gnn_bv):
    import jax
    import jax.numpy as jnp

    def _L0_gnn_ref(x, adj_a, adj_b, W_sa, a_sa, W_gcnb, b_gcnb, Wa, ba, Wb, bb):
        import jax, jax.numpy as jnp
        import numpy as np
        N = 3072
        D_IN = 256
        D_OUT = 256
        DENSITY = 0.005
        type_sum_a = adj_a @ x
        type_sum_b = adj_b @ x
        attn_a = jax.nn.sigmoid(jnp.concatenate([type_sum_a, x], axis=1) @ Wa.T + ba)
        attn_b = jax.nn.sigmoid(jnp.concatenate([type_sum_b, x], axis=1) @ Wb.T + bb)
        h = x @ W_sa
        Hd = h.shape[1]
        s_left = h @ a_sa[0, :Hd]
        s_right = h @ a_sa[0, Hd:]
        scores = s_left[:, None] + s_right[None, :]
        e = jnp.where(adj_a != 0, jnp.exp(-jax.nn.leaky_relu(scores, 0.01)), 0.0)
        attn = e / (jnp.sum(e, axis=1, keepdims=True) + 1e-05)
        x_a = attn @ h
        x_b = adj_b @ (x @ W_gcnb) + b_gcnb
        return jax.nn.sigmoid(attn_a * x_a + attn_b * x_b)

    def _L1_gnn_ref(x, b, edge_encoding, ptr, Wq, bq, Wk, bk, Wv, bv):
        import jax, jax.numpy as jnp
        import numpy as np
        N = 2048
        DIM_IN = 256
        DIM_Q = 256
        DIM_K = 256
        N_GRAPHS = 32
        n = x.shape[0]
        graph_id = jnp.searchsorted(ptr, jnp.arange(n), side='right') - 1
        mask = graph_id[:, None] == graph_id[None, :]
        query = x @ Wq.T + bq
        key = x @ Wk.T + bk
        value = x @ Wv.T + bv
        scale = 1.0 / jnp.sqrt(jnp.float32(query.shape[-1]))
        a = jnp.where(mask, query @ key.T * scale, 0.0)
        scores = (a + b + edge_encoding) * jnp.where(mask, 1.0, -1000000.0)
        softmax = jax.nn.softmax(scores, axis=-1) * mask
        return softmax @ value
    h = jnp.maximum(_layernorm(x, axis=-1), 0.0)
    x = x + _L0_gnn_ref(h, adj, adj, L0_gnn_W_sa, L0_gnn_a_sa, L0_gnn_W_gcnb, L0_gnn_b_gcnb, L0_gnn_Wa, L0_gnn_ba, L0_gnn_Wb, L0_gnn_bb)
    h = jnp.maximum(_layernorm(x, axis=-1), 0.0)
    x = x + _L1_gnn_ref(h, adj, adj, L1_gnn_ptr, L1_gnn_Wq, L1_gnn_bq, L1_gnn_Wk, L1_gnn_bk, L1_gnn_Wv, L1_gnn_bv)
    return x

_drawn_inputs = setup_inputs


def setup_inputs(seed=0):
    import zlib

    import numpy as np

    out = dict(_drawn_inputs(seed))
    spreads = {'L1_gnn_bq': (0.0, 0.8), 'L1_gnn_bk': (0.0, 0.8), 'L1_gnn_bv': (0.0, 0.8)}
    factors = {'L0_gnn_a_sa': 8.0,
     'L0_gnn_b_gcnb': 8.0,
     'L0_gnn_Wa': 5.227,
     'L1_gnn_Wq': 8.0,
     'L1_gnn_Wk': 8.0,
     'L1_gnn_Wv': 3.74}
    for name, (base, spread) in spreads.items():
        noise = np.random.default_rng([zlib.crc32(name.encode()), seed]).standard_normal(out[name].shape)
        drawn = base * np.exp(spread * noise) if base else spread * noise
        out[name] = jnp.asarray(drawn.astype(out[name].dtype))
    for name, factor in factors.items():
        out[name] = (out[name] * factor).astype(out[name].dtype)
    return out
```

```python
from contextlib import ExitStack

import concourse.bass as bass
from concourse import mybir

P = 128
F32 = mybir.dt.float32
F16 = mybir.dt.float16
BF16 = mybir.dt.bfloat16
I32 = mybir.dt.int32
ALU = mybir.AluOpType
ACT = mybir.ActivationFunctionType
AX = mybir.AxisListType.X

SLOPE = 0.01
LN_EPS = 1e-5
ATTN_EPS = 1e-5
OFF = -1e6
H_SCALE = 2.0 ** 11
E_SCALE = 2.0 ** 15
BIG = 1e30


def two_graph_layers(nc, x, adj, adj_t, W_sa, a_sa, W_gcnb, b_gcnb, gate_w, ba, bb, ptr,
                     Wq, Wk, WvT, bq_bk, bv, out):
    N, D = x.shape
    NP = ptr.shape[0]
    NT = N // P
    KT = D // P
    CT = 4
    NC = NT // CT
    CW = CT * P
    RING = 4
    PAIRS = NT // 2
    E1 = D + 2
    CHUNK = NT * CW
    PW = 2 * CW
    N_WEIGHTS = 14
    QK_SCALE = float(D) ** -0.5

    tb_dram = nc.dram_tensor("neighbour_sums", (NT, P, 2 * D), F32, kind="Internal").ap()

    with ExitStack() as ctx:
        def sb(name, shape, dt=F32):
            return ctx.enter_context(nc.sbuf_tensor(name, shape, dt))

        def sem(name):
            return ctx.enter_context(nc.semaphore(name))

        adjt = sb("adjt", [P, 2 * CHUNK])
        nat = sb("nat", [P, 2 * N])
        h16 = sb("h16", [P, NT, 2, D], F16)
        hd16 = sb("hd16", [P, NT, 2, E1], F16)
        s_row = sb("s_row", [P, N])
        e_raw = sb("e_raw", [P, 2 * PW])
        e_mask = sb("e_mask", [P, 2 * PW])
        e_hi = sb("e_hi", [P, RING * PW], F16)
        e_lo = sb("e_lo", [P, RING * PW], F16)
        tb_out = sb("tb_out", [P, CT * 2 * D])
        junk = sb("junk", [P, N], BF16)
        gid_row = sb("gid_row", [P, N], BF16)
        big = sb("big", [P, P])
        ident = sb("ident", [P, P])
        ones = sb("ones", [P, P])
        ones_b = sb("ones_b", [P, P], BF16)
        cmp_ptr = junk[0:NP, :]
        iota_n = s_row[0:NP, :]

        w_sa = sb("w_sa", [P, KT, D])
        w_b = sb("w_b", [P, KT, E1])
        w_v = sb("w_v", [P, KT, D + 1])
        w_qk = sb("w_qk", [P, KT, D])
        w4 = sb("w4", [P, KT, 4])
        wl_wide = sb("wl_wide", [P, KT, P])
        a_row = sb("a_row", [P, 2, D])
        bg_row = sb("bg_row", [P, D])
        bv_row = sb("bv_row", [P, D + 1])
        gate_bias = sb("gate_bias", [P, 2])
        bqk_col = sb("bqk_col", [P, KT, 2])
        bq_wide = sb("bq_wide", [P, KT, P])
        u_col = sb("u_col", [P, KT])
        ptr_i = sb("ptr_i", [NP, 1], I32)
        ptr_f = sb("ptr_f", [NP, 1])
        gid_col = sb("gid_col", [P, NT])
        hc = sb("hc", [P, NT, 4])
        st6 = sb("st6", [P, NT, 6])
        mv = sb("mv", [P, NT, 2])
        var_e = sb("var_e", [P, NT])
        half_neg = sb("half_neg", [P, NT])
        rstd = sb("rstd", [P, NT])
        ln_b = sb("ln_b", [P, NT])
        nbias = sb("nbias", [P, NT])
        dp = sb("dp", [P, NT])
        dp_s = sb("dp_s", [P, NT])
        es = sb("es", [P, NT])
        rm = sb("rm", [P, 4])
        den = sb("den", [P, CT])
        rden = sb("rden", [P, CT])
        mn = sb("mn", [P, NT])
        mn_b = sb("mn_b", [P, NT])
        z_off = sb("z_off", [P, NT])
        wq = e_mask[:, 0:KT * D].rearrange("p (k d) -> p k d", k=KT)
        wk = e_mask[:, PW:PW + KT * D].rearrange("p (k d) -> p k d", k=KT)

        xs = adjt[:, CHUNK:CHUNK + NT * D].rearrange("p (t d) -> p t d", d=D)
        h = adjt[:, CHUNK + NT * D:2 * CHUNK].rearrange("p (t d) -> p t d", d=D)
        hT = nat[:, :].rearrange("p (k n) -> p k n", k=KT)

        x1_all = adjt[:, 0:NT * D]
        h1T_all = adjt[:, NT * D:2 * NT * D].rearrange("p (k n) -> p k n", k=KT)
        v_all = adjt[:, 2 * NT * D:3 * NT * D]
        c_all = adjt[:, 3 * NT * D:3 * NT * D + NT]
        adj_row, score_row = nat[:, 0:N], nat[:, N:2 * N]
        mask_row = s_row
        fac_row = e_hi[:, :].bitcast(F32)
        prob_row = e_lo[:, :].bitcast(F32)
        probT_row = e_raw

        tb_in = sb("tb_in", [P, 2, 2 * D])
        x_in = sb("x_in", [P, 2, D])
        adj_diag = sb("adj_diag", [P, 2, P])
        tbT = e_raw[:, 0:1024].rearrange("p (q n) -> p q n", q=2)
        xbb, xag, u, th = (e_raw[:, 1024 + D * n:1024 + D * (n + 1)] for n in range(4))
        h1, h1T, gT, x_half = (e_mask[:, 512 * n:512 * n + 512].rearrange("p (q n) -> p q n", q=2)
                               for n in range(4))
        v_sb = sb("v_sb", [P, 2, D + 2])
        mask = sb("mask", [P, 2, P])
        fac = sb("fac", [P, 2, P])
        sc1 = sb("sc1", [P, P])
        sc2 = sb("sc2", [P, P])
        sc3 = sb("sc3", [P, P])
        prob = sb("prob", [P, P])
        probm = sb("probm", [P, 2, P])
        pT = sb("pT", [P, 2, P])
        o_sb = sb("o_sb", [P, 2, D])
        gz = sb("gz", [P, 2])
        gt = sb("gt", [P, 2])
        gates = sb("gates", [P, 2, 2])
        st6b = sb("st6b", [P, 6])
        mvb = sb("mvb", [P, 2])
        veb = sb("veb", [P, 1])
        rs_all = sb("rs_all", [P, NT])
        nb_all = sb("nb_all", [P, NT])
        diff = sb("diff", [1, NT])
        general = sb("general", [1, 1], I32)
        neg_mw = sb("neg_mw", [P, 1])
        neg_m = sb("neg_m", [P, 2])
        zw = sb("zw", [P, 1])
        fo = sb("fo", [P, 1])
        zs = sb("zs", [P, 1])
        rz = sb("rz", [P, 2])

        bank = [ctx.enter_context(nc.psum_tensor(f"bank{b}", [P, 512], F32)) for b in range(8)]
        TB_T, X_A, X_B, H_T, G_T, V_S, S_S, PV = bank
        P_T = PV[:, D:D + P]

        x_loaded = [sem(f"x_loaded{g}") for g in range(CT)]
        weights_loaded = sem("weights_loaded")
        consts_made = sem("consts_made")
        iota_made = sem("iota_made")
        ptr_made = sem("ptr_made")
        cmp_made = sem("cmp_made")
        gid_summed = sem("gid_summed")
        gid_kept = sem("gid_kept")
        w_made = sem("w_made")
        wide_made = sem("wide_made")
        qk_summed = sem("qk_summed")
        qk_kept = sem("qk_kept")
        stats_made = sem("stats_made")
        moments_made = sem("moments_made")
        var_made = sem("var_made")
        rstd_made = sem("rstd_made")
        lnb_made = sem("lnb_made")
        h_made = sem("h_made")
        h_turned = sem("h_turned")
        hT_kept_a = sem("hT_kept_a")
        hT_kept_v = sem("hT_kept_v")
        cols_summed = sem("cols_summed")
        cols_kept = sem("cols_kept")
        rows_summed = sem("rows_summed")
        rows_kept = sem("rows_kept")
        rmin_v = sem("rmin_v")
        rmin_t = sem("rmin_t")
        bias_made = sem("bias_made")
        factors_made = sem("factors_made")
        h_hi_made = sem("h_hi_made")
        h_lo_made = sem("h_lo_made")
        hd_made = sem("hd_made")
        hd_hi_made = sem("hd_hi_made")
        hd_lo_made = sem("hd_lo_made")
        dp_scaled = sem("dp_scaled")
        adjt_loaded = [sem(f"adjt_loaded{m}") for m in range(CT)]
        nat_loaded = [sem(f"nat_loaded{q}") for q in range(2)]
        raw_ready = sem("raw_ready")
        mask_ready = sem("mask_ready")
        hi_ready = sem("hi_ready")
        lo_ready = sem("lo_ready")
        slot_free = sem("slot_free")
        big_set = sem("big_set")
        least_ready = sem("least_ready")
        off_bias = sem("off_bias")
        off_done = sem("off_done")
        b_summed = sem("b_summed")
        b_kept = sem("b_kept")
        t_kept = sem("t_kept")
        den_ready = sem("den_ready")
        rden_ready = sem("rden_ready")
        tb_stored = [sem(f"tb_stored{r}") for r in range(CT)]
        passed = sem("passed")
        tb_loaded = [sem(f"tb_loaded{q}") for q in range(2)]
        tb_turned = sem("tb_turned")
        tbT_kept = sem("tbT_kept")
        x_read = [sem(f"x_read{q}") for q in range(2)]
        b_mix_summed = sem("b_mix_summed")
        mix_summed = sem("mix_summed")
        z_ready = sem("z_ready")
        xbb_ready = sem("xbb_ready")
        tz_ready = sem("tz_ready")
        gates_ready = sem("gates_ready")
        xag_ready = sem("xag_ready")
        u_ready = sem("u_ready")
        th_ready = sem("th_ready")
        half_ready = sem("half_ready")
        x1_ready = sem("x1_ready")
        st_ready = sem("st_ready")
        mv_ready = sem("mv_ready")
        ve_ready = sem("ve_ready")
        rs_ready = sem("rs_ready")
        nb_ready = sem("nb_ready")
        h1_ready = sem("h1_ready")
        h1_turned = sem("h1_turned")
        h1T_kept = sem("h1T_kept")
        g_summed = sem("g_summed")
        v_summed = sem("v_summed")
        g_kept = sem("g_kept")
        v_kept = sem("v_kept")
        diag_loaded = [sem(f"diag_loaded{q}") for q in range(2)]
        msk_ready = sem("msk_ready")
        fac_ready = sem("fac_ready")
        s_summed = sem("s_summed")
        s1_ready = sem("s1_ready")
        s2_ready = sem("s2_ready")
        s3_ready = sem("s3_ready")
        mw_ready = sem("mw_ready")
        m_ready = sem("m_ready")
        p_ready = sem("p_ready")
        fo_ready = sem("fo_ready")
        pm_ready = sem("pm_ready")
        z_sum = sem("z_sum")
        rz_ready = sem("rz_ready")
        p_turned = sem("p_turned")
        pT_kept = sem("pT_kept")
        pv_summed = sem("pv_summed")
        o_ready = sem("o_ready")
        o_stored = [sem(f"o_stored{q}") for q in range(2)]

        flag_made = sem("flag_made")
        all_h1 = sem("all_h1")
        all_h1_turned = sem("all_h1_turned")
        all_h1T_kept = sem("all_h1T_kept")
        all_v_summed = sem("all_v_summed")
        all_v_kept = sem("all_v_kept")
        row_loaded = sem("row_loaded")
        row_g_summed = sem("row_g_summed")
        row_g_kept = sem("row_g_kept")
        row_s_summed = sem("row_s_summed")
        row_masked = sem("row_masked")
        row_scored = sem("row_scored")
        row_m_ready = sem("row_m_ready")
        row_p_ready = sem("row_p_ready")
        row_pm_ready = sem("row_pm_ready")
        row_p_turned = sem("row_p_turned")
        row_pT_kept = sem("row_pT_kept")
        row_pv_summed = sem("row_pv_summed")
        row_o_ready = sem("row_o_ready")
        row_stored = sem("row_stored")

        block = ctx.enter_context(nc.Block())

        def wait(eng, signal, value):
            if not isinstance(value, int) or value > 0:
                eng.wait_ge(signal, value)

        def apart(eng):
            eng.sem_inc(passed, 1)

        def if_general(eng):
            eng.wait_ge(o_ready, NT)
            eng.wait_ge(flag_made, 3)
            return eng.If(eng.value_load(general[0:1, 0:1], min_val=0, max_val=1) > 0)

        LEAD, LAG = 1, 2

        def turns(eng, turn):
            first = 2 * LAG
            last = (NT - LEAD) // 2 * 2

            def written_out(t):
                turn(lambda d: (t + d, (t + d) // 2, (t + d) % 2) if 0 <= t + d < NT else None)

            for t in range(-LEAD, first):
                written_out(t)
            with eng.Fori(first // 2, last // 2) as half:
                for q in range(2):
                    turn(lambda d, q=q: (2 * half + (q + d), half + (q + d) // 2, (q + d) % 2))
            for t in range(last, NT + LAG):
                written_out(t)

        @block.sync
        def _(eng):
            def load_adjt(k, m):
                base = (k % 2) * CHUNK + CT * m * CW
                eng.dma_start(adjt[:, bass.ds(base, CT * CW)].rearrange("p (t c) -> p t c", c=CW),
                              adj_t[m * CW:(m + 1) * CW, bass.ds(k * CW, CW)]
                              .rearrange("(t p) c -> p t c", p=P)).then_inc(adjt_loaded[m], 16)

            def load_nat(i, q):
                eng.dma_start(nat[:, q * N:(q + 1) * N], adj[bass.ds(i * P, P), :]) \
                   .then_inc(nat_loaded[q], 16)

            for g in range(CT):
                eng.dma_start(xs[:, CT * g:CT * g + CT, :],
                              x[g * CW:(g + 1) * CW, :].rearrange("(t p) d -> p t d", p=P)) \
                   .then_inc(x_loaded[g], 16)
            for m in range(CT):
                load_adjt(0, m)
            eng.wait_ge(rows_summed, 4)
            load_nat(0, 0)
            load_nat(1, 1)
            eng.wait_ge(h_lo_made, CT)
            eng.wait_ge(hd_made, CT)
            for m in range(CT):
                eng.wait_ge(adjt_loaded[m], 16)
                load_adjt(1, m)

            def chunk(k, tiles, chunk_ahead):
                for m in range(tiles):
                    eng.wait_ge(off_done, CT * k + m + 1)
                    load_nat(CT * k + m + 2, m % 2)
                for r in range(CT):
                    eng.wait_ge(t_kept, CT * (k + 1) + r + 1)
                    eng.wait_ge(b_kept, CT * (k + 1) + r + 1)
                    eng.dma_start(tb_dram[bass.ds(CT * k + r, 1), :, :].rearrange("t p n -> p (t n)"),
                                  tb_out[:, r * 2 * D:(r + 1) * 2 * D]).then_inc(tb_stored[r], 16)
                if chunk_ahead:
                    for m in range(CT):
                        eng.wait_ge(slot_free, RING + PAIRS * (k + 1))
                        eng.wait_ge(adjt_loaded[m], 16 * (k + 2))
                        load_adjt(k + 2, m)

            with eng.Fori(0, NC - 2) as k:
                chunk(k, CT, True)
            chunk(NC - 2, CT, False)
            chunk(NC - 1, CT - 2, False)

            def load_tile(i, half, q):
                wait(eng, tb_turned, i - 1)
                eng.dma_start(tb_in[:, q, :], tb_dram[bass.ds(i, 1), :, :].rearrange("t p n -> p (t n)")) \
                   .then_inc(tb_loaded[q], 16)
                wait(eng, half_ready, i - 1)
                eng.dma_start(x_in[:, q, :], x[bass.ds(i * P, P), :]).then_inc(x_read[q], 16)

            def load_diag(i, half, q):
                wait(eng, s2_ready, i - 1)
                eng.dma_start(adj_diag[:, q, :], adj[bass.ds(i * P, P), bass.ds(i * P, P)]) \
                   .then_inc(diag_loaded[q], 16)

            def turn(at):
                if at(1):
                    load_tile(*at(1))
                if at(0):
                    load_diag(*at(0))
                if at(-2):
                    i, half, q = at(-2)
                    eng.wait_ge(o_ready, i + 1)
                    eng.dma_start(out[bass.ds(i * P, P), :], o_sb[:, q, :]).then_inc(o_stored[q], 16)

            for r in range(CT):
                eng.wait_ge(tb_stored[r], 16 * (NC + 1))
            turns(eng, turn)
            for q in range(2):
                eng.wait_ge(o_stored[q], 16 * (NT // 2))
            with if_general(eng):
                with eng.Fori(0, NT) as i:
                    eng.dma_start(adj_row, adj[bass.ds(i * P, P), :]).then_inc(row_loaded, 16)
                    eng.wait_ge(row_o_ready, i + 1)
                    eng.dma_start(out[bass.ds(i * P, P), :], o_sb[:, 0, :]).then_inc(row_stored, 16)
                    eng.wait_ge(row_stored, 16 * (i + 1))
                    apart(eng)

        @block.gpsimd
        def _(eng):
            eng.memset(ident[:, :], 0.0).then_inc(consts_made, 1)
            eng.memset(ones[:, :], 1.0).then_inc(consts_made, 1)
            eng.memset(ones_b[:, :], 1.0).then_inc(consts_made, 1)
            eng.memset(half_neg[:, :], -0.5).then_inc(consts_made, 1)
            eng.wait_ge(consts_made, 4)
            eng.affine_select(out=ident[:, :], in_=ident[:, :], compare_op=ALU.not_equal, fill=1.0, base=0,
                              pattern=[[-1, P]], channel_multiplier=1).then_inc(consts_made, 1)
            eng.iota(iota_n, pattern=[[1, N]], base=0, channel_multiplier=0,
                     allow_small_or_imprecise_dtypes=True).then_inc(iota_made, 1)
            eng.memset(big[:, :], BIG).then_inc(consts_made, 1)
            for g in range(CT):
                eng.wait_ge(var_made, g + 1)
                eng.tensor_tensor(rstd[:, CT * g:CT * g + CT], var_e[:, CT * g:CT * g + CT],
                                  half_neg[:, CT * g:CT * g + CT], ALU.pow).then_inc(rstd_made, 1)

            def turn(at):
                if at(-1):
                    i, half, q = at(-1)
                    eng.wait_ge(msk_ready, i + 1)
                    wait(eng, s3_ready, i - 1)
                    apart(eng)
                    eng.tensor_scalar(fac[:, q, :], mask[:, q, :], 1.0 - OFF, OFF, ALU.mult, ALU.add) \
                       .then_inc(fac_ready, 1)
                if at(0):
                    i, half, q = at(0)
                    eng.wait_ge(x_read[q], 16 * (half + 1))
                    wait(eng, x1_ready, i - 1)
                    apart(eng)
                    eng.tensor_scalar(x_half[:, q, :], x_in[:, q, :], 0.5, None, ALU.add) \
                       .then_inc(half_ready, 1)
                    eng.wait_ge(mv_ready, i + 1)
                    apart(eng)
                    eng.tensor_scalar(veb[:, :], mvb[:, 1:2], LN_EPS, None, ALU.add).then_inc(ve_ready, 1)
                    eng.wait_ge(ve_ready, i + 1)
                    eng.tensor_tensor(rs_all[:, bass.ds(i, 1)], veb[:, :], half_neg[:, 0:1], ALU.pow) \
                       .then_inc(rs_ready, 1)

            eng.wait_ge(lo_ready, PAIRS * NC)
            turns(eng, turn)

        @block.scalar
        def _(eng):
            def rows(v, n):
                return v.rearrange("(a n) -> a n", a=1).broadcast_to([P, n])

            loads = [
                (ptr_i[:, :], ptr.rearrange("(g a) -> g a", a=1)),
                (wq, Wq.rearrange("(k p) d -> p k d", p=P)),
                (wk, Wk.rearrange("(k p) d -> p k d", p=P)),
                (bqk_col[:, :, :], bq_bk),
                (w_sa[:, :, :], W_sa.rearrange("(k p) d -> p k d", p=P)),
                (a_row[:, :, :].rearrange("p a d -> p (a d)"), a_sa.broadcast_to([P, 2 * D])),
                (w_v[:, :, 0:D], WvT.rearrange("(k p) d -> p k d", p=P)),
                (w_b[:, :, 0:D], W_gcnb.rearrange("(k p) d -> p k d", p=P)),
                (w_b[:, :, D:D + 2], gate_w[:, :, 0:2]),
                (w4[:, :, 2:4], gate_w[:, :, 2:4]),
                (bg_row[:, :], rows(b_gcnb, D)),
                (bv_row[:, 0:D], rows(bv, D)),
                (gate_bias[:, 0:1], rows(ba, 1)),
                (gate_bias[:, 1:2], rows(bb, 1)),
            ]
            assert len(loads) == N_WEIGHTS
            for to, source in loads:
                eng.dma_start(to, source).then_inc(weights_loaded, 16)
            eng.preload_act_table(ACT.Exp)
            eng.sem_inc(hi_ready, 2)
            eng.sem_inc(b_kept, CT)
            eng.sem_inc(t_kept, CT)

            def keep_hT(g):
                eng.wait_ge(h_turned, g + 1)
                eng.activation(hT[:, :, 2 * P * g:2 * P * (g + 1)],
                               bank[g][:, :].rearrange("p (k n) -> p k n", k=KT), ACT.Copy) \
                   .then_inc(hT_kept_a, 1)

            for g in range(CT):
                eng.wait_ge(x_loaded[g], 16)
                eng.wait_ge(lnb_made, g + 1)
                for t in range(CT * g, CT * g + CT):
                    eng.activation(h[:, t, :], xs[:, t, :], ACT.Relu, scale=rstd[:, t:t + 1],
                                   bias=ln_b[:, t:t + 1]).then_inc(h_made, 1)
                eng.wait_ge(h_made, CT * g + CT)
                eng.activation(h16[:, CT * g:CT * g + CT, 0, :], h[:, CT * g:CT * g + CT, :], ACT.Copy,
                               scale=H_SCALE).then_inc(h_hi_made, 1)
                keep_hT(2 * g)
            eng.wait_ge(cols_kept, 1)
            eng.activation(nbias[:, :], hc[:, :, 1], ACT.Copy, scale=SLOPE - 1.0).then_inc(bias_made, 1)
            eng.wait_ge(rmin_v, 4)
            eng.activation(dp[:, :], hc[:, :, 1], ACT.Exp, scale=-SLOPE, bias=rm[:, 3:4]) \
               .then_inc(factors_made, 1)
            eng.activation(es[:, :], hc[:, :, 0], ACT.Exp, scale=SLOPE, bias=rm[:, 3:4]) \
               .then_inc(factors_made, 1)
            for c in range(4):
                eng.wait_ge(rows_summed, c + 1)
                if c == 0:
                    eng.wait_ge(cmp_made, 1)
                eng.activation(s_row[:, c * 512:(c + 1) * 512], bank[1 + c][:, :], ACT.Copy) \
                   .then_inc(rows_kept, 1)
            for g in range(CT):
                eng.wait_ge(hd_made, g + 1)
                eng.activation(hd16[:, CT * g:CT * g + CT, 0, 0:D],
                               e_raw[:, (g % 2) * PW:(g % 2 + 1) * PW].rearrange("p (t d) -> p t d", d=D),
                               ACT.Copy).then_inc(hd_hi_made, 1)
            eng.wait_ge(dp_scaled, 1)
            eng.activation(hd16[:, :, 0, D], dp_s[:, :], ACT.Copy).then_inc(hd_hi_made, 1)

            eng.wait_ge(rows_kept, 4)
            eng.wait_ge(bias_made, 1)
            eng.wait_ge(hd_lo_made, CT)
            eng.wait_ge(gid_summed, 1)
            with eng.Fori(0, NC) as k:
                for m in range(CT):
                    i = CT * k + m
                    for q in range(2):
                        eng.wait_ge(mask_ready, 2 * i + q + 1)
                        apart(eng)
                        for n in range(2):
                            j = CT * m + 2 * q + n
                            ins = eng.activation(e_raw[:, q * PW + n * CW:q * PW + (n + 1) * CW],
                                                 s_row[:, bass.ds(k * CW, CW)], ACT.Exp,
                                                 scale=SLOPE - 1.0, bias=nbias[:, j:j + 1])
                        ins.then_inc(raw_ready, 1)
                    for q in range(2):
                        slot = (2 * m + q) % RING
                        eng.wait_ge(mask_ready, 2 * i + q + 3)
                        eng.wait_ge(slot_free, 2 * i + q + 1)
                        eng.activation(e_hi[:, slot * PW:(slot + 1) * PW], e_mask[:, q * PW:(q + 1) * PW],
                                       ACT.Copy, scale=E_SCALE).then_inc(hi_ready, 1)
                    eng.wait_ge(off_bias, i + 1)
                    eng.activation(junk[:, :], nat[:, (m % 2) * N:(m % 2 + 1) * N], ACT.Exp,
                                   scale=2.0 * OFF, bias=mn_b[:, bass.ds(i, 1)],
                                   accum_out=z_off[:, bass.ds(i, 1)]).then_inc(off_done, 1)
                    eng.wait_ge(b_summed, CT * (i + 1))
                    eng.wait_ge(tb_stored[m], 16 * (k + 1))
                    eng.activation(tb_out[:, (2 * m + 1) * D:(2 * m + 2) * D], bank[4 + m][:, 0:D],
                                   ACT.Copy, scale=1.0 / H_SCALE).then_inc(b_kept, 1)
                eng.wait_ge(rden_ready, k + 1)
                for r in range(CT):
                    eng.activation(tb_out[:, 2 * r * D:(2 * r + 1) * D], bank[r][:, 0:D], ACT.Copy,
                                   scale=rden[:, r:r + 1]).then_inc(t_kept, 1)

            def turn(at):
                if at(-1):
                    i, half, q = at(-1)
                    eng.wait_ge(nb_ready, i + 1)
                    wait(eng, h1_turned, i - 1)
                    apart(eng)
                    eng.activation(h1[:, q, :], x1_all[:, bass.ds(i * D, D)], ACT.Relu,
                                   scale=rs_all[:, bass.ds(i, 1)], bias=nb_all[:, bass.ds(i, 1)]) \
                       .then_inc(h1_ready, 1)
                if at(-2):
                    i, half, q = at(-2)
                    eng.wait_ge(m_ready, i + 1)
                    wait(eng, pm_ready, i)
                    wait(eng, z_sum, i)
                    eng.activation(prob[:, :], sc3[:, :], ACT.Exp, bias=neg_m[:, q:q + 1],
                                   accum_out=zw[:, :]).then_inc(p_ready, 1)
                if at(0):
                    i, half, q = at(0)
                    eng.wait_ge(z_ready, i + 1)
                    wait(eng, gates_ready, i)
                    eng.activation(gt[:, :], gz[:, :], ACT.Tanh, scale=0.5).then_inc(tz_ready, 1)
                if at(-1):
                    i, half, q = at(-1)
                    eng.wait_ge(h1_turned, i + 1)
                    wait(eng, s_summed, i - 1)
                    eng.activation(h1T[:, q, :], H_T[:, 0:D], ACT.Copy).then_inc(h1T_kept, 1)
                if at(-2):
                    i, half, q = at(-2)
                    eng.activation(fo[:, :], mn[:, bass.ds(i, 1)], ACT.Exp, scale=2.0 * OFF,
                                   bias=neg_m[:, q:q + 1]).then_inc(fo_ready, 1)
                if at(0):
                    i, half, q = at(0)
                    eng.wait_ge(mix_summed, i + 1)
                    eng.wait_ge(gates_ready, i + 1)
                    wait(eng, u_ready, i)
                    eng.activation(xag, X_A[:, 0:D], ACT.Copy, scale=gates[:, q, 0:1]).then_inc(xag_ready, 1)
                if at(-2):
                    i, half, q = at(-2)
                    eng.wait_ge(p_turned, i + 1)
                    wait(eng, pv_summed, i - 1)
                    eng.activation(pT[:, q, :], P_T, ACT.Copy).then_inc(pT_kept, 1)
                if at(0):
                    i, half, q = at(0)
                    eng.wait_ge(u_ready, i + 1)
                    wait(eng, x1_ready, i)
                    eng.activation(th, u, ACT.Tanh, scale=0.5).then_inc(th_ready, 1)
                if at(-1):
                    i, half, q = at(-1)
                    eng.wait_ge(g_summed, i + 1)
                    wait(eng, s_summed, i - 1)
                    for c in range(KT):
                        eng.activation(gT[:, q, c * P:(c + 1) * P], G_T[:, c * P:(c + 1) * P], ACT.Identity,
                                       scale=QK_SCALE, bias=u_col[:, c:c + 1]).then_inc(g_kept, 1)
                if at(1):
                    i, half, q = at(1)
                    eng.wait_ge(tb_turned, i + 1)
                    wait(eng, mix_summed, i - 1)
                    eng.activation(tbT[:, q, :], TB_T[:, :], ACT.Copy).then_inc(tbT_kept, 1)

            eng.wait_ge(lo_ready, PAIRS * NC)
            turns(eng, turn)
            with if_general(eng):
                eng.sem_inc(all_v_summed, 1)
                with eng.Fori(0, NT) as i:
                    eng.activation(h1[:, 0, :], x1_all[:, bass.ds(i * D, D)], ACT.Relu,
                                   scale=rs_all[:, bass.ds(i, 1)], bias=nb_all[:, bass.ds(i, 1)]) \
                       .then_inc(all_h1, 1)
                    eng.wait_ge(all_h1_turned, i + 1)
                    eng.wait_ge(all_v_summed, i + 1)
                    apart(eng)
                    eng.activation(h1T[:, 0, :], H_T[:, 0:D], ACT.Copy).then_inc(all_h1T_kept, 1)
                    eng.activation(h1T_all[:, :, bass.ds(i * P, P)],
                                   H_T[:, 0:D].rearrange("p (k n) -> p k n", k=KT), ACT.Copy) \
                       .then_inc(all_h1T_kept, 1)
                with eng.Fori(0, NT) as i:
                    eng.wait_ge(row_g_summed, i + 1)
                    apart(eng)
                    for c in range(KT):
                        eng.activation(gT[:, 0, c * P:(c + 1) * P], G_T[:, c * P:(c + 1) * P], ACT.Identity,
                                       scale=QK_SCALE, bias=u_col[:, c:c + 1]).then_inc(row_g_kept, 1)
                    eng.wait_ge(row_m_ready, i + 1)
                    apart(eng)
                    eng.activation(prob_row, score_row, ACT.Exp, bias=neg_m[:, 0:1], accum_out=zw[:, :]) \
                       .then_inc(row_p_ready, 1)
                    for g in range(NT // CT):
                        eng.wait_ge(row_p_turned, CT * i + g + 1)
                        apart(eng)
                        eng.activation(probT_row[:, g * 512:(g + 1) * 512], bank[4 + g][:, :], ACT.Copy) \
                           .then_inc(row_pT_kept, 1)

        @block.tensor
        def _(eng):
            eng.wait_ge(consts_made, 6)
            eng.wait_ge(weights_loaded, 16 * N_WEIGHTS)
            for c in range(KT):
                for kk in range(KT):
                    mm = eng.matmul(bank[0][:, c * D:(c + 1) * D], wq[:, kk, c * P:(c + 1) * P],
                                    wk[:, kk, :], start=(kk == 0), stop=(kk == KT - 1))
            mm.then_inc(qk_summed, 1)
            eng.wait_ge(wide_made, 2)
            for c in range(KT):
                for kk in range(KT):
                    eng.matmul(bank[1][:, c:c + 1], wk[:, kk, c * P:(c + 1) * P], bqk_col[:, kk, 0:1],
                               start=(kk == 0), stop=(kk == KT - 1))
            for c in range(KT):
                for kk in range(KT):
                    eng.matmul(bank[1][:, KT + c:KT + c + 1], wq[:, kk, c * P:(c + 1) * P],
                               bqk_col[:, kk, 1:2], start=(kk == 0), stop=(kk == KT - 1))
            for kk in range(KT):
                mm = eng.matmul(bank[1][:, 2 * KT:2 * KT + 1], bq_wide[:, kk, :], bqk_col[:, kk, 1:2],
                                start=(kk == 0), stop=(kk == KT - 1))
            mm.then_inc(qk_summed, 1)
            eng.wait_ge(cmp_made, 1)
            for c in range(N // 512):
                eng.matmul(bank[2 + c][:, :], ones_b[0:NP, :], cmp_ptr[:, c * 512:(c + 1) * 512],
                           start=True, stop=True)
            for t in range(NT):
                mm = eng.matmul(bank[6][:, t:t + 1], cmp_ptr[:, t * P:(t + 1) * P], ones_b[0:NP, 0:1],
                                start=True, stop=True)
            mm.then_inc(gid_summed, 1)
            for g in range(NT // 2):
                if g == 0:
                    eng.wait_ge(qk_kept, 5)
                if g == 2:
                    eng.wait_ge(gid_kept, 2)
                eng.wait_ge(h_made, 2 * g + 2)
                for c in range(KT):
                    for n in range(2):
                        mm = eng.transpose(bank[g][:, (2 * c + n) * P:(2 * c + n + 1) * P],
                                           h[:, 2 * g + n, c * P:(c + 1) * P], ident[:, :])
                mm.then_inc(h_turned, 1)
            eng.wait_ge(hT_kept_a, NT // 4)
            eng.wait_ge(hT_kept_v, NT // 4)
            eng.wait_ge(w_made, 2 * KT)
            for t in range(NT):
                for kk in range(KT):
                    mm = eng.matmul(bank[0][:, 4 * t:4 * t + 4], hT[:, kk, t * P:(t + 1) * P], w4[:, kk, :],
                                    start=(kk == 0), stop=(kk == KT - 1))
            mm.then_inc(cols_summed, 1)
            for c in range(4):
                for kk in range(KT):
                    mm = eng.matmul(bank[1 + c][:, :], wl_wide[:, kk, :], hT[:, kk, c * 512:(c + 1) * 512],
                                    start=(kk == 0), stop=(kk == KT - 1))
                mm.then_inc(rows_summed, 1)
                if c == 1:
                    eng.wait_ge(rmin_v, 1)
                    eng.transpose(bank[5][0:1, 0:P], rm[:, 0:1], ident[:, :]).then_inc(rmin_t, 1)
                if c == 2:
                    eng.wait_ge(rmin_v, 2)
                    eng.matmul(bank[5][:, 2 * P:2 * P + 1], ones[0:1, :], rm[0:1, 1:2], start=True, stop=True) \
                       .then_inc(rmin_t, 1)

            adjt_b = adjt[:, :].bitcast(BF16)
            eng.wait_ge(h_hi_made, CT)
            eng.wait_ge(h_lo_made, CT)
            eng.wait_ge(rows_kept, 4)
            eng.wait_ge(rmin_v, 4)
            eng.wait_ge(hT_kept_v, NT // 4)

            def adj_group(k, r, jg, first):
                for n in range(CT):
                    j = CT * jg + n
                    word = (k % 2) * CHUNK + j * CW + r * P
                    for part in range(2):
                        mm = eng.matmul(bank[4 + r][:, 0:D], adjt_b[:, bass.ds(2 * word + 1, P, 2)],
                                        h16_cols(j, part), start=(first and n == 0 and part == 0),
                                        stop=False, skip_group_check=True)
                mm.then_inc(b_summed, 1)

            h16_f = h16[:, :, :, :].rearrange("p t a d -> p (t a d)")
            hd16_f = hd16[:, :, :, :].rearrange("p t a d -> p (t a d)")

            def h16_cols(j, part):
                return h16_f[:, bass.ds(2 * D * j + D * part, D)]

            def hd16_cols(j, part, width):
                return hd16_f[:, bass.ds(2 * E1 * j + E1 * part, width)]

            def e_group(k, m, first):
                for q in range(2):
                    base = ((2 * m + q) % RING) * PW
                    eng.wait_ge(lo_ready, PAIRS * k + 2 * m + q + 1)
                    for n in range(2):
                        j = CT * m + 2 * q + n
                        for r in range(CT):
                            high = e_hi[:, bass.ds(base + n * CW + r * P, P)]
                            low = e_lo[:, bass.ds(base + n * CW + r * P, P)]
                            eng.matmul(bank[r][:, 0:D + 1], high, hd16_cols(j, 0, D + 1),
                                       start=(first and q == 0 and n == 0), stop=False, skip_group_check=True)
                            eng.matmul(bank[r][:, 0:D + 1], low, hd16_cols(j, 0, D + 1),
                                       start=False, stop=False, skip_group_check=True)
                            mm = eng.matmul(bank[r][:, 0:D + 1], high, hd16_cols(j, 1, D + 1),
                                            start=False, stop=False, skip_group_check=True)
                    mm.then_inc(slot_free, 1)

            with eng.Fori(0, NC) as k:
                for r in range(CT):
                    if r == 0:
                        for m in range(CT):
                            eng.wait_ge(adjt_loaded[m], 16 * (k + 1))
                    eng.wait_ge(b_kept, CT * k + r + 1)
                    adj_group(k, r, 0, True)
                    with eng.Fori(1, CT) as jg:
                        adj_group(k, r, jg, False)
                eng.wait_ge(t_kept, CT * (k + 1))
                eng.wait_ge(hd_lo_made, CT + 1)
                e_group(k, 0, True)
                with eng.Fori(1, CT) as m:
                    e_group(k, m, False)

            def turn(at):
                if at(0):
                    i, half, q = at(0)
                    eng.wait_ge(tbT_kept, i + 1)
                    wait(eng, xbb_ready, i)
                    for kk in range(KT):
                        mm = eng.matmul(X_B[:, 0:E1], tbT[:, q, (KT + kk) * P:(KT + kk + 1) * P], w_b[:, kk, :],
                                        start=(kk == 0), stop=(kk == KT - 1))
                    mm.then_inc(b_mix_summed, 1)
                if at(-1):
                    i, half, q = at(-1)
                    eng.wait_ge(h1_ready, i + 1)
                    wait(eng, h1T_kept, i)
                    for c in range(KT):
                        mm = eng.transpose(H_T[:, c * P:(c + 1) * P], h1[:, q, c * P:(c + 1) * P], ident[:, :])
                    mm.then_inc(h1_turned, 1)
                if at(0):
                    i, half, q = at(0)
                    wait(eng, xag_ready, i)
                    for kk in range(KT):
                        mm = eng.matmul(X_A[:, 0:D], tbT[:, q, kk * P:(kk + 1) * P], w_sa[:, kk, :],
                                        start=(kk == 0), stop=(kk == KT - 1))
                    mm.then_inc(mix_summed, 1)
                if at(-2):
                    i, half, q = at(-2)
                    eng.wait_ge(pm_ready, i + 1)
                    wait(eng, o_ready, i)
                    eng.transpose(P_T, probm[:, q, :], ident[:, :]).then_inc(p_turned, 1)
                if at(-1):
                    i, half, q = at(-1)
                    eng.wait_ge(h1T_kept, i + 1)
                    wait(eng, g_kept, KT * i)
                    for c in range(KT):
                        for kk in range(KT):
                            mm = eng.matmul(G_T[:, c * P:(c + 1) * P], w_qk[:, kk, c * P:(c + 1) * P],
                                            h1T[:, q, kk * P:(kk + 1) * P],
                                            start=(kk == 0), stop=(kk == KT - 1))
                    mm.then_inc(g_summed, 1)
                if at(-2):
                    i, half, q = at(-2)
                    eng.wait_ge(pT_kept, i + 1)
                    eng.wait_ge(v_kept, i + 1)
                    eng.matmul(PV[:, 0:D], pT[:, q, :], v_sb[:, q, 0:D], start=True, stop=True) \
                       .then_inc(pv_summed, 1)
                if at(-1):
                    i, half, q = at(-1)
                    wait(eng, v_kept, i)
                    for kk in range(KT):
                        mm = eng.matmul(V_S[:, 0:D + 1], h1T[:, q, kk * P:(kk + 1) * P], w_v[:, kk, :],
                                        start=(kk == 0), stop=(kk == KT - 1))
                    mm.then_inc(v_summed, 1)
                    eng.wait_ge(g_kept, KT * (i + 1))
                    wait(eng, s1_ready, i)
                    for kk in range(KT):
                        mm = eng.matmul(S_S[:, 0:P], gT[:, q, kk * P:(kk + 1) * P],
                                        h1T[:, q, kk * P:(kk + 1) * P], start=(kk == 0), stop=(kk == KT - 1))
                    mm.then_inc(s_summed, 1)
                if at(1):
                    i, half, q = at(1)
                    eng.wait_ge(tb_loaded[q], 16 * (half + 1))
                    wait(eng, tbT_kept, i)
                    for c in range(2 * KT):
                        mm = eng.transpose(TB_T[:, c * P:(c + 1) * P], tb_in[:, q, c * P:(c + 1) * P],
                                           ident[:, :])
                    mm.then_inc(tb_turned, 1)

            eng.wait_ge(t_kept, CT * (NC + 1))
            eng.wait_ge(b_kept, CT * (NC + 1))
            turns(eng, turn)
            with if_general(eng):
                with eng.Fori(0, NT) as i:
                    eng.wait_ge(all_h1, i + 1)
                    apart(eng)
                    for c in range(KT):
                        mm = eng.transpose(H_T[:, c * P:(c + 1) * P], h1[:, 0, c * P:(c + 1) * P], ident[:, :])
                    mm.then_inc(all_h1_turned, 1)
                    eng.wait_ge(all_h1T_kept, 2 * i + 2)
                    eng.wait_ge(all_v_kept, 2 * i + 2)
                    apart(eng)
                    for kk in range(KT):
                        mm = eng.matmul(V_S[:, 0:D + 1], h1T[:, 0, kk * P:(kk + 1) * P], w_v[:, kk, :],
                                        start=(kk == 0), stop=(kk == KT - 1))
                    mm.then_inc(all_v_summed, 1)
                eng.wait_ge(all_v_kept, 2 * NT + 2)
                with eng.Fori(0, NT) as i:
                    for c in range(KT):
                        for kk in range(KT):
                            mm = eng.matmul(G_T[:, c * P:(c + 1) * P], w_qk[:, kk, c * P:(c + 1) * P],
                                            h1T_all[:, kk, bass.ds(i * P, P)],
                                            start=(kk == 0), stop=(kk == KT - 1))
                    mm.then_inc(row_g_summed, 1)
                    eng.wait_ge(row_g_kept, KT * (i + 1))
                    apart(eng)
                    for c in range(N // 512):
                        for kk in range(KT):
                            mm = eng.matmul(bank[c][:, :], gT[:, 0, kk * P:(kk + 1) * P],
                                            h1T_all[:, kk, c * 512:(c + 1) * 512],
                                            start=(kk == 0), stop=(kk == KT - 1))
                    mm.then_inc(row_s_summed, 1)
                    eng.wait_ge(row_pm_ready, i + 1)
                    apart(eng)
                    for g in range(NT // CT):
                        for n in range(CT):
                            mm = eng.transpose(bank[4 + g][:, n * P:(n + 1) * P],
                                               score_row[:, (CT * g + n) * P:(CT * g + n + 1) * P], ident[:, :])
                        mm.then_inc(row_p_turned, 1)
                    eng.wait_ge(row_pT_kept, CT * (i + 1))
                    apart(eng)
                    for j in range(NT):
                        mm = eng.matmul(bank[4][:, 0:D], probT_row[:, j * P:(j + 1) * P],
                                        v_all[:, j * D:(j + 1) * D], start=(j == 0), stop=(j == NT - 1))
                    mm.then_inc(row_pv_summed, 1)
                    eng.wait_ge(row_o_ready, i + 1)
                    apart(eng)

        @block.vector
        def _(eng):
            eng.sem_inc(mask_ready, 2)
            eng.sem_inc(slot_free, RING)
            for r in range(CT):
                eng.sem_inc(tb_stored[r], 16)

            eng.wait_ge(weights_loaded, 16 * N_WEIGHTS)
            eng.wait_ge(consts_made, 6)
            eng.tensor_copy(ptr_f[:, :], ptr_i[:, :]).then_inc(ptr_made, 1)
            for kk in range(KT):
                eng.tensor_scalar(bq_wide[:, kk, :], ones[:, :], bqk_col[:, kk, 0:1], None, ALU.mult) \
                   .then_inc(wide_made, 1)
            eng.wait_ge(ptr_made, 1)
            eng.wait_ge(iota_made, 1)
            eng.tensor_scalar(cmp_ptr, iota_n, ptr_f[:, :], None, ALU.is_ge).then_inc(cmp_made, 1)

            def moments(g):
                eng.wait_ge(x_loaded[g], 16)
                for t in range(CT * g, CT * g + CT):
                    eng.bn_stats(st6[:, t, :], xs[:, t, :]).then_inc(stats_made, 1)
                for t in range(CT * g, CT * g + CT):
                    eng.wait_ge(stats_made, t + 1)
                    eng.bn_aggr(mv[:, t, :], st6[:, t, :]).then_inc(moments_made, 1)
                eng.wait_ge(moments_made, CT * g + CT)
                eng.tensor_scalar(var_e[:, CT * g:CT * g + CT], mv[:, CT * g:CT * g + CT, 1], LN_EPS, None,
                                  ALU.add).then_inc(var_made, 1)

            def shift(g):
                eng.wait_ge(rstd_made, g + 1)
                eng.scalar_tensor_tensor(out=ln_b[:, CT * g:CT * g + CT], in0=mv[:, CT * g:CT * g + CT, 0],
                                         scalar=-1.0, in1=rstd[:, CT * g:CT * g + CT],
                                         op0=ALU.mult, op1=ALU.mult).then_inc(lnb_made, 1)

            def keep_hT(g):
                eng.wait_ge(h_turned, g + 1)
                eng.tensor_copy(hT[:, :, 2 * P * g:2 * P * (g + 1)],
                                bank[g][:, :].rearrange("p (k n) -> p k n", k=KT)).then_inc(hT_kept_v, 1)

            def h_low(g):
                eng.wait_ge(h_hi_made, g + 1)
                eng.scalar_tensor_tensor(out=h16[:, CT * g:CT * g + CT, 1, :],
                                         in0=h[:, CT * g:CT * g + CT, :], scalar=H_SCALE,
                                         in1=h16[:, CT * g:CT * g + CT, 0, :],
                                         op0=ALU.mult, op1=ALU.subtract).then_inc(h_lo_made, 1)

            moments(0)
            shift(0)
            for kk in range(KT):
                for side in range(2):
                    eng.tensor_tensor_reduce(e_raw[:, (2 * kk + side) * D:(2 * kk + side + 1) * D],
                                             w_sa[:, kk, :], a_row[:, side, :], 1.0, 0.0,
                                             ALU.mult, ALU.add, w4[:, kk, side:side + 1]).then_inc(w_made, 1)
            moments(1)
            shift(1)
            eng.wait_ge(qk_summed, 2)
            eng.tensor_copy(w_qk[:, :, :].rearrange("p k d -> p (k d)"), bank[0][:, :]).then_inc(qk_kept, 1)
            eng.tensor_scalar(u_col[:, :], bank[1][:, 0:KT], QK_SCALE, None, ALU.mult).then_inc(qk_kept, 1)
            for kk in range(KT):
                eng.tensor_copy(w_v[:, kk, D:D + 1], bank[1][:, KT + kk:KT + kk + 1]).then_inc(qk_kept, 1)
            eng.tensor_copy(bv_row[:, D:D + 1], bank[1][:, 2 * KT:2 * KT + 1]).then_inc(qk_kept, 1)
            eng.wait_ge(qk_kept, 5)
            eng.tensor_scalar(w_v[:, :, D], w_v[:, :, D], QK_SCALE, None, ALU.mult).then_inc(qk_kept, 1)
            eng.tensor_scalar(bv_row[:, D:D + 1], bv_row[:, D:D + 1], QK_SCALE, None, ALU.mult) \
               .then_inc(qk_kept, 1)
            eng.wait_ge(gid_summed, 1)
            for c in range(N // 512):
                ins = eng.tensor_copy(gid_row[:, c * 512:(c + 1) * 512], bank[2 + c][:, :])
            ins.then_inc(gid_kept, 1)
            eng.tensor_copy(gid_col[:, :], bank[6][:, 0:NT]).then_inc(gid_kept, 1)
            eng.wait_ge(gid_kept, 2)
            eng.tensor_tensor(diff[0:1, 1:NT], gid_row[0:1, P - 1:N - P:P], gid_row[0:1, P:N:P], ALU.is_equal) \
               .then_inc(flag_made, 1)
            eng.wait_ge(flag_made, 1)
            eng.tensor_reduce(diff[0:1, 0:1], diff[0:1, 1:NT], AX, ALU.max).then_inc(flag_made, 1)
            eng.wait_ge(flag_made, 2)
            eng.tensor_copy(general[0:1, 0:1], diff[0:1, 0:1]).then_inc(flag_made, 1)
            moments(2)
            shift(2)
            keep_hT(1)
            eng.wait_ge(w_made, 2 * KT)
            for kk in range(KT):
                eng.tensor_scalar(wl_wide[:, kk, :], ones[:, :], w4[:, kk, 0:1], None, ALU.mult) \
                   .then_inc(wide_made, 1)
            moments(3)
            shift(3)
            keep_hT(3)
            h_low(0)
            keep_hT(5)
            h_low(1)
            keep_hT(7)
            h_low(2)
            h_low(3)
            eng.wait_ge(cols_summed, 1)
            eng.tensor_copy(hc[:, :, :].rearrange("p t c -> p (t c)"), bank[0][:, 0:4 * NT]).then_inc(cols_kept, 1)
            eng.wait_ge(cols_kept, 1)
            eng.tensor_reduce(rm[:, 0:1], hc[:, :, 1], AX, ALU.min).then_inc(rmin_v, 1)
            for c in range(2):
                eng.tensor_scalar(hc[:, :, 2 + c], hc[:, :, 2 + c], gate_bias[:, c:c + 1], None, ALU.add) \
                   .then_inc(cols_kept, 1)
            eng.wait_ge(rmin_t, 1)
            eng.tensor_reduce(rm[0:1, 1:2], bank[5][0:1, 0:P], AX, ALU.min).then_inc(rmin_v, 1)
            eng.wait_ge(rmin_t, 2)
            eng.tensor_copy(rm[:, 2:3], bank[5][:, 2 * P:2 * P + 1]).then_inc(rmin_v, 1)
            eng.wait_ge(rmin_v, 3)
            eng.tensor_scalar(rm[:, 3:4], rm[:, 2:3], SLOPE, None, ALU.mult).then_inc(rmin_v, 1)
            eng.wait_ge(factors_made, 2)
            eng.tensor_scalar(dp_s[:, :], dp[:, :], H_SCALE, None, ALU.mult).then_inc(dp_scaled, 1)
            eng.wait_ge(w_made, 2 * KT)

            def h_times_dp(g):
                if g >= 2:
                    eng.wait_ge(hd_lo_made, g - 1)
                    eng.wait_ge(hd_hi_made, g - 1)
                for n in range(CT):
                    t = CT * g + n
                    ins = eng.tensor_scalar(e_raw[:, (g % 2) * PW + n * D:(g % 2) * PW + (n + 1) * D],
                                            h[:, t, :], dp[:, t:t + 1], H_SCALE, ALU.mult, ALU.mult)
                ins.then_inc(hd_made, 1)

            def hd_low(g):
                eng.wait_ge(hd_hi_made, g + 1)
                eng.wait_ge(hd_made, g + 1)
                part = hd16[:, CT * g:CT * g + CT, :, 0:D]
                eng.tensor_tensor(part[:, :, 1, :],
                                  e_raw[:, (g % 2) * PW:(g % 2 + 1) * PW].rearrange("p (t d) -> p t d", d=D),
                                  part[:, :, 0, :], ALU.subtract).then_inc(hd_lo_made, 1)

            h_times_dp(0)
            h_times_dp(1)
            for g in range(CT):
                hd_low(g)
                if g + 2 < CT:
                    h_times_dp(g + 2)
            eng.wait_ge(hd_hi_made, CT + 1)
            eng.wait_ge(dp_scaled, 1)
            eng.tensor_tensor(hd16[:, :, 1, D], dp_s[:, :], hd16[:, :, 0, D], ALU.subtract) \
               .then_inc(hd_lo_made, 1)

            with eng.Fori(0, NC) as k:
                for m in range(CT):
                    i = CT * k + m
                    for q in range(2):
                        if q == 0:
                            eng.wait_ge(adjt_loaded[m], 16 * (k + 1))
                        eng.wait_ge(raw_ready, 2 * i + q + 1)
                        eng.wait_ge(hi_ready, 2 * i + q + 1)
                        j = CT * m + 2 * q
                        eng.scalar_tensor_tensor(out=e_mask[:, q * PW:(q + 1) * PW],
                                                 in0=e_raw[:, q * PW:(q + 1) * PW], scalar=1.0,
                                                 in1=adjt[:, bass.ds((k % 2) * CHUNK + j * CW, PW)],
                                                 op0=ALU.min, op1=ALU.mult).then_inc(mask_ready, 1)
                    eng.wait_ge(nat_loaded[m % 2], 16 * (2 * k + m // 2 + 1))
                    eng.tensor_copy(nat[:, bass.ds((m % 2) * N + i * P, P)], big[:, :]).then_inc(big_set, 1)
                    for q in range(2):
                        slot = (2 * m + q) % RING
                        eng.wait_ge(hi_ready, 2 * i + q + 3)
                        eng.scalar_tensor_tensor(out=e_lo[:, slot * PW:(slot + 1) * PW],
                                                 in0=e_mask[:, q * PW:(q + 1) * PW], scalar=E_SCALE,
                                                 in1=e_hi[:, slot * PW:(slot + 1) * PW],
                                                 op0=ALU.mult, op1=ALU.subtract).then_inc(lo_ready, 1)
                    eng.wait_ge(big_set, i + 1)
                    eng.tensor_reduce(mn[:, bass.ds(i, 1)], nat[:, (m % 2) * N:(m % 2 + 1) * N], AX, ALU.min) \
                       .then_inc(least_ready, 1)
                    eng.wait_ge(least_ready, i + 1)
                    eng.tensor_scalar(mn_b[:, bass.ds(i, 1)], mn[:, bass.ds(i, 1)], -2.0 * OFF, None,
                                      ALU.mult).then_inc(off_bias, 1)
                eng.wait_ge(slot_free, RING + PAIRS * (k + 1))
                eng.wait_ge(t_kept, CT * (k + 1))
                for r in range(CT):
                    ins = eng.scalar_tensor_tensor(out=den[:, r:r + 1], in0=es[:, bass.ds(CT * k + r, 1)],
                                                   scalar=ATTN_EPS * H_SCALE * E_SCALE,
                                                   in1=bank[r][:, D:D + 1], op0=ALU.mult, op1=ALU.add)
                ins.then_inc(den_ready, 1)
                eng.wait_ge(den_ready, k + 1)
                eng.reciprocal(rden[:, :], den[:, :]).then_inc(rden_ready, 1)

            def turn(at):
                if at(-1):
                    i, half, q = at(-1)
                    eng.wait_ge(rs_ready, i + 1)
                    eng.scalar_tensor_tensor(out=nb_all[:, bass.ds(i, 1)], in0=mvb[:, 0:1], scalar=-1.0,
                                             in1=rs_all[:, bass.ds(i, 1)],
                                             op0=ALU.mult, op1=ALU.mult).then_inc(nb_ready, 1)
                if at(-2):
                    i, half, q = at(-2)
                    eng.wait_ge(s3_ready, i + 1)
                    eng.tensor_reduce(neg_mw[:, :], sc3[:, :], AX, ALU.max, negate=True).then_inc(mw_ready, 1)
                    eng.wait_ge(mw_ready, i + 1)
                    wait(eng, fo_ready, i - 1)
                    eng.tensor_tensor(neg_m[:, q:q + 1], neg_mw[:, :], mn_b[:, bass.ds(i, 1)], ALU.min) \
                       .then_inc(m_ready, 1)
                if at(-1):
                    i, half, q = at(-1)
                    wait(eng, fac_ready, i - 1)
                    eng.tensor_scalar(mask[:, q, :], gid_row[:, bass.ds(i * P, P)],
                                      gid_col[:, bass.ds(i, 1)], None, ALU.is_equal).then_inc(msk_ready, 1)
                if at(0):
                    i, half, q = at(0)
                    eng.wait_ge(b_mix_summed, i + 1)
                    wait(eng, tz_ready, i)
                    eng.tensor_tensor(gz[:, :], X_B[:, D:D + 2],
                                      hc_f[:, bass.ds(4 * i + 2, 2)], ALU.add).then_inc(z_ready, 1)
                if at(-2):
                    i, half, q = at(-2)
                    eng.wait_ge(p_ready, i + 1)
                    wait(eng, p_turned, i - 1)
                    eng.tensor_tensor(probm[:, q, :], prob[:, :], mask[:, q, :], ALU.mult).then_inc(pm_ready, 1)
                if at(0):
                    i, half, q = at(0)
                    eng.wait_ge(tz_ready, i + 1)
                    eng.tensor_scalar(gates[:, q, :], gt[:, :], 0.5, 0.5, ALU.mult, ALU.add) \
                       .then_inc(gates_ready, 1)
                    wait(eng, u_ready, i)
                    eng.tensor_tensor(xbb, X_B[:, 0:D], bg_row[:, :], ALU.add).then_inc(xbb_ready, 1)
                if at(-2):
                    i, half, q = at(-2)
                    eng.wait_ge(fo_ready, i + 1)
                    wait(eng, rz_ready, i)
                    eng.scalar_tensor_tensor(out=zs[:, :], in0=z_off[:, bass.ds(i, 1)], scalar=fo[:, :],
                                             in1=zw[:, :], op0=ALU.mult, op1=ALU.add).then_inc(z_sum, 1)
                    eng.wait_ge(z_sum, i + 1)
                    wait(eng, o_ready, i - 1)
                    eng.reciprocal(rz[:, q:q + 1], zs[:, :]).then_inc(rz_ready, 1)
                if at(0):
                    i, half, q = at(0)
                    eng.wait_ge(xag_ready, i + 1)
                    eng.wait_ge(xbb_ready, i + 1)
                    wait(eng, th_ready, i)
                    eng.scalar_tensor_tensor(out=u, in0=xbb, scalar=gates[:, q, 1:2], in1=xag,
                                             op0=ALU.mult, op1=ALU.add).then_inc(u_ready, 1)
                    eng.wait_ge(th_ready, i + 1)
                    eng.wait_ge(half_ready, i + 1)
                    x1 = x1_all[:, bass.ds(i * D, D)]
                    eng.scalar_tensor_tensor(out=x1, in0=th, scalar=0.5, in1=x_half[:, q, :],
                                             op0=ALU.mult, op1=ALU.add).then_inc(x1_ready, 1)
                if at(-2):
                    i, half, q = at(-2)
                    eng.wait_ge(pv_summed, i + 1)
                    eng.wait_ge(rz_ready, i + 1)
                    wait(eng, o_stored[q], 16 * half)
                    eng.scalar_tensor_tensor(out=o_sb[:, q, :], in0=PV[:, 0:D], scalar=rz[:, q:q + 1],
                                             in1=x1_all[:, bass.ds(i * D, D)], op0=ALU.mult, op1=ALU.add) \
                       .then_inc(o_ready, 1)
                if at(0):
                    i, half, q = at(0)
                    eng.wait_ge(x1_ready, i + 1)
                    wait(eng, mv_ready, i)
                    apart(eng)
                    eng.bn_stats(st6b[:, :], x1_all[:, bass.ds(i * D, D)]).then_inc(st_ready, 1)
                if at(-1):
                    i, half, q = at(-1)
                    eng.wait_ge(v_summed, i + 1)
                    wait(eng, pv_summed, i - 1)
                    eng.tensor_tensor(v_sb[:, q, 0:D + 1], V_S[:, 0:D + 1], bv_row[:, :], ALU.add) \
                       .then_inc(v_kept, 1)
                if at(0):
                    i, half, q = at(0)
                    eng.wait_ge(st_ready, i + 1)
                    wait(eng, ve_ready, i)
                    wait(eng, nb_ready, i)
                    apart(eng)
                    eng.bn_aggr(mvb[:, :], st6b[:, :]).then_inc(mv_ready, 1)
                if at(-1):
                    i, half, q = at(-1)
                    eng.wait_ge(s_summed, i + 1)
                    eng.wait_ge(msk_ready, i + 1)
                    eng.wait_ge(v_kept, i + 1)
                    wait(eng, s2_ready, i)
                    eng.scalar_tensor_tensor(out=sc1[:, :], in0=S_S[:, 0:P], scalar=v_sb[:, q, D:D + 1],
                                             in1=mask[:, q, :], op0=ALU.add, op1=ALU.mult) \
                       .then_inc(s1_ready, 1)
                    eng.wait_ge(s1_ready, i + 1)
                    eng.wait_ge(diag_loaded[q], 16 * (half + 1))
                    wait(eng, s3_ready, i)
                    eng.scalar_tensor_tensor(out=sc2[:, :], in0=adj_diag[:, q, :], scalar=2.0, in1=sc1[:, :],
                                             op0=ALU.mult, op1=ALU.add).then_inc(s2_ready, 1)
                    eng.wait_ge(s2_ready, i + 1)
                    eng.wait_ge(fac_ready, i + 1)
                    wait(eng, p_ready, i)
                    eng.tensor_tensor(sc3[:, :], sc2[:, :], fac[:, q, :], ALU.mult).then_inc(s3_ready, 1)

            hc_f = hc[:, :, :].rearrange("p t c -> p (t c)")
            eng.wait_ge(b_summed, NT * CT)
            eng.wait_ge(cols_kept, 3)
            turns(eng, turn)
            with if_general(eng):
                eng.sem_inc(all_v_kept, 2)
                with eng.Fori(0, NT) as i:
                    eng.wait_ge(all_v_summed, i + 2)
                    apart(eng)
                    eng.tensor_tensor(v_all[:, bass.ds(i * D, D)], V_S[:, 0:D], bv_row[:, 0:D], ALU.add) \
                       .then_inc(all_v_kept, 1)
                    eng.tensor_tensor(c_all[:, bass.ds(i, 1)], V_S[:, D:D + 1], bv_row[:, D:D + 1], ALU.add) \
                       .then_inc(all_v_kept, 1)
                with eng.Fori(0, NT) as i:
                    eng.wait_ge(row_loaded, 16 * (i + 1))
                    apart(eng)
                    eng.tensor_scalar(mask_row[:, :], gid_row[:, :], gid_col[:, bass.ds(i, 1)], None,
                                      ALU.is_equal).then_inc(row_masked, 1)
                    eng.wait_ge(row_masked, 2 * i + 1)
                    apart(eng)
                    eng.tensor_scalar(fac_row, mask_row[:, :], 1.0 - OFF, OFF, ALU.mult, ALU.add) \
                       .then_inc(row_masked, 1)
                    eng.wait_ge(row_s_summed, i + 1)
                    apart(eng)
                    for c in range(N // 512):
                        ins = eng.scalar_tensor_tensor(out=score_row[:, c * 512:(c + 1) * 512],
                                                       in0=bank[c][:, :], scalar=c_all[:, bass.ds(i, 1)],
                                                       in1=mask_row[:, c * 512:(c + 1) * 512],
                                                       op0=ALU.add, op1=ALU.mult)
                    ins.then_inc(row_scored, 1)
                    eng.wait_ge(row_scored, 3 * i + 1)
                    apart(eng)
                    eng.scalar_tensor_tensor(out=score_row, in0=adj_row, scalar=2.0, in1=score_row,
                                             op0=ALU.mult, op1=ALU.add).then_inc(row_scored, 1)
                    eng.wait_ge(row_masked, 2 * i + 2)
                    eng.wait_ge(row_scored, 3 * i + 2)
                    apart(eng)
                    eng.tensor_tensor(score_row, score_row, fac_row, ALU.mult).then_inc(row_scored, 1)
                    eng.wait_ge(row_scored, 3 * i + 3)
                    apart(eng)
                    eng.tensor_reduce(neg_m[:, 0:1], score_row, AX, ALU.max, negate=True) \
                       .then_inc(row_m_ready, 1)
                    eng.wait_ge(row_p_ready, i + 1)
                    apart(eng)
                    eng.reciprocal(rz[:, 0:1], zw[:, :])
                    eng.tensor_tensor(score_row, prob_row, mask_row[:, :], ALU.mult).then_inc(row_pm_ready, 1)
                    eng.wait_ge(row_pv_summed, i + 1)
                    apart(eng)
                    eng.scalar_tensor_tensor(out=o_sb[:, 0, :], in0=bank[4][:, 0:D], scalar=rz[:, 0:1],
                                             in1=x1_all[:, bass.ds(i * D, D)], op0=ALU.mult, op1=ALU.add) \
                       .then_inc(row_o_ready, 1)


_INPUTS = ["x", "adj", "adj_t", "L0_gnn_W_sa", "L0_gnn_a_sa", "L0_gnn_W_gcnb", "L0_gnn_b_gcnb", "gate_w",
           "L0_gnn_ba", "L0_gnn_bb", "L1_gnn_ptr", "L1_gnn_Wq", "L1_gnn_Wk", "WvT", "bq_bk", "L1_gnn_bv"]


def kernel(**inputs):
    import numpy as np
    import concourse.bacc as bacc
    from concourse.bass_utils import run_bass_kernel_spmd

    given = {name: np.ascontiguousarray(a) for name, a in inputs.items()}
    given["adj_t"] = np.ascontiguousarray(given["adj"].T)
    given["WvT"] = np.ascontiguousarray(given["L1_gnn_Wv"].T)
    both = np.stack([given["L0_gnn_Wa"].reshape(2, -1, P), given["L0_gnn_Wb"].reshape(2, -1, P)], axis=1)
    given["gate_w"] = np.ascontiguousarray(both.transpose(3, 2, 0, 1).reshape(P, -1, 4))
    biases = np.stack([given["L1_gnn_bq"].reshape(-1, P), given["L1_gnn_bk"].reshape(-1, P)])
    given["bq_bk"] = np.ascontiguousarray(biases.transpose(2, 1, 0))

    nc = bacc.Bacc("TRN2", target_bir_lowering=False, num_devices=1)
    arrays, args = {}, []
    for name in _INPUTS:
        arrays[f"in_{name}"] = given[name]
        args.append(nc.dram_tensor(f"in_{name}", given[name].shape, mybir.dt.from_np(given[name].dtype),
                                   kind="ExternalInput").ap())
    args.append(nc.dram_tensor("out", given["x"].shape, F32, kind="ExternalOutput").ap())
    two_graph_layers(nc, *args)
    return run_bass_kernel_spmd(nc, [arrays], core_ids=[0]).results[0]["out"]
```

```python
from contextlib import ExitStack

import concourse.bass as bass
from concourse import mybir

P = 128
F32 = mybir.dt.float32
F16 = mybir.dt.float16
BF16 = mybir.dt.bfloat16
I32 = mybir.dt.int32
ALU = mybir.AluOpType
ACT = mybir.ActivationFunctionType
AX = mybir.AxisListType.X

SLOPE = 0.01
LN_EPS = 1e-5
ATTN_EPS = 1e-5
OFF = -1e6
H_SCALE = 2.0 ** 11
E_SCALE = 2.0 ** 15
TINY = 1e-30


def two_graph_layers(nc, x, adj, adj_t, W_sa, a_sa, W_gcnb, b_gcnb, gate_w, ba, bb, ptr,
                     Wq, Wk, WvT, bq_bk, bv, out):
    N, D = x.shape
    NP = ptr.shape[0]
    NT = N // P
    KT = D // P
    CT = 4
    NC = NT // CT
    CW = CT * P
    RING = 4
    PAIRS = NT // 2
    E1 = D + 2
    B1 = D + 4
    CHUNK = NT * CW
    PW = 2 * CW
    N_LOADS = 7
    QK_SCALE = float(D) ** -0.5

    with ExitStack() as ctx:
        def sb(name, shape, dt=F32):
            return ctx.enter_context(nc.sbuf_tensor(name, shape, dt))

        def sem(name):
            return ctx.enter_context(nc.semaphore(name))

        adjt = sb("adjt", [P, 2 * CHUNK])
        hb16 = sb("hb16", [P, NT, 2, B1], F16)
        hd16 = sb("hd16", [P, NT, 2, E1], F16)
        s_row = sb("s_row", [P, N])
        e_raw = sb("e_raw", [P, 2 * PW])
        e_mask = sb("e_mask", [P, 2 * PW])
        e_hi = sb("e_hi", [P, RING * PW], F16)
        e_lo = sb("e_lo", [P, RING * PW], F16)
        x1_all = sb("x1_all", [P, NT * D])
        diag = sb("diag", [P, N])
        mask = sb("mask", [P, N], BF16)
        fac = sb("fac", [P, CW])
        x_in = sb("x_in", [P, CT, D])
        xb = sb("xb", [P, CT, D])
        xa = sb("xa", [P, CT, D])
        gid_row = sb("gid_row", [P, N], BF16)
        ident = sb("ident", [P, P])
        ones = sb("ones", [P, P])
        ones_b = sb("ones_b", [P, P], BF16)

        w_sa = sb("w_sa", [P, KT, D])
        w_b = sb("w_b", [P, KT, E1])
        w_v = sb("w_v", [P, KT, D + 1])
        w_qk = sb("w_qk", [P, KT, D])
        w4 = sb("w4", [P, KT, 4])
        wl_wide = sb("wl_wide", [P, KT, P])
        a_row = sb("a_row", [P, 2, D])
        bg_row = sb("bg_row", [P, D])
        bv_row = sb("bv_row", [P, D + 1])
        gate_bias = sb("gate_bias", [P, 2])
        bqk_col = sb("bqk_col", [P, KT, 2])
        bq_wide = sb("bq_wide", [P, KT, P])
        u_col = sb("u_col", [P, KT])
        ptr_i = sb("ptr_i", [NP, 1], I32)
        ptr_f = sb("ptr_f", [NP, 1])
        gid_col = sb("gid_col", [P, NT])
        sq = sb("sq", [P, KT, 4])
        norm_sq = sb("norm_sq", [P, 3])
        norm_inv = sb("norm_inv", [P, 3])
        norm = sb("norm", [P, 3])
        norm_h = sb("norm_h", [P, 3])
        hc = sb("hc", [P, NT, 4])
        st6 = sb("st6", [P, NT, 6])
        mv = sb("mv", [P, NT, 2])
        var_e = sb("var_e", [P, NT])
        half_neg = sb("half_neg", [P, NT])
        rstd = sb("rstd", [P, NT])
        ln_b = sb("ln_b", [P, NT])
        nbias = sb("nbias", [P, NT])
        dp = sb("dp", [P, NT])
        dp_s = sb("dp_s", [P, NT])
        es = sb("es", [P, NT])
        rm = sb("rm", [P, 4])
        den = sb("den", [P, CT])
        rden = sb("rden", [P, CT])
        ga = sb("ga", [P, CT])
        gz = sb("gz", [P, CT, 2])
        gt = sb("gt", [P, CT, 2])
        gates = sb("gates", [P, CT, 2])
        st6b = sb("st6b", [P, CT, 6])
        mvb = sb("mvb", [P, CT, 2])
        veb = sb("veb", [P, CT])
        rs_all = sb("rs_all", [P, NT])
        nb_all = sb("nb_all", [P, NT])
        deg = sb("deg", [P, NT])
        deg_w = sb("deg_w", [P, NT])
        off_1 = sb("off_1", [P, NT])
        off_0 = sb("off_0", [P, NT])
        mn = sb("mn", [P, NT])
        mn_b = sb("mn_b", [P, NT])
        eo = sb("eo", [P, NT])
        z_one = sb("z_one", [P, NT])
        z_off = sb("z_off", [P, NT])
        diff = sb("diff", [1, NT])
        off_score = sb("off_score", [P, 1])
        general = sb("general", [1, 1], I32)

        wq = e_mask[:, 0:KT * D].rearrange("p (k d) -> p k d", k=KT)
        wk = e_mask[:, PW:PW + KT * D].rearrange("p (k d) -> p k d", k=KT)
        iota_n = s_row[0:NP, :]
        cmp_ptr = e_hi[0:NP, 0:N].bitcast(BF16)
        hT = x1_all[:, :].rearrange("p (k n) -> p k n", k=KT)
        xs = adjt[:, CHUNK:CHUNK + NT * D].rearrange("p (t d) -> p t d", d=D)
        h = adjt[:, CHUNK + NT * D:2 * CHUNK].rearrange("p (t d) -> p t d", d=D)

        h1T_all = adjt[:, 0:NT * D].rearrange("p (k n) -> p k n", k=KT)
        v_all = adjt[:, NT * D:2 * NT * D]
        adj_row = adjt[:, 2 * NT * D:2 * NT * D + N]
        score_row = adjt[:, 2 * NT * D + N:2 * NT * D + 2 * N]
        c_all = adjt[:, 3 * NT * D:3 * NT * D + NT]
        mask_row = s_row
        fac_row = e_hi[:, :].bitcast(F32)
        prob_row = e_lo[:, :].bitcast(F32)
        probT_row = e_raw

        h1, h1T, gT, o_sb = (e_mask[:, 512 * n:512 * n + 512].rearrange("p (q n) -> p q n", q=2)
                             for n in range(4))
        v_sb = sb("v_sb", [P, 2, D + 2])
        sc3, probm, pT = (e_raw[:, 256 * n:256 * n + 256].rearrange("p (q n) -> p q n", q=2)
                          for n in range(3))
        sc1 = e_raw[:, 768:768 + P]
        prob = e_raw[:, 896:896 + P]
        neg_mw = sb("neg_mw", [P, 1])
        neg_m = sb("neg_m", [P, 2])
        zw = sb("zw", [P, 2])
        fo = sb("fo", [P, 1])
        zs = sb("zs", [P, 1])
        rz = sb("rz", [P, 2])

        bank = [ctx.enter_context(nc.psum_tensor(f"bank{b}", [P, 512], F32)) for b in range(8)]
        S_S, P_T, H_T, G_T, V_S = bank[0], bank[3], bank[4], bank[5], bank[6]
        PV = [bank[1], bank[2]]
        V = [bank[6], bank[7]]

        x_loaded = [sem(f"x_loaded{m}") for m in range(CT)]
        layer0_loaded = sem("layer0_loaded")
        layer1_loaded = sem("layer1_loaded")
        consts_made = sem("consts_made")
        iota_made = sem("iota_made")
        ptr_made = sem("ptr_made")
        cmp_made = sem("cmp_made")
        gid_summed = sem("gid_summed")
        gid_kept = sem("gid_kept")
        w_made = sem("w_made")
        wide_made = sem("wide_made")
        sq_made = sem("sq_made")
        norm_summed = sem("norm_summed")
        norm_made = sem("norm_made")
        inv_made = sem("inv_made")
        w_scaled = sem("w_scaled")
        qk_summed = sem("qk_summed")
        qk_kept = sem("qk_kept")
        stats_made = sem("stats_made")
        moments_made = sem("moments_made")
        var_made = sem("var_made")
        rstd_made = sem("rstd_made")
        lnb_made = sem("lnb_made")
        h_made = sem("h_made")
        h_turned = sem("h_turned")
        hT_kept_a = sem("hT_kept_a")
        hT_kept_v = sem("hT_kept_v")
        hb_summed = sem("hb_summed")
        hb_hi_made = sem("hb_hi_made")
        hb_lo_made = sem("hb_lo_made")
        cols_summed = sem("cols_summed")
        cols_kept = sem("cols_kept")
        rows_summed = sem("rows_summed")
        rows_kept = sem("rows_kept")
        rmin_v = sem("rmin_v")
        rmin_t = sem("rmin_t")
        bias_made = sem("bias_made")
        factors_made = sem("factors_made")
        dp_scaled = sem("dp_scaled")
        hd_summed = sem("hd_summed")
        hd_hi_made = sem("hd_hi_made")
        hd_lo_made = sem("hd_lo_made")
        score_made = sem("score_made")
        adjt_loaded = [sem(f"adjt_loaded{m}") for m in range(CT)]
        x_read = sem("x_read")
        diag_loaded = sem("diag_loaded")
        raw_ready = sem("raw_ready")
        mask_ready = sem("mask_ready")
        hi_ready = sem("hi_ready")
        lo_ready = sem("lo_ready")
        slot_free = sem("slot_free")
        b_summed = sem("b_summed")
        b_kept = sem("b_kept")
        t_kept = sem("t_kept")
        z_ready = sem("z_ready")
        tz_ready = sem("tz_ready")
        deg_ready = sem("deg_ready")
        deg_w_ready = sem("deg_w_ready")
        den_ready = sem("den_ready")
        rden_ready = sem("rden_ready")
        gates_ready = sem("gates_ready")
        ga_ready = sem("ga_ready")
        u_ready = sem("u_ready")
        th_ready = sem("th_ready")
        half_ready = sem("half_ready")
        x1_ready = sem("x1_ready")
        stats_ready = sem("stats_ready")
        mvb_ready = sem("mvb_ready")
        ve_ready = sem("ve_ready")
        rs_ready = sem("rs_ready")
        nb_ready = sem("nb_ready")
        off_made = sem("off_made")
        off_ready = sem("off_ready")
        off_exp = sem("off_exp")
        passed = sem("passed")
        h1_ready = sem("h1_ready")
        h1_turned = sem("h1_turned")
        h1T_kept = sem("h1T_kept")
        g_summed = sem("g_summed")
        v_summed = sem("v_summed")
        g_kept = sem("g_kept")
        v_kept = sem("v_kept")
        msk_ready = sem("msk_ready")
        fac_ready = sem("fac_ready")
        s_summed = sem("s_summed")
        s1_ready = sem("s1_ready")
        adj_f_ready = sem("adj_f_ready")
        s3_ready = sem("s3_ready")
        mw_ready = sem("mw_ready")
        m_ready = sem("m_ready")
        p_ready = sem("p_ready")
        fo_ready = sem("fo_ready")
        pm_ready = sem("pm_ready")
        z_sum = sem("z_sum")
        rz_ready = sem("rz_ready")
        p_turned = sem("p_turned")
        pT_kept = sem("pT_kept")
        pv_summed = sem("pv_summed")
        o_ready = sem("o_ready")
        o_stored = [sem(f"o_stored{q}") for q in range(2)]
        flag_made = sem("flag_made")
        all_h1 = sem("all_h1")
        all_h1_turned = sem("all_h1_turned")
        all_h1T_kept = sem("all_h1T_kept")
        all_v_summed = sem("all_v_summed")
        all_v_kept = sem("all_v_kept")
        row_loaded = sem("row_loaded")
        row_g_summed = sem("row_g_summed")
        row_g_kept = sem("row_g_kept")
        row_s_summed = sem("row_s_summed")
        row_masked = sem("row_masked")
        row_scored = sem("row_scored")
        row_m_ready = sem("row_m_ready")
        row_p_ready = sem("row_p_ready")
        row_pm_ready = sem("row_pm_ready")
        row_p_turned = sem("row_p_turned")
        row_pT_kept = sem("row_pT_kept")
        row_pv_summed = sem("row_pv_summed")
        row_o_ready = sem("row_o_ready")
        row_stored = sem("row_stored")

        block = ctx.enter_context(nc.Block())

        def wait(eng, signal, value):
            if not isinstance(value, int) or value > 0:
                eng.wait_ge(signal, value)

        def apart(eng):
            eng.sem_inc(passed, 1)

        def if_general(eng):
            eng.wait_ge(o_ready, NT)
            eng.wait_ge(flag_made, 3)
            return eng.If(eng.value_load(general[0:1, 0:1], min_val=0, max_val=1) > 0)

        LEAD, LAG = 2, 2

        def turns(eng, turn, before=None):
            first = 2 * LAG
            before = before or {}
            last = (NT - LEAD) // 2 * 2

            def written_out(t):
                if t in before:
                    before[t]()
                turn(lambda d: (t + d, (t + d) // 2, (t + d) % 2) if 0 <= t + d < NT else None)

            for t in range(-LEAD, first):
                written_out(t)
            with eng.Fori(first // 2, last // 2) as half:
                for q in range(2):
                    turn(lambda d, q=q: (2 * half + (q + d), half + (q + d) // 2, (q + d) % 2))
            for t in range(last, NT + LAG):
                written_out(t)

        def chunks(eng, turn):
            turn(0, None)
            with eng.Fori(1, NC) as k:
                turn(k, k - 1)

        @block.sync
        def _(eng):
            def load_adjt(k, m):
                base = (k % 2) * CHUNK + CT * m * CW
                eng.dma_start(adjt[:, bass.ds(base, CT * CW)].rearrange("p (t c) -> p t c", c=CW),
                              adj_t[m * CW:(m + 1) * CW, bass.ds(k * CW, CW)]
                              .rearrange("(t p) c -> p t c", p=P)).then_inc(adjt_loaded[m], 16)

            def load_x(k):
                eng.dma_start(x_in[:, :, :], x[bass.ds(k * CW, CW), :].rearrange("(t p) d -> p t d", p=P)) \
                   .then_inc(x_read, 16)

            for g in range(CT):
                eng.dma_start(xs[:, CT * g:CT * g + CT, :],
                              x[g * CW:(g + 1) * CW, :].rearrange("(t p) d -> p t d", p=P)) \
                   .then_inc(x_loaded[g], 16)
            eng.wait_ge(x_loaded[CT - 1], 16)
            for m in range(CT):
                load_adjt(0, m)
            load_x(0)
            eng.wait_ge(h_turned, NT // 2)
            eng.wait_ge(h_made, NT)
            for m in range(CT):
                eng.wait_ge(adjt_loaded[m], 16)
                load_adjt(1, m)
            with eng.Fori(0, NT) as i:
                eng.dma_start(diag[:, bass.ds(i * P, P)],
                              adj[bass.ds(i * P, P), bass.ds(i * P, P)]).then_inc(diag_loaded, 16)

            with eng.Fori(0, NC - 2) as k:
                eng.wait_ge(b_summed, CT * (k + 1))
                for m in range(CT):
                    eng.wait_ge(mask_ready, PAIRS * k + 2 * (m + 1) + 2)
                    eng.wait_ge(adjt_loaded[m], 16 * (k + 2))
                    apart(eng)
                    load_adjt(k + 2, m)
                eng.wait_ge(x1_ready, k + 2)
                apart(eng)
                load_x(k + 1)
            eng.wait_ge(x1_ready, NC)
            load_x(NC - 1)

            def turn(at):
                if at(-2):
                    i, half, q = at(-2)
                    eng.wait_ge(o_ready, i + 1)
                    eng.dma_start(out[bass.ds(i * P, P), :], o_sb[:, q, :]).then_inc(o_stored[q], 16)

            turns(eng, turn)
            for q in range(2):
                eng.wait_ge(o_stored[q], 16 * (NT // 2))
            with if_general(eng):
                with eng.Fori(0, NT) as i:
                    eng.dma_start(adj_row, adj[bass.ds(i * P, P), :]).then_inc(row_loaded, 16)
                    eng.wait_ge(row_o_ready, i + 1)
                    eng.dma_start(out[bass.ds(i * P, P), :], o_sb[:, 0, :]).then_inc(row_stored, 16)
                    eng.wait_ge(row_stored, 16 * (i + 1))
                    apart(eng)

        @block.gpsimd
        def _(eng):
            eng.memset(ident[:, :], 0.0).then_inc(consts_made, 1)
            eng.memset(ones[:, :], 1.0).then_inc(consts_made, 1)
            eng.memset(ones_b[:, :], 1.0).then_inc(consts_made, 1)
            eng.memset(half_neg[:, :], -0.5).then_inc(consts_made, 1)
            eng.wait_ge(consts_made, 4)
            eng.affine_select(out=ident[:, :], in_=ident[:, :], compare_op=ALU.not_equal, fill=1.0, base=0,
                              pattern=[[-1, P]], channel_multiplier=1).then_inc(consts_made, 1)
            eng.iota(iota_n, pattern=[[1, N]], base=0, channel_multiplier=0,
                     allow_small_or_imprecise_dtypes=True).then_inc(iota_made, 1)

            def inv_deviation(g):
                eng.wait_ge(var_made, g + 1)
                eng.tensor_tensor(rstd[:, CT * g:CT * g + CT], var_e[:, CT * g:CT * g + CT],
                                  half_neg[:, CT * g:CT * g + CT], ALU.pow).then_inc(rstd_made, 1)

            inv_deviation(0)
            eng.wait_ge(norm_made, 1)
            eng.tensor_tensor(norm_inv[:, :], norm_sq[:, :], half_neg[:, 0:3], ALU.pow).then_inc(inv_made, 1)
            for g in range(1, CT):
                inv_deviation(g)
            eng.memset(hb16[:, :, 0, D + 2], 1.0).then_inc(consts_made, 1)

            def add_half(k):
                eng.wait_ge(x_read, 16 * (k + 1))
                apart(eng)
                eng.tensor_scalar(x_in[:, :, :], x_in[:, :, :], 0.5, None, ALU.add).then_inc(half_ready, 1)

            def inv_deviations(k):
                eng.wait_ge(mvb_ready, CT * (k + 1))
                apart(eng)
                eng.tensor_scalar(veb[:, :], mvb[:, :, 1], LN_EPS, None, ALU.add).then_inc(ve_ready, 1)
                eng.wait_ge(ve_ready, k + 1)
                eng.tensor_tensor(rs_all[:, bass.ds(CT * k, CT)], veb[:, :], half_neg[:, 0:CT], ALU.pow) \
                   .then_inc(rs_ready, 1)

            with eng.Fori(0, NC) as k:
                add_half(k)
                inv_deviations(k)

        @block.scalar
        def _(eng):
            def rows(v, n):
                return v.rearrange("(a n) -> a n", a=1).broadcast_to([P, n])

            loads = [
                (layer0_loaded, [
                    (w_sa[:, :, :], W_sa.rearrange("(k p) d -> p k d", p=P)),
                    (a_row[:, :, :].rearrange("p a d -> p (a d)"), a_sa.broadcast_to([P, 2 * D])),
                    (w_b[:, :, 0:D], W_gcnb.rearrange("(k p) d -> p k d", p=P)),
                    (w_b[:, :, D:D + 2], gate_w[:, :, 0:2]),
                    (w4[:, :, 2:4], gate_w[:, :, 2:4]),
                    (gate_bias[:, 0:1], rows(ba, 1)),
                    (gate_bias[:, 1:2], rows(bb, 1))]),
                (layer1_loaded, [
                    (ptr_i[:, :], ptr.rearrange("(g a) -> g a", a=1)),
                    (wq, Wq.rearrange("(k p) d -> p k d", p=P)),
                    (wk, Wk.rearrange("(k p) d -> p k d", p=P)),
                    (bqk_col[:, :, :], bq_bk),
                    (w_v[:, :, 0:D], WvT.rearrange("(k p) d -> p k d", p=P)),
                    (bg_row[:, :], rows(b_gcnb, D)),
                    (bv_row[:, 0:D], rows(bv, D))]),
            ]
            for signal, group in loads:
                assert len(group) == N_LOADS
                for to, source in group:
                    eng.dma_start(to, source).then_inc(signal, 16)
            eng.preload_act_table(ACT.Exp)
            eng.sem_inc(hi_ready, 2)
            eng.sem_inc(t_kept, CT)

            def h_tiles(g):
                eng.wait_ge(x_loaded[g], 16)
                eng.wait_ge(lnb_made, g + 1)
                for t in range(CT * g, CT * g + CT):
                    eng.activation(h[:, t, :], xs[:, t, :], ACT.Relu, scale=rstd[:, t:t + 1],
                                   bias=ln_b[:, t:t + 1]).then_inc(h_made, 1)

            def keep_hT(g):
                eng.wait_ge(h_turned, g + 1)
                eng.activation(hT[:, :, 2 * P * g:2 * P * (g + 1)],
                               bank[g % 2][:, :].rearrange("p (k n) -> p k n", k=KT), ACT.Copy) \
                   .then_inc(hT_kept_a, 1)

            def hb_high(t):
                eng.wait_ge(hb_summed, t + 1)
                eng.activation(hb16[:, t, 0, 0:D + 2], bank[2 + t % 4][:, 0:D + 2], ACT.Copy, scale=H_SCALE) \
                   .then_inc(hb_hi_made, 1)

            h_tiles(0)
            for g in range(CT):
                keep_hT(2 * g)
                if g + 1 < CT:
                    h_tiles(g + 1)
                for t in range(CT * g, CT * g + CT):
                    hb_high(t)
            eng.wait_ge(cols_kept, 1)
            eng.activation(nbias[:, :], hc[:, :, 1], ACT.Copy, scale=SLOPE - 1.0).then_inc(bias_made, 1)
            eng.wait_ge(rmin_v, 4)
            eng.activation(dp[:, :], hc[:, :, 1], ACT.Exp, scale=-SLOPE, bias=rm[:, 3:4]) \
               .then_inc(factors_made, 1)
            eng.activation(es[:, :], hc[:, :, 0], ACT.Exp, scale=SLOPE, bias=rm[:, 3:4]) \
               .then_inc(factors_made, 1)
            for c in range(4):
                eng.wait_ge(rows_summed, c + 1)
                if c == 0:
                    eng.wait_ge(cmp_made, 1)
                eng.activation(s_row[:, c * 512:(c + 1) * 512], bank[c][:, :], ACT.Copy) \
                   .then_inc(rows_kept, 1)
            eng.wait_ge(dp_scaled, 1)
            for t in range(NT):
                eng.wait_ge(hd_summed, t + 1)
                eng.activation(hd16[:, t, 0, 0:D], bank[4 + t % 4][:, 0:D], ACT.Copy,
                               scale=dp_s[:, t:t + 1]).then_inc(hd_hi_made, 1)
            eng.activation(hd16[:, :, 0, D], dp_s[:, :], ACT.Copy).then_inc(hd_hi_made, 1)

            eng.wait_ge(rows_kept, 4)
            eng.wait_ge(bias_made, 1)
            eng.wait_ge(w_made, 2 * KT)
            eng.wait_ge(sq_made, 3 * KT)
            eng.wait_ge(gid_summed, 5)

            def raw(k, m):
                for q in range(2):
                    eng.wait_ge(mask_ready, PAIRS * k + 2 * m + q + 1)
                    apart(eng)
                    for n in range(2):
                        j = CT * m + 2 * q + n
                        ins = eng.activation(e_raw[:, q * PW + n * CW:q * PW + (n + 1) * CW],
                                             s_row[:, bass.ds(k * CW, CW)], ACT.Exp,
                                             scale=SLOPE - 1.0, bias=nbias[:, j:j + 1])
                    ins.then_inc(raw_ready, 1)

            def high(k, m):
                for q in range(2):
                    slot = (2 * m + q) % RING
                    eng.wait_ge(mask_ready, PAIRS * k + 2 * m + q + 3)
                    eng.wait_ge(slot_free, PAIRS * k + 2 * m + q + 1)
                    eng.activation(e_hi[:, slot * PW:(slot + 1) * PW], e_mask[:, q * PW:(q + 1) * PW],
                                   ACT.Copy, scale=E_SCALE).then_inc(hi_ready, 1)

            def keep_a(p):
                eng.wait_ge(ga_ready, p + 1)
                eng.wait_ge(x1_ready, p + 1)
                for r in range(CT):
                    eng.activation(xa[:, r, :], bank[r][:, 0:D], ACT.Copy, scale=ga[:, r:r + 1]) \
                       .then_inc(t_kept, 1)

            def tanh_mix(p):
                eng.wait_ge(u_ready, p + 1)
                eng.activation(xa[:, :, :], xa[:, :, :], ACT.Tanh, scale=0.5).then_inc(th_ready, 1)

            def turn(k, p):
                raw(k, 0)
                high(k, 0)
                raw(k, 1)
                if p is not None:
                    keep_a(p)
                high(k, 1)
                raw(k, 2)
                if p is not None:
                    tanh_mix(p)
                high(k, 2)
                raw(k, 3)
                high(k, 3)
                eng.wait_ge(z_ready, k + 1)
                eng.wait_ge(gates_ready, k + 1)
                eng.activation(gt[:, :, :], gz[:, :, :], ACT.Tanh, scale=0.5).then_inc(tz_ready, 1)

            chunks(eng, turn)

            eng.wait_ge(off_ready, 1)
            eng.activation(eo[:, :], mn_b[:, :], ACT.Exp, bias=off_score[:, 0:1]).then_inc(off_exp, 1)

            def turn(at):
                if at(1):
                    i, half, q = at(1)
                    eng.wait_ge(h1_turned, i + 1)
                    wait(eng, s_summed, i - 1)
                    eng.activation(h1T[:, q, :], H_T[:, 0:D], ACT.Copy).then_inc(h1T_kept, 1)
                if at(2):
                    i, half, q = at(2)
                    wait(eng, h1_turned, i - 1)
                    apart(eng)
                    eng.activation(h1[:, q, :], x1_all[:, bass.ds(i * D, D)], ACT.Relu,
                                   scale=rs_all[:, bass.ds(i, 1)], bias=nb_all[:, bass.ds(i, 1)]) \
                       .then_inc(h1_ready, 1)
                if at(0):
                    i, half, q = at(0)
                    eng.wait_ge(g_summed, i + 1)
                    wait(eng, s_summed, i - 1)
                    for c in range(KT):
                        eng.activation(gT[:, q, c * P:(c + 1) * P], G_T[:, c * P:(c + 1) * P],
                                       ACT.Identity, scale=QK_SCALE, bias=u_col[:, c:c + 1]) \
                           .then_inc(g_kept, 1)
                if at(-2):
                    i, half, q = at(-2)
                    eng.wait_ge(p_turned, i + 1)
                    wait(eng, pv_summed, i - 1)
                    eng.activation(pT[:, q, :], P_T[:, 0:P], ACT.Copy).then_inc(pT_kept, 1)
                if at(-1):
                    i, half, q = at(-1)
                    eng.wait_ge(m_ready, i + 1)
                    wait(eng, pm_ready, i)
                    eng.activation(prob[:, :], sc3[:, q, :], ACT.Exp, bias=neg_m[:, q:q + 1],
                                   accum_out=zw[:, q:q + 1]).then_inc(p_ready, 1)
                    wait(eng, z_sum, i)
                    eng.activation(fo[:, :], mn[:, bass.ds(i, 1)], ACT.Exp, scale=2.0 * OFF,
                                   bias=neg_m[:, q:q + 1]).then_inc(fo_ready, 1)

            eng.wait_ge(lo_ready, PAIRS * NC)
            eng.wait_ge(nb_ready, NC - 1)
            turns(eng, turn, {0: lambda: keep_a(NC - 1), 1: lambda: tanh_mix(NC - 1),
                              3: lambda: eng.wait_ge(nb_ready, NC)})
            with if_general(eng):
                eng.sem_inc(all_v_summed, 1)
                with eng.Fori(0, NT) as i:
                    eng.activation(h1[:, 0, :], x1_all[:, bass.ds(i * D, D)], ACT.Relu,
                                   scale=rs_all[:, bass.ds(i, 1)], bias=nb_all[:, bass.ds(i, 1)]) \
                       .then_inc(all_h1, 1)
                    eng.wait_ge(all_h1_turned, i + 1)
                    eng.wait_ge(all_v_summed, i + 1)
                    apart(eng)
                    eng.activation(h1T[:, 0, :], H_T[:, 0:D], ACT.Copy).then_inc(all_h1T_kept, 1)
                    eng.activation(h1T_all[:, :, bass.ds(i * P, P)],
                                   H_T[:, 0:D].rearrange("p (k n) -> p k n", k=KT), ACT.Copy) \
                       .then_inc(all_h1T_kept, 1)
                with eng.Fori(0, NT) as i:
                    eng.wait_ge(row_g_summed, i + 1)
                    apart(eng)
                    for c in range(KT):
                        eng.activation(gT[:, 0, c * P:(c + 1) * P], G_T[:, c * P:(c + 1) * P], ACT.Identity,
                                       scale=QK_SCALE, bias=u_col[:, c:c + 1]).then_inc(row_g_kept, 1)
                    eng.wait_ge(row_m_ready, i + 1)
                    apart(eng)
                    eng.activation(prob_row, score_row, ACT.Exp, bias=neg_m[:, 0:1], accum_out=zw[:, 0:1]) \
                       .then_inc(row_p_ready, 1)
                    for g in range(NT // CT):
                        eng.wait_ge(row_p_turned, CT * i + g + 1)
                        apart(eng)
                        eng.activation(probT_row[:, g * 512:(g + 1) * 512], bank[4 + g][:, :], ACT.Copy) \
                           .then_inc(row_pT_kept, 1)

        @block.tensor
        def _(eng):
            eng.wait_ge(consts_made, 5)
            eng.wait_ge(sq_made, 3 * KT)
            for kk in range(KT):
                mm = eng.matmul(bank[7][:, 0:3], ones[:, :], sq[:, kk, 0:3], start=(kk == 0), stop=(kk == KT - 1))
            mm.then_inc(norm_summed, 1)

            def turn_h(g):
                eng.wait_ge(h_made, 2 * g + 2)
                if g >= 2:
                    if g % 2 == 0:
                        eng.wait_ge(hT_kept_a, g // 2)
                    else:
                        eng.wait_ge(hT_kept_v, g // 2)
                for c in range(KT):
                    for n in range(2):
                        mm = eng.transpose(bank[g % 2][:, (2 * c + n) * P:(2 * c + n + 1) * P],
                                           h[:, 2 * g + n, c * P:(c + 1) * P], ident[:, :])
                mm.then_inc(h_turned, 1)

            def times_weights(g):
                if g % 2 == 0:
                    eng.wait_ge(hT_kept_a, g // 2 + 1)
                else:
                    eng.wait_ge(hT_kept_v, g // 2 + 1)
                for t in range(2 * g, 2 * g + 2):
                    if t >= 4:
                        eng.wait_ge(hb_lo_made, t - 3)
                    for kk in range(KT):
                        mm = eng.matmul(bank[2 + t % 4][:, 0:D + 2], hT[:, kk, t * P:(t + 1) * P], w_b[:, kk, :],
                                        start=(kk == 0), stop=(kk == KT - 1))
                    mm.then_inc(hb_summed, 1)
                    for kk in range(KT):
                        mm = eng.matmul(bank[6][:, 4 * t:4 * t + 4], hT[:, kk, t * P:(t + 1) * P], w4[:, kk, :],
                                        start=(kk == 0), stop=(kk == KT - 1))
                    mm.then_inc(cols_summed, 1)

            turn_h(0)
            eng.wait_ge(w_made, 2 * KT)
            eng.wait_ge(w_scaled, 3)
            for g in range(1, NT // 2):
                turn_h(g)
                times_weights(g - 1)
            times_weights(NT // 2 - 1)
            eng.wait_ge(wide_made, KT)
            for c in range(4):
                if c >= 2:
                    eng.wait_ge(hb_lo_made, NT - 4 + c - 1)
                for kk in range(KT):
                    mm = eng.matmul(bank[c][:, :], wl_wide[:, kk, :], hT[:, kk, c * 512:(c + 1) * 512],
                                    start=(kk == 0), stop=(kk == KT - 1))
                mm.then_inc(rows_summed, 1)
                if c == 0:
                    eng.wait_ge(rmin_v, 1)
                    eng.transpose(bank[7][0:1, 0:P], rm[:, 0:1], ident[:, :]).then_inc(rmin_t, 1)
                if c == 1:
                    eng.wait_ge(rmin_v, 2)
                    eng.matmul(bank[7][:, 2 * P:2 * P + 1], ones[0:1, :], rm[0:1, 1:2], start=True, stop=True) \
                       .then_inc(rmin_t, 1)
            for t in range(NT):
                if t < 2:
                    eng.wait_ge(hb_lo_made, NT - 1 + t)
                elif t == 2:
                    eng.wait_ge(cols_kept, 1)
                elif t == 3:
                    eng.wait_ge(rmin_v, 4)
                else:
                    eng.wait_ge(hd_lo_made, t - 3)
                for kk in range(KT):
                    mm = eng.matmul(bank[4 + t % 4][:, 0:D], hT[:, kk, t * P:(t + 1) * P], w_sa[:, kk, :],
                                    start=(kk == 0), stop=(kk == KT - 1))
                mm.then_inc(hd_summed, 1)
            eng.wait_ge(layer1_loaded, 16 * N_LOADS)
            eng.wait_ge(wide_made, 2 * KT)
            eng.wait_ge(rows_kept, 4)
            for c in range(KT):
                for kk in range(KT):
                    mm = eng.matmul(bank[0][:, c * D:(c + 1) * D], wq[:, kk, c * P:(c + 1) * P],
                                    wk[:, kk, :], start=(kk == 0), stop=(kk == KT - 1))
            mm.then_inc(qk_summed, 1)
            for c in range(KT):
                for kk in range(KT):
                    eng.matmul(bank[1][:, c:c + 1], wk[:, kk, c * P:(c + 1) * P], bqk_col[:, kk, 0:1],
                               start=(kk == 0), stop=(kk == KT - 1))
            for c in range(KT):
                for kk in range(KT):
                    eng.matmul(bank[1][:, KT + c:KT + c + 1], wq[:, kk, c * P:(c + 1) * P],
                               bqk_col[:, kk, 1:2], start=(kk == 0), stop=(kk == KT - 1))
            for kk in range(KT):
                mm = eng.matmul(bank[1][:, 2 * KT:2 * KT + 1], bq_wide[:, kk, :], bqk_col[:, kk, 1:2],
                                start=(kk == 0), stop=(kk == KT - 1))
            mm.then_inc(qk_summed, 1)
            eng.wait_ge(cmp_made, 1)
            for c in range(N // 512):
                if c == 2:
                    eng.wait_ge(gid_kept, 1)
                if c == 3:
                    eng.wait_ge(gid_kept, 2)
                mm = eng.matmul(bank[2 + c % 2][:, :], ones_b[0:NP, :], cmp_ptr[:, c * 512:(c + 1) * 512],
                                start=True, stop=True)
                mm.then_inc(gid_summed, 1)
            eng.wait_ge(gid_kept, 3)
            for t in range(NT):
                mm = eng.matmul(bank[2][:, t:t + 1], cmp_ptr[:, t * P:(t + 1) * P], ones_b[0:NP, 0:1],
                                start=True, stop=True)
            mm.then_inc(gid_summed, 1)

            adjt_b = adjt[:, :].bitcast(BF16)

            def adj_group(place, r):
                for j in range(NT):
                    word = place * CHUNK + j * CW + r * P
                    for part in range(2):
                        cols = D + 3 - part
                        mm = eng.matmul(bank[4 + r][:, 0:cols], adjt_b[:, bass.ds(2 * word + 1, P, 2)],
                                        hb16[:, j, part, 0:cols], start=(j == 0 and part == 0),
                                        stop=(j == NT - 1 and part == 1), skip_group_check=True)
                mm.then_inc(b_summed, 1)

            def e_group(k, m):
                for q in range(2):
                    base = ((2 * m + q) % RING) * PW
                    eng.wait_ge(lo_ready, PAIRS * k + 2 * m + q + 1)
                    for n in range(2):
                        j = CT * m + 2 * q + n
                        for r in range(CT):
                            at = base + n * CW + r * P
                            high, low = e_hi[:, at:at + P], e_lo[:, at:at + P]
                            eng.matmul(bank[r][:, 0:D + 1], high, hd16[:, j, 0, 0:D + 1],
                                       start=(j == 0), stop=False, skip_group_check=True)
                            eng.matmul(bank[r][:, 0:D + 1], high, hd16[:, j, 1, 0:D + 1],
                                       start=False, stop=False, skip_group_check=True)
                            mm = eng.matmul(bank[r][:, 0:D + 1], low, hd16[:, j, 0, 0:D + 1],
                                            start=False, stop=(j == NT - 1), skip_group_check=True)
                    mm.then_inc(slot_free, 1)

            eng.wait_ge(hb_lo_made, NT)
            eng.wait_ge(consts_made, 6)
            eng.wait_ge(hd_lo_made, NT + 1)
            with eng.Fori(0, NC // 2) as pair:
                for place in range(2):
                    k = 2 * pair + place
                    for m in range(CT):
                        eng.wait_ge(adjt_loaded[m], 16 * (k + 1))
                    eng.wait_ge(b_kept, CT * k + 1)
                    adj_group(place, 0)
                    eng.wait_ge(b_kept, CT * k + 2)
                    adj_group(place, 1)
                    eng.wait_ge(t_kept, CT * (k + 1))
                    if place == 0:
                        eng.wait_ge(gid_kept, 5)
                        eng.wait_ge(qk_kept, 5)
                    e_group(k, 0)
                    eng.wait_ge(b_kept, CT * k + 3)
                    adj_group(place, 2)
                    e_group(k, 1)
                    eng.wait_ge(b_kept, CT * k + 4)
                    adj_group(place, 3)
                    e_group(k, 2)
                    e_group(k, 3)

            def turn(at):
                if at(1):
                    i, half, q = at(1)
                    eng.wait_ge(h1_ready, i + 1)
                    wait(eng, h1T_kept, i)
                    for c in range(KT):
                        mm = eng.transpose(H_T[:, c * P:(c + 1) * P], h1[:, q, c * P:(c + 1) * P], ident[:, :])
                    mm.then_inc(h1_turned, 1)
                if at(0):
                    i, half, q = at(0)
                    eng.wait_ge(h1T_kept, i + 1)
                    wait(eng, g_kept, KT * i)
                    for c in range(KT):
                        for kk in range(KT):
                            mm = eng.matmul(G_T[:, c * P:(c + 1) * P], w_qk[:, kk, c * P:(c + 1) * P],
                                            h1T[:, q, kk * P:(kk + 1) * P],
                                            start=(kk == 0), stop=(kk == KT - 1))
                    mm.then_inc(g_summed, 1)
                if at(-2):
                    i, half, q = at(-2)
                    eng.wait_ge(pm_ready, i + 1)
                    wait(eng, pT_kept, i)
                    eng.transpose(P_T[:, 0:P], probm[:, q, :], ident[:, :]).then_inc(p_turned, 1)
                if at(0):
                    i, half, q = at(0)
                    wait(eng, v_kept, i - 1)
                    for kk in range(KT):
                        mm = eng.matmul(V[q][:, 0:D + 1], h1T[:, q, kk * P:(kk + 1) * P], w_v[:, kk, :],
                                        start=(kk == 0), stop=(kk == KT - 1))
                    mm.then_inc(v_summed, 1)
                if at(-2):
                    i, half, q = at(-2)
                    eng.wait_ge(pT_kept, i + 1)
                    eng.wait_ge(v_kept, i + 1)
                    wait(eng, o_ready, i - 1)
                    eng.matmul(PV[q][:, 0:D], pT[:, q, :], v_sb[:, q, 0:D], start=True, stop=True) \
                       .then_inc(pv_summed, 1)
                if at(0):
                    i, half, q = at(0)
                    eng.wait_ge(g_kept, KT * (i + 1))
                    wait(eng, s1_ready, i)
                    for kk in range(KT):
                        mm = eng.matmul(S_S[:, 0:P], gT[:, q, kk * P:(kk + 1) * P],
                                        h1T[:, q, kk * P:(kk + 1) * P], start=(kk == 0), stop=(kk == KT - 1))
                    mm.then_inc(s_summed, 1)

            eng.wait_ge(b_kept, CT * (NC + 1))
            eng.wait_ge(qk_kept, 7)
            turns(eng, turn, {0: lambda: eng.wait_ge(t_kept, CT * (NC + 1))})
            with if_general(eng):
                with eng.Fori(0, NT) as i:
                    eng.wait_ge(all_h1, i + 1)
                    apart(eng)
                    for c in range(KT):
                        mm = eng.transpose(H_T[:, c * P:(c + 1) * P], h1[:, 0, c * P:(c + 1) * P], ident[:, :])
                    mm.then_inc(all_h1_turned, 1)
                    eng.wait_ge(all_h1T_kept, 2 * i + 2)
                    eng.wait_ge(all_v_kept, 2 * i + 2)
                    apart(eng)
                    for kk in range(KT):
                        mm = eng.matmul(V_S[:, 0:D + 1], h1T[:, 0, kk * P:(kk + 1) * P], w_v[:, kk, :],
                                        start=(kk == 0), stop=(kk == KT - 1))
                    mm.then_inc(all_v_summed, 1)
                eng.wait_ge(all_v_kept, 2 * NT + 2)
                with eng.Fori(0, NT) as i:
                    for c in range(KT):
                        for kk in range(KT):
                            mm = eng.matmul(G_T[:, c * P:(c + 1) * P], w_qk[:, kk, c * P:(c + 1) * P],
                                            h1T_all[:, kk, bass.ds(i * P, P)],
                                            start=(kk == 0), stop=(kk == KT - 1))
                    mm.then_inc(row_g_summed, 1)
                    eng.wait_ge(row_g_kept, KT * (i + 1))
                    apart(eng)
                    for c in range(N // 512):
                        for kk in range(KT):
                            mm = eng.matmul(bank[c][:, :], gT[:, 0, kk * P:(kk + 1) * P],
                                            h1T_all[:, kk, c * 512:(c + 1) * 512],
                                            start=(kk == 0), stop=(kk == KT - 1))
                    mm.then_inc(row_s_summed, 1)
                    eng.wait_ge(row_pm_ready, i + 1)
                    apart(eng)
                    for g in range(NT // CT):
                        for n in range(CT):
                            mm = eng.transpose(bank[4 + g][:, n * P:(n + 1) * P],
                                               score_row[:, (CT * g + n) * P:(CT * g + n + 1) * P], ident[:, :])
                        mm.then_inc(row_p_turned, 1)
                    eng.wait_ge(row_pT_kept, CT * (i + 1))
                    apart(eng)
                    for j in range(NT):
                        mm = eng.matmul(bank[4][:, 0:D], probT_row[:, j * P:(j + 1) * P],
                                        v_all[:, j * D:(j + 1) * D], start=(j == 0), stop=(j == NT - 1))
                    mm.then_inc(row_pv_summed, 1)
                    eng.wait_ge(row_o_ready, i + 1)
                    apart(eng)

        @block.vector
        def _(eng):
            eng.sem_inc(mask_ready, 2)
            eng.sem_inc(slot_free, RING)
            eng.sem_inc(b_kept, CT)
            eng.sem_inc(x1_ready, 1)
            eng.sem_inc(gates_ready, 1)
            eng.memset(off_score[:, :], 2.0 * OFF).then_inc(score_made, 1)

            def moments(g):
                eng.wait_ge(x_loaded[g], 16)
                for t in range(CT * g, CT * g + CT):
                    eng.bn_stats(st6[:, t, :], xs[:, t, :]).then_inc(stats_made, 1)
                for t in range(CT * g, CT * g + CT):
                    eng.wait_ge(stats_made, t + 1)
                    eng.bn_aggr(mv[:, t, :], st6[:, t, :]).then_inc(moments_made, 1)
                eng.wait_ge(moments_made, CT * g + CT)
                eng.tensor_scalar(var_e[:, CT * g:CT * g + CT], mv[:, CT * g:CT * g + CT, 1], LN_EPS, None,
                                  ALU.add).then_inc(var_made, 1)

            def shift(g):
                eng.wait_ge(rstd_made, g + 1)
                eng.scalar_tensor_tensor(out=ln_b[:, CT * g:CT * g + CT], in0=mv[:, CT * g:CT * g + CT, 0],
                                         scalar=-1.0, in1=rstd[:, CT * g:CT * g + CT],
                                         op0=ALU.mult, op1=ALU.mult).then_inc(lnb_made, 1)

            def keep_hT(g):
                eng.wait_ge(h_turned, g + 1)
                eng.tensor_copy(hT[:, :, 2 * P * g:2 * P * (g + 1)],
                                bank[g % 2][:, :].rearrange("p (k n) -> p k n", k=KT)).then_inc(hT_kept_v, 1)

            def hb_low(t):
                eng.wait_ge(hb_hi_made, t + 1)
                eng.scalar_tensor_tensor(out=hb16[:, t, 1, 0:D + 2], in0=bank[2 + t % 4][:, 0:D + 2],
                                         scalar=H_SCALE, in1=hb16[:, t, 0, 0:D + 2],
                                         op0=ALU.mult, op1=ALU.subtract).then_inc(hb_lo_made, 1)

            moments(0)
            eng.wait_ge(layer0_loaded, 16 * N_LOADS)
            terms = 0
            for kk in range(KT):
                for side, weights in enumerate((w_sa[:, kk, :], w_b[:, kk, 0:D], w_b[:, kk, D:D + 2])):
                    n = weights.shape[1]
                    eng.tensor_tensor_reduce(e_raw[:, terms:terms + n], weights, weights, 1.0, 0.0,
                                             ALU.mult, ALU.add, sq[:, kk, side:side + 1]).then_inc(sq_made, 1)
                    terms += n
            shift(0)
            eng.wait_ge(norm_summed, 1)
            eng.tensor_scalar(norm_sq[:, :], bank[7][:, 0:3], TINY, None, ALU.add).then_inc(norm_made, 1)
            for kk in range(KT):
                for side in range(2):
                    eng.tensor_tensor_reduce(e_mask[:, 512 + side * D:512 + (side + 1) * D] if kk == 0 else
                                             e_mask[:, 1536 + side * D:1536 + (side + 1) * D],
                                             w_sa[:, kk, :], a_row[:, side, :], 1.0, 0.0,
                                             ALU.mult, ALU.add, w4[:, kk, side:side + 1]).then_inc(w_made, 1)
            moments(1)
            eng.wait_ge(inv_made, 1)
            eng.wait_ge(w_made, 2 * KT)
            for side, weights in ((1, w_b[:, :, 0:D]), (2, w_b[:, :, D:D + 2]), (0, w_sa[:, :, :])):
                eng.tensor_scalar(weights, weights, norm_inv[:, side:side + 1], None, ALU.mult) \
                   .then_inc(w_scaled, 1)
            shift(1)
            eng.wait_ge(norm_made, 1)
            eng.tensor_tensor(norm[:, :], norm_sq[:, :], norm_inv[:, :], ALU.mult).then_inc(norm_made, 1)
            eng.wait_ge(norm_made, 2)
            eng.tensor_scalar(norm_h[:, :], norm[:, :], 1.0 / H_SCALE, None, ALU.mult).then_inc(norm_made, 1)
            for kk in range(KT):
                eng.tensor_scalar(wl_wide[:, kk, :], ones[:, :], w4[:, kk, 0:1], None, ALU.mult) \
                   .then_inc(wide_made, 1)
            keep_hT(1)
            for g in range(2, CT):
                moments(g)
                for t in range(4 * (g - 2), 4 * (g - 2) + 2):
                    hb_low(t)
                shift(g)
                for t in range(4 * (g - 2) + 2, 4 * (g - 1)):
                    hb_low(t)
                keep_hT(2 * g - 1)
            for t in range(NT // 2, NT):
                hb_low(t)
                if t == NT // 2 + 3:
                    keep_hT(NT // 2 - 1)
            eng.wait_ge(cols_summed, NT)
            eng.tensor_copy(hc[:, :, :].rearrange("p t c -> p (t c)"), bank[6][:, 0:4 * NT]).then_inc(cols_kept, 1)
            eng.wait_ge(cols_kept, 1)
            eng.tensor_reduce(rm[:, 0:1], hc[:, :, 1], AX, ALU.min).then_inc(rmin_v, 1)
            for c in range(2):
                eng.tensor_scalar(hc[:, :, 2 + c], hc[:, :, 2 + c], gate_bias[:, c:c + 1], None, ALU.add) \
                   .then_inc(cols_kept, 1)
            eng.wait_ge(rmin_t, 1)
            eng.tensor_reduce(rm[0:1, 1:2], bank[7][0:1, 0:P], AX, ALU.min).then_inc(rmin_v, 1)
            eng.wait_ge(layer1_loaded, 16 * N_LOADS)
            eng.tensor_copy(ptr_f[:, :], ptr_i[:, :]).then_inc(ptr_made, 1)
            eng.wait_ge(iota_made, 1)
            eng.wait_ge(ptr_made, 1)
            eng.tensor_scalar(cmp_ptr, iota_n, ptr_f[:, :], None, ALU.is_ge).then_inc(cmp_made, 1)
            eng.wait_ge(rmin_t, 2)
            eng.tensor_copy(rm[:, 2:3], bank[7][:, 2 * P:2 * P + 1]).then_inc(rmin_v, 1)
            eng.wait_ge(rmin_v, 3)
            eng.tensor_scalar(rm[:, 3:4], rm[:, 2:3], SLOPE, None, ALU.mult).then_inc(rmin_v, 1)
            for kk in range(KT):
                eng.tensor_scalar(bq_wide[:, kk, :], ones[:, :], bqk_col[:, kk, 0:1], None, ALU.mult) \
                   .then_inc(wide_made, 1)
            eng.wait_ge(factors_made, 2)
            eng.tensor_scalar(dp_s[:, :], dp[:, :], H_SCALE, None, ALU.mult).then_inc(dp_scaled, 1)
            for t in range(NT):
                eng.wait_ge(hd_hi_made, t + 1)
                if t == 0:
                    eng.wait_ge(dp_scaled, 1)
                eng.scalar_tensor_tensor(out=hd16[:, t, 1, 0:D], in0=bank[4 + t % 4][:, 0:D],
                                         scalar=dp_s[:, t:t + 1], in1=hd16[:, t, 0, 0:D],
                                         op0=ALU.mult, op1=ALU.subtract).then_inc(hd_lo_made, 1)
            eng.wait_ge(hd_hi_made, NT + 1)
            eng.tensor_tensor(hd16[:, :, 1, D], dp_s[:, :], hd16[:, :, 0, D], ALU.subtract) \
               .then_inc(hd_lo_made, 1)
            eng.wait_ge(qk_summed, 2)
            eng.tensor_copy(w_qk[:, :, :].rearrange("p k d -> p (k d)"), bank[0][:, :]).then_inc(qk_kept, 1)
            eng.tensor_scalar(u_col[:, :], bank[1][:, 0:KT], QK_SCALE, None, ALU.mult).then_inc(qk_kept, 1)
            for kk in range(KT):
                eng.tensor_copy(w_v[:, kk, D:D + 1], bank[1][:, KT + kk:KT + kk + 1]).then_inc(qk_kept, 1)
            eng.tensor_copy(bv_row[:, D:D + 1], bank[1][:, 2 * KT:2 * KT + 1]).then_inc(qk_kept, 1)
            eng.wait_ge(qk_kept, 5)
            eng.tensor_scalar(w_v[:, :, D], w_v[:, :, D], QK_SCALE, None, ALU.mult).then_inc(qk_kept, 1)
            eng.tensor_scalar(bv_row[:, D:D + 1], bv_row[:, D:D + 1], QK_SCALE, None, ALU.mult) \
               .then_inc(qk_kept, 1)
            for c in range(N // 512):
                eng.wait_ge(gid_summed, c + 1)
                eng.tensor_copy(gid_row[:, c * 512:(c + 1) * 512], bank[2 + c % 2][:, :]).then_inc(gid_kept, 1)
            eng.wait_ge(gid_summed, 5)
            eng.tensor_copy(gid_col[:, :], bank[2][:, 0:NT]).then_inc(gid_kept, 1)

            def pairs(k, m):
                eng.wait_ge(adjt_loaded[m], 16 * (k + 1))
                for q in range(2):
                    eng.wait_ge(raw_ready, PAIRS * k + 2 * m + q + 1)
                    eng.wait_ge(hi_ready, PAIRS * k + 2 * m + q + 1)
                    wait(eng, lo_ready, PAIRS * k + 2 * m + q - 1)
                    apart(eng)
                    eng.scalar_tensor_tensor(out=e_mask[:, q * PW:(q + 1) * PW],
                                             in0=e_raw[:, q * PW:(q + 1) * PW], scalar=1.0,
                                             in1=adjt[:, bass.ds((k % 2) * CHUNK + (CT * m + 2 * q) * CW, PW)],
                                             op0=ALU.min, op1=ALU.mult).then_inc(mask_ready, 1)
                for q in range(2):
                    slot = (2 * m + q) % RING
                    eng.wait_ge(hi_ready, PAIRS * k + 2 * m + q + 3)
                    eng.scalar_tensor_tensor(out=e_lo[:, slot * PW:(slot + 1) * PW],
                                             in0=e_mask[:, q * PW:(q + 1) * PW], scalar=E_SCALE,
                                             in1=e_hi[:, slot * PW:(slot + 1) * PW],
                                             op0=ALU.mult, op1=ALU.subtract).then_inc(lo_ready, 1)

            def keep_b(k, r):
                eng.wait_ge(b_summed, CT * k + r + 1)
                if r == 0:
                    wait(eng, u_ready, k)
                apart(eng)
                ins = eng.scalar_tensor_tensor(out=gz[:, r, :], in0=bank[4 + r][:, D:D + 2],
                                               scalar=norm_h[:, 2:3], in1=hc_f[:, bass.ds(4 * (CT * k + r) + 2, 2)],
                                               op0=ALU.mult, op1=ALU.add)
                if r == CT - 1:
                    ins.then_inc(z_ready, 1)
                eng.tensor_copy(deg[:, bass.ds(CT * k + r, 1)], bank[4 + r][:, D + 2:D + 3]).then_inc(deg_ready, 1)
                eng.scalar_tensor_tensor(out=xb[:, r, :], in0=bank[4 + r][:, 0:D], scalar=norm_h[:, 1:2],
                                         in1=bg_row[:, :], op0=ALU.mult, op1=ALU.add).then_inc(b_kept, 1)

            def gates_and_denominators(p):
                eng.wait_ge(tz_ready, p + 1)
                eng.tensor_scalar(gates[:, :, :], gt[:, :, :], 0.5, 0.5, ALU.mult, ALU.add) \
                   .then_inc(gates_ready, 1)
                eng.wait_ge(slot_free, RING + PAIRS * (p + 1))
                apart(eng)
                for r in range(CT):
                    ins = eng.scalar_tensor_tensor(out=den[:, r:r + 1], in0=es[:, bass.ds(CT * p + r, 1)],
                                                   scalar=ATTN_EPS * H_SCALE * E_SCALE,
                                                   in1=bank[r][:, D:D + 1], op0=ALU.mult, op1=ALU.add)
                ins.then_inc(den_ready, 1)
                eng.wait_ge(den_ready, p + 1)
                eng.reciprocal(rden[:, :], den[:, :]).then_inc(rden_ready, 1)
                eng.wait_ge(rden_ready, p + 1)
                eng.wait_ge(gates_ready, p + 2)
                eng.scalar_tensor_tensor(out=ga[:, :], in0=rden[:, :], scalar=norm[:, 0:1],
                                         in1=gates[:, :, 0], op0=ALU.mult, op1=ALU.mult).then_inc(ga_ready, 1)

            def mix(p):
                for r in range(CT):
                    eng.wait_ge(t_kept, CT * (p + 1) + r + 1)
                    eng.wait_ge(b_kept, CT * (p + 1) + r + 1)
                    ins = eng.scalar_tensor_tensor(out=xa[:, r, :], in0=xb[:, r, :], scalar=gates[:, r, 1:2],
                                                   in1=xa[:, r, :], op0=ALU.mult, op1=ALU.add)
                ins.then_inc(u_ready, 1)

            def add_mix(p):
                eng.wait_ge(th_ready, p + 1)
                eng.wait_ge(half_ready, p + 1)
                apart(eng)
                eng.scalar_tensor_tensor(out=x1_all[:, bass.ds(CT * D * p, CT * D)],
                                         in0=xa[:, :, :].rearrange("p t d -> p (t d)"), scalar=0.5,
                                         in1=x_in[:, :, :].rearrange("p t d -> p (t d)"),
                                         op0=ALU.mult, op1=ALU.add).then_inc(x1_ready, 1)

            def new_moments(p):
                eng.wait_ge(x1_ready, p + 2)
                apart(eng)
                for r in range(CT):
                    eng.bn_stats(st6b[:, r, :], x1_all[:, bass.ds(CT * D * p + r * D, D)]) \
                       .then_inc(stats_ready, 1)
                for r in range(CT):
                    eng.wait_ge(stats_ready, CT * p + r + 1)
                    apart(eng)
                    eng.bn_aggr(mvb[:, r, :], st6b[:, r, :]).then_inc(mvb_ready, 1)

            def shifts(p):
                eng.wait_ge(rs_ready, p + 1)
                apart(eng)
                eng.scalar_tensor_tensor(out=nb_all[:, bass.ds(CT * p, CT)], in0=mvb[:, :, 0], scalar=-1.0,
                                         in1=rs_all[:, bass.ds(CT * p, CT)],
                                         op0=ALU.mult, op1=ALU.mult).then_inc(nb_ready, 1)

            def window_masks(k):
                eng.wait_ge(diag_loaded, 16 * NT)
                for n in range(CT):
                    t = CT * k + n
                    ins = eng.tensor_scalar(mask[:, bass.ds(t * P, P)], gid_row[:, bass.ds(t * P, P)],
                                            gid_col[:, bass.ds(t, 1)], None, ALU.is_equal)
                ins.then_inc(msk_ready, 1)
                eng.tensor_reduce(deg_w[:, bass.ds(CT * k, CT)],
                                  diag[:, bass.ds(k * CW, CW)].rearrange("p (t n) -> p t n", n=P), AX, ALU.add) \
                   .then_inc(deg_w_ready, 1)

            def window_factors(k):
                eng.wait_ge(msk_ready, k + 1)
                wait(eng, adj_f_ready, k)
                apart(eng)
                eng.tensor_scalar(fac[:, :], mask[:, bass.ds(k * CW, CW)], 1.0 - OFF, OFF, ALU.mult, ALU.add) \
                   .then_inc(fac_ready, 1)

            def window_adj(k):
                eng.wait_ge(fac_ready, k + 1)
                eng.wait_ge(deg_w_ready, k + 1)
                apart(eng)
                eng.scalar_tensor_tensor(out=diag[:, bass.ds(k * CW, CW)], in0=diag[:, bass.ds(k * CW, CW)],
                                         scalar=2.0, in1=fac[:, :], op0=ALU.mult, op1=ALU.mult) \
                   .then_inc(adj_f_ready, 1)

            def turn(k, p):
                pairs(k, 0)
                if p is not None:
                    gates_and_denominators(p)
                pairs(k, 1)
                if p is not None:
                    mix(p)
                keep_b(k, 0)
                keep_b(k, 1)
                pairs(k, 2)
                keep_b(k, 2)
                window_masks(k)
                if p is not None:
                    add_mix(p)
                    new_moments(p)
                pairs(k, 3)
                window_factors(k)
                keep_b(k, 3)
                window_adj(k)
                if p is not None:
                    shifts(p)

            hc_f = hc[:, :, :].rearrange("p t c -> p (t c)")
            eng.wait_ge(cols_kept, 3)
            eng.wait_ge(norm_made, 3)
            chunks(eng, turn)

            eng.wait_ge(deg_ready, NT)
            eng.wait_ge(deg_w_ready, NC)
            eng.tensor_tensor(off_1[:, :], deg[:, :], deg_w[:, :], ALU.subtract).then_inc(off_made, 1)
            eng.wait_ge(off_made, 1)
            eng.tensor_scalar(off_0[:, :], off_1[:, :], -1.0, float(N - P), ALU.mult, ALU.add) \
               .then_inc(off_made, 1)
            eng.wait_ge(off_made, 2)
            eng.tensor_scalar(mn[:, :], off_0[:, :], 0.0, None, ALU.is_equal).then_inc(off_made, 1)
            eng.wait_ge(off_made, 3)
            eng.wait_ge(score_made, 1)
            eng.tensor_scalar(mn_b[:, :], mn[:, :], -2.0 * OFF, None, ALU.mult).then_inc(off_ready, 1)
            eng.wait_ge(off_exp, 1)
            eng.tensor_tensor(z_one[:, :], off_1[:, :], eo[:, :], ALU.mult).then_inc(off_made, 1)
            eng.wait_ge(off_made, 4)
            eng.tensor_tensor(z_off[:, :], z_one[:, :], off_0[:, :], ALU.add).then_inc(off_made, 1)
            eng.wait_ge(gid_kept, 5)
            eng.tensor_tensor(diff[0:1, 1:NT], gid_row[0:1, P - 1:N - P:P], gid_row[0:1, P:N:P], ALU.is_equal) \
               .then_inc(flag_made, 1)
            eng.wait_ge(flag_made, 1)
            eng.tensor_reduce(diff[0:1, 0:1], diff[0:1, 1:NT], AX, ALU.max).then_inc(flag_made, 1)
            eng.wait_ge(flag_made, 2)
            eng.tensor_copy(general[0:1, 0:1], diff[0:1, 0:1]).then_inc(flag_made, 1)

            def turn(at):
                if at(-1):
                    i, half, q = at(-1)
                    eng.wait_ge(p_ready, i + 1)
                    wait(eng, p_turned, i - 1)
                    apart(eng)
                    eng.tensor_tensor(probm[:, q, :], prob[:, :], mask[:, bass.ds(i * P, P)], ALU.mult) \
                       .then_inc(pm_ready, 1)
                if at(-1):
                    i, half, q = at(-1)
                    eng.wait_ge(fo_ready, i + 1)
                    wait(eng, rz_ready, i)
                    eng.scalar_tensor_tensor(out=zs[:, :], in0=z_off[:, bass.ds(i, 1)], scalar=fo[:, :],
                                             in1=zw[:, q:q + 1], op0=ALU.mult, op1=ALU.add).then_inc(z_sum, 1)
                if at(0):
                    i, half, q = at(0)
                    eng.wait_ge(v_summed, i + 1)
                    wait(eng, pv_summed, i - 1)
                    eng.tensor_tensor(v_sb[:, q, 0:D + 1], V[q][:, 0:D + 1], bv_row[:, :], ALU.add) \
                       .then_inc(v_kept, 1)
                if at(-1):
                    i, half, q = at(-1)
                    eng.wait_ge(z_sum, i + 1)
                    wait(eng, o_ready, i - 1)
                    eng.reciprocal(rz[:, q:q + 1], zs[:, :]).then_inc(rz_ready, 1)
                if at(0):
                    i, half, q = at(0)
                    eng.wait_ge(s_summed, i + 1)
                    eng.wait_ge(v_kept, i + 1)
                    wait(eng, s3_ready, i)
                    apart(eng)
                    eng.scalar_tensor_tensor(out=sc1[:, :], in0=S_S[:, 0:P],
                                             scalar=v_sb[:, q, D:D + 1], in1=mask[:, bass.ds(i * P, P)],
                                             op0=ALU.add, op1=ALU.mult).then_inc(s1_ready, 1)
                if at(0):
                    i, half, q = at(0)
                    eng.wait_ge(s1_ready, i + 1)
                    wait(eng, p_ready, i - 1)
                    apart(eng)
                    eng.tensor_tensor(sc3[:, q, :], sc1[:, :], diag[:, bass.ds(i * P, P)], ALU.add) \
                       .then_inc(s3_ready, 1)
                if at(0):
                    i, half, q = at(0)
                    eng.wait_ge(s3_ready, i + 1)
                    wait(eng, m_ready, i)
                    eng.tensor_reduce(neg_mw[:, :], sc3[:, q, :], AX, ALU.max, negate=True).then_inc(mw_ready, 1)
                if at(0):
                    i, half, q = at(0)
                    eng.wait_ge(mw_ready, i + 1)
                    wait(eng, fo_ready, i - 1)
                    eng.tensor_tensor(neg_m[:, q:q + 1], neg_mw[:, :], mn_b[:, bass.ds(i, 1)], ALU.min) \
                       .then_inc(m_ready, 1)
                if at(-2):
                    i, half, q = at(-2)
                    eng.wait_ge(pv_summed, i + 1)
                    eng.wait_ge(rz_ready, i + 1)
                    wait(eng, o_stored[q], 16 * half)
                    eng.scalar_tensor_tensor(out=o_sb[:, q, :], in0=PV[q][:, 0:D], scalar=rz[:, q:q + 1],
                                             in1=x1_all[:, bass.ds(i * D, D)], op0=ALU.mult, op1=ALU.add) \
                       .then_inc(o_ready, 1)

            eng.wait_ge(adj_f_ready, NC)
            eng.wait_ge(off_made, 5)
            turns(eng, turn, {-1: lambda: gates_and_denominators(NC - 1), 0: lambda: mix(NC - 1),
                              1: lambda: add_mix(NC - 1), 2: lambda: new_moments(NC - 1),
                              3: lambda: shifts(NC - 1)})
            with if_general(eng):
                eng.sem_inc(all_v_kept, 2)
                with eng.Fori(0, NT) as i:
                    eng.wait_ge(all_v_summed, i + 2)
                    apart(eng)
                    eng.tensor_tensor(v_all[:, bass.ds(i * D, D)], V_S[:, 0:D], bv_row[:, 0:D], ALU.add) \
                       .then_inc(all_v_kept, 1)
                    eng.tensor_tensor(c_all[:, bass.ds(i, 1)], V_S[:, D:D + 1], bv_row[:, D:D + 1], ALU.add) \
                       .then_inc(all_v_kept, 1)
                with eng.Fori(0, NT) as i:
                    eng.wait_ge(row_loaded, 16 * (i + 1))
                    apart(eng)
                    eng.tensor_scalar(mask_row[:, :], gid_row[:, :], gid_col[:, bass.ds(i, 1)], None,
                                      ALU.is_equal).then_inc(row_masked, 1)
                    eng.wait_ge(row_masked, 2 * i + 1)
                    apart(eng)
                    eng.tensor_scalar(fac_row, mask_row[:, :], 1.0 - OFF, OFF, ALU.mult, ALU.add) \
                       .then_inc(row_masked, 1)
                    eng.wait_ge(row_s_summed, i + 1)
                    apart(eng)
                    for c in range(N // 512):
                        ins = eng.scalar_tensor_tensor(out=score_row[:, c * 512:(c + 1) * 512],
                                                       in0=bank[c][:, :], scalar=c_all[:, bass.ds(i, 1)],
                                                       in1=mask_row[:, c * 512:(c + 1) * 512],
                                                       op0=ALU.add, op1=ALU.mult)
                    ins.then_inc(row_scored, 1)
                    eng.wait_ge(row_scored, 3 * i + 1)
                    apart(eng)
                    eng.scalar_tensor_tensor(out=score_row, in0=adj_row, scalar=2.0, in1=score_row,
                                             op0=ALU.mult, op1=ALU.add).then_inc(row_scored, 1)
                    eng.wait_ge(row_masked, 2 * i + 2)
                    eng.wait_ge(row_scored, 3 * i + 2)
                    apart(eng)
                    eng.tensor_tensor(score_row, score_row, fac_row, ALU.mult).then_inc(row_scored, 1)
                    eng.wait_ge(row_scored, 3 * i + 3)
                    apart(eng)
                    eng.tensor_reduce(neg_m[:, 0:1], score_row, AX, ALU.max, negate=True) \
                       .then_inc(row_m_ready, 1)
                    eng.wait_ge(row_p_ready, i + 1)
                    apart(eng)
                    eng.reciprocal(rz[:, 0:1], zw[:, 0:1])
                    eng.tensor_tensor(score_row, prob_row, mask_row[:, :], ALU.mult).then_inc(row_pm_ready, 1)
                    eng.wait_ge(row_pv_summed, i + 1)
                    apart(eng)
                    eng.scalar_tensor_tensor(out=o_sb[:, 0, :], in0=bank[4][:, 0:D], scalar=rz[:, 0:1],
                                             in1=x1_all[:, bass.ds(i * D, D)], op0=ALU.mult, op1=ALU.add) \
                       .then_inc(row_o_ready, 1)


_INPUTS = ["x", "adj", "adj_t", "L0_gnn_W_sa", "L0_gnn_a_sa", "L0_gnn_W_gcnb", "L0_gnn_b_gcnb", "gate_w",
           "L0_gnn_ba", "L0_gnn_bb", "L1_gnn_ptr", "L1_gnn_Wq", "L1_gnn_Wk", "WvT", "bq_bk", "L1_gnn_bv"]


def kernel(**inputs):
    import numpy as np
    import concourse.bacc as bacc
    from concourse.bass_utils import run_bass_kernel_spmd

    given = {name: np.ascontiguousarray(a) for name, a in inputs.items()}
    given["adj_t"] = np.ascontiguousarray(given["adj"].T)
    given["WvT"] = np.ascontiguousarray(given["L1_gnn_Wv"].T)
    both = np.stack([given["L0_gnn_Wa"].reshape(2, -1, P), given["L0_gnn_Wb"].reshape(2, -1, P)], axis=1)
    given["gate_w"] = np.ascontiguousarray(both.transpose(3, 2, 0, 1).reshape(P, -1, 4))
    biases = np.stack([given["L1_gnn_bq"].reshape(-1, P), given["L1_gnn_bk"].reshape(-1, P)])
    given["bq_bk"] = np.ascontiguousarray(biases.transpose(2, 1, 0))

    nc = bacc.Bacc("TRN2", target_bir_lowering=False, num_devices=1)
    arrays, args = {}, []
    for name in _INPUTS:
        arrays[f"in_{name}"] = given[name]
        args.append(nc.dram_tensor(f"in_{name}", given[name].shape, mybir.dt.from_np(given[name].dtype),
                                   kind="ExternalInput").ap())
    args.append(nc.dram_tensor("out", given["x"].shape, F32, kind="ExternalOutput").ap())
    two_graph_layers(nc, *args)
    return run_bass_kernel_spmd(nc, [arrays], core_ids=[0]).results[0]["out"]
```

```python
from contextlib import ExitStack

import concourse.bass as bass
from concourse import mybir

P = 128
F32 = mybir.dt.float32
F16 = mybir.dt.float16
BF16 = mybir.dt.bfloat16
I32 = mybir.dt.int32
ALU = mybir.AluOpType
ACT = mybir.ActivationFunctionType
AX = mybir.AxisListType.X

SLOPE = 0.01
LN_EPS = 1e-5
ATTN_EPS = 1e-5
OFF = -1e6
H_SCALE = 2.0 ** 11
E_SCALE = 2.0 ** 15
TINY = 1e-30


def two_graph_layers(nc, x, adj, adj_t, W_sa, a_sa, W_gcnb, b_gcnb, gate_w, gate_b, ptr,
                     Wq, Wk, WvT, bq_bk, bv, out):
    N, D = x.shape
    NP = ptr.shape[0]
    NT = N // P
    KT = D // P
    CT = 4
    NC = NT // CT
    CW = CT * P
    RING = 4
    PAIRS = NT // 2
    E1 = D + 2
    B1 = D + 4
    CHUNK = NT * CW
    PW = 2 * CW
    QK_SCALE = float(D) ** -0.5

    with ExitStack() as ctx:
        def sb(name, shape, dt=F32):
            return ctx.enter_context(nc.sbuf_tensor(name, shape, dt))

        def sem(name):
            return ctx.enter_context(nc.semaphore(name))

        adjt = sb("adjt", [P, 2 * CHUNK])
        hb16 = sb("hb16", [P, NT, 2, B1], F16)
        hd16 = sb("hd16", [P, NT, 2, E1], F16)
        s_row = sb("s_row", [P, N])
        e_raw = sb("e_raw", [P, 2 * PW])
        e_mask = sb("e_mask", [P, 2 * PW])
        e_hi = sb("e_hi", [P, RING * PW], F16)
        e_lo = sb("e_lo", [P, RING * PW], F16)
        x1_all = sb("x1_all", [P, NT * D])
        diag = sb("diag", [P, N])
        mask = sb("mask", [P, N], BF16)
        fac = sb("fac", [P, CW])
        x_in = sb("x_in", [P, CT, D])
        xb = sb("xb", [P, CT, D])
        xa = sb("xa", [P, CT, D])
        gid_row = sb("gid_row", [P, N], BF16)
        ident = sb("ident", [P, P])
        ones = sb("ones", [P, P])
        ones_b = sb("ones_b", [P, P], BF16)

        w_sa = sb("w_sa", [P, KT, D])
        w_b = sb("w_b", [P, KT, D + 6])
        w_v = sb("w_v", [P, KT, D + 1])
        w_qk = sb("w_qk", [P, KT, D])
        w4 = w_b[:, :, D + 2:D + 6]
        a_row = sb("a_row", [P, 2, D])
        bg_row = sb("bg_row", [P, D])
        bv_row = sb("bv_row", [P, D + 1])
        gate_bias = sb("gate_bias", [P, 2])
        bqk_col = sb("bqk_col", [P, KT, 2])
        bq_wide = sb("bq_wide", [P, KT, P])
        u_col = sb("u_col", [P, KT])
        ptr_i = sb("ptr_i", [NP, 1], I32)
        ptr_f = sb("ptr_f", [NP, 1])
        gid_col = sb("gid_col", [P, NT])
        sq = sb("sq", [P, 3])
        norm_sq = sb("norm_sq", [P, 3])
        norm_inv = sb("norm_inv", [P, 3])
        norm = sb("norm", [P, 3])
        norm_h = sb("norm_h", [P, 3])
        hc = sb("hc", [P, NT, 4])
        st6 = sb("st6", [P, NT, 6])
        mv = sb("mv", [P, NT, 2])
        var_e = sb("var_e", [P, NT])
        half_neg = sb("half_neg", [P, NT])
        rstd = sb("rstd", [P, NT])
        ln_b = sb("ln_b", [P, NT])
        nbias = sb("nbias", [P, NT])
        dp = sb("dp", [P, NT])
        dp_s = sb("dp_s", [P, NT])
        es = sb("es", [P, NT])
        rm = sb("rm", [P, 4])
        den = sb("den", [P, CT])
        rden = sb("rden", [P, CT])
        ga = sb("ga", [P, CT])
        gz = sb("gz", [P, CT, 2])
        gt = sb("gt", [P, CT, 2])
        gates = sb("gates", [P, CT, 2])
        st6b = sb("st6b", [P, CT, 6])
        mvb = sb("mvb", [P, CT, 2])
        veb = sb("veb", [P, CT])
        rs_all = sb("rs_all", [P, NT])
        nb_all = sb("nb_all", [P, NT])
        deg = sb("deg", [P, NT])
        deg_w = sb("deg_w", [P, NT])
        off_1 = sb("off_1", [P, NT])
        off_0 = sb("off_0", [P, NT])
        mn = sb("mn", [P, NT])
        mn_b = sb("mn_b", [P, NT])
        eo = sb("eo", [P, NT])
        z_one = sb("z_one", [P, NT])
        z_off = sb("z_off", [P, NT])
        diff = sb("diff", [1, NT])
        off_score = sb("off_score", [P, 1])
        general = sb("general", [1, 1], I32)

        wq = e_mask[:, 0:KT * D].rearrange("p (k d) -> p k d", k=KT)
        wk = e_lo[:, :].bitcast(F32)[:, PW:PW + KT * D].rearrange("p (k d) -> p k d", k=KT)
        iota_n = s_row[0:NP, :]
        junk = e_mask[:, KT * D:KT * D + 3 * KT * D].rearrange("p (w k d) -> p w k d", w=3, k=KT)
        s_diag = e_raw[:, 1280:1280 + CT * P].rearrange("p (t n) -> p t n", t=CT)
        cmp_ptr = e_hi[0:NP, 0:N].bitcast(BF16)
        hT = x1_all[:, :].rearrange("p (k n) -> p k n", k=KT)
        xs = adjt[:, CHUNK:CHUNK + NT * D].rearrange("p (t d) -> p t d", d=D)
        h = adjt[:, CHUNK + NT * D:2 * CHUNK].rearrange("p (t d) -> p t d", d=D)

        h1T_all = adjt[:, 0:NT * D].rearrange("p (k n) -> p k n", k=KT)
        v_all = adjt[:, NT * D:2 * NT * D]
        adj_row = adjt[:, 2 * NT * D:2 * NT * D + N]
        score_row = adjt[:, 2 * NT * D + N:2 * NT * D + 2 * N]
        c_all = adjt[:, 3 * NT * D:3 * NT * D + NT]
        mask_row = s_row
        fac_row = e_hi[:, :].bitcast(F32)
        prob_row = e_lo[:, :].bitcast(F32)
        probT_row = e_raw

        h1, h1T, gT, o_sb = (e_mask[:, 512 * n:512 * n + 512].rearrange("p (q n) -> p q n", q=2)
                             for n in range(4))
        v_sb = sb("v_sb", [P, 2, D + 2])
        sc3, probm, pT = (e_raw[:, 256 * n:256 * n + 256].rearrange("p (q n) -> p q n", q=2)
                          for n in range(3))
        sc1 = e_raw[:, 768:768 + P]
        prob = e_raw[:, 896:896 + P]
        neg_mw = sb("neg_mw", [P, 1])
        neg_m = sb("neg_m", [P, 2])
        zw = sb("zw", [P, 2])
        fo = sb("fo", [P, 1])
        zs = sb("zs", [P, 1])
        rz = sb("rz", [P, 2])

        bank = [ctx.enter_context(nc.psum_tensor(f"bank{b}", [P, 512], F32)) for b in range(8)]
        S_S, P_T, H_T, G_T, V_S = bank[0], bank[3], bank[4], bank[5], bank[6]
        PV = [bank[1], bank[2]]
        V = [bank[6], bank[7]]

        x_loaded = [sem(f"x_loaded{m}") for m in range(CT)]
        layer0_loaded = sem("layer0_loaded")
        layer1_loaded = sem("layer1_loaded")
        rest_loaded = sem("rest_loaded")
        ptr_loaded = sem("ptr_loaded")
        norms_loaded = sem("norms_loaded")
        consts_made = sem("consts_made")
        iota_made = sem("iota_made")
        ptr_made = sem("ptr_made")
        cmp_made = sem("cmp_made")
        gid_summed = sem("gid_summed")
        gid_kept = sem("gid_kept")
        w_made = sem("w_made")
        wide_made = sem("wide_made")
        sq_made = sem("sq_made")
        norm_summed = sem("norm_summed")
        norm_made = sem("norm_made")
        inv_made = sem("inv_made")
        w_scaled = sem("w_scaled")
        qk_summed = sem("qk_summed")
        qk_kept = sem("qk_kept")
        bias_summed = sem("bias_summed")
        gid_col_kept = sem("gid_col_kept")
        stats_made = sem("stats_made")
        moments_made = sem("moments_made")
        var_made = sem("var_made")
        rstd_made = sem("rstd_made")
        lnb_made = sem("lnb_made")
        h_made = sem("h_made")
        h_turned = sem("h_turned")
        hT_kept_a = sem("hT_kept_a")
        hT_kept_v = sem("hT_kept_v")
        hb_summed = sem("hb_summed")
        hb_hi_made = sem("hb_hi_made")
        hb_lo_made = sem("hb_lo_made")
        s_diag_made = sem("s_diag_made")
        cols_kept = sem("cols_kept")
        rows_summed = sem("rows_summed")
        rows_kept = sem("rows_kept")
        rmin_v = sem("rmin_v")
        rmin_t = sem("rmin_t")
        bias_made = sem("bias_made")
        factors_made = sem("factors_made")
        dp_scaled = sem("dp_scaled")
        hd_summed = sem("hd_summed")
        hd_hi_made = sem("hd_hi_made")
        hd_lo_made = sem("hd_lo_made")
        score_made = sem("score_made")
        adjt_loaded = [sem(f"adjt_loaded{m}") for m in range(CT)]
        x_read = sem("x_read")
        diag_loaded = sem("diag_loaded")
        raw_ready = sem("raw_ready")
        mask_ready = sem("mask_ready")
        hi_ready = sem("hi_ready")
        lo_ready = sem("lo_ready")
        slot_free = sem("slot_free")
        b_summed = sem("b_summed")
        b_kept = sem("b_kept")
        t_kept = sem("t_kept")
        z_ready = sem("z_ready")
        tz_ready = sem("tz_ready")
        deg_ready = sem("deg_ready")
        deg_w_ready = sem("deg_w_ready")
        den_ready = sem("den_ready")
        rden_ready = sem("rden_ready")
        gates_ready = sem("gates_ready")
        ga_ready = sem("ga_ready")
        u_ready = sem("u_ready")
        th_ready = sem("th_ready")
        half_ready = sem("half_ready")
        x1_ready = sem("x1_ready")
        stats_ready = sem("stats_ready")
        mvb_ready = sem("mvb_ready")
        ve_ready = sem("ve_ready")
        rs_ready = sem("rs_ready")
        nb_ready = sem("nb_ready")
        off_made = sem("off_made")
        off_ready = sem("off_ready")
        off_exp = sem("off_exp")
        passed = sem("passed")
        h1_ready = sem("h1_ready")
        h1_turned = sem("h1_turned")
        h1T_kept = sem("h1T_kept")
        g_summed = sem("g_summed")
        v_summed = sem("v_summed")
        g_kept = sem("g_kept")
        v_kept = sem("v_kept")
        msk_ready = sem("msk_ready")
        fac_ready = sem("fac_ready")
        s_summed = sem("s_summed")
        s1_ready = sem("s1_ready")
        adj_f_ready = sem("adj_f_ready")
        s3_ready = sem("s3_ready")
        mw_ready = sem("mw_ready")
        m_ready = sem("m_ready")
        p_ready = sem("p_ready")
        fo_ready = sem("fo_ready")
        pm_ready = sem("pm_ready")
        z_sum = sem("z_sum")
        rz_ready = sem("rz_ready")
        p_turned = sem("p_turned")
        pT_kept = sem("pT_kept")
        pv_summed = sem("pv_summed")
        o_ready = sem("o_ready")
        o_stored = [sem(f"o_stored{q}") for q in range(2)]
        flag_made = sem("flag_made")
        all_h1 = sem("all_h1")
        all_h1_turned = sem("all_h1_turned")
        all_h1T_kept = sem("all_h1T_kept")
        all_v_summed = sem("all_v_summed")
        all_v_kept = sem("all_v_kept")
        row_loaded = sem("row_loaded")
        row_g_summed = sem("row_g_summed")
        row_g_kept = sem("row_g_kept")
        row_s_summed = sem("row_s_summed")
        row_masked = sem("row_masked")
        row_scored = sem("row_scored")
        row_m_ready = sem("row_m_ready")
        row_p_ready = sem("row_p_ready")
        row_pm_ready = sem("row_pm_ready")
        row_p_turned = sem("row_p_turned")
        row_pT_kept = sem("row_pT_kept")
        row_pv_summed = sem("row_pv_summed")
        row_o_ready = sem("row_o_ready")
        row_stored = sem("row_stored")

        block = ctx.enter_context(nc.Block())

        def wait(eng, signal, value):
            if not isinstance(value, int) or value > 0:
                eng.wait_ge(signal, value)

        def apart(eng):
            eng.sem_inc(passed, 1)

        def if_general(eng):
            eng.wait_ge(o_ready, NT)
            eng.wait_ge(flag_made, 3)
            return eng.If(eng.value_load(general[0:1, 0:1], min_val=0, max_val=1) > 0)

        LEAD, LAG = 2, 2

        def turns(eng, turn, before=None):
            first = 2 * LAG
            before = before or {}
            last = (NT - LEAD) // 2 * 2

            def written_out(t):
                if t in before:
                    before[t]()
                turn(lambda d: (t + d, (t + d) // 2, (t + d) % 2) if 0 <= t + d < NT else None)

            for t in range(-LEAD, first):
                written_out(t)
            with eng.Fori(first // 2, last // 2) as half:
                for q in range(2):
                    turn(lambda d, q=q: (2 * half + (q + d), half + (q + d) // 2, (q + d) % 2))
            for t in range(last, NT + LAG):
                written_out(t)

        def chunks(eng, turn):
            turn(0, None)
            with eng.Fori(1, NC) as k:
                turn(k, k - 1)

        @block.sync
        def _(eng):
            def load_adjt(k, m):
                base = (k % 2) * CHUNK + CT * m * CW
                eng.dma_start(adjt[:, bass.ds(base, CT * CW)].rearrange("p (t c) -> p t c", c=CW),
                              adj_t[m * CW:(m + 1) * CW, bass.ds(k * CW, CW)]
                              .rearrange("(t p) c -> p t c", p=P)).then_inc(adjt_loaded[m], 16)

            def load_x(k):
                eng.dma_start(x_in[:, :, :], x[bass.ds(k * CW, CW), :].rearrange("(t p) d -> p t d", p=P)) \
                   .then_inc(x_read, 16)

            def rows(v, n):
                return v.rearrange("(a n) -> a n", a=1).broadcast_to([P, n])

            def load_group(g):
                eng.dma_start(xs[:, CT * g:CT * g + CT, :],
                              x[g * CW:(g + 1) * CW, :].rearrange("(t p) d -> p t d", p=P)) \
                   .then_inc(x_loaded[g], 16)

            load_group(0)
            eng.dma_start(w_b[:, :, 0:D], W_gcnb.rearrange("(k p) d -> p k d", p=P)).then_inc(norms_loaded, 16)
            load_group(1)
            eng.dma_start(wq, Wq.rearrange("(k p) d -> p k d", p=P)).then_inc(layer1_loaded, 16)
            eng.dma_start(wk, Wk.rearrange("(k p) d -> p k d", p=P)).then_inc(layer1_loaded, 16)
            load_group(2)
            load_group(3)
            eng.dma_start(gate_bias[:, :], rows(gate_b, 2)).then_inc(rest_loaded, 16)
            eng.dma_start(bg_row[:, :], rows(b_gcnb, D)).then_inc(rest_loaded, 16)
            eng.dma_start(bv_row[:, 0:D], rows(bv, D)).then_inc(rest_loaded, 16)
            eng.dma_start(w_v[:, :, 0:D], WvT.rearrange("(k p) d -> p k d", p=P)).then_inc(rest_loaded, 16)
            for m in range(CT):
                load_adjt(0, m)
            load_x(0)
            eng.wait_ge(h_turned, NT // 2)
            eng.wait_ge(h_made, NT)
            for m in range(CT):
                eng.wait_ge(adjt_loaded[m], 16)
                load_adjt(1, m)
            with eng.Fori(0, NT) as i:
                eng.dma_start(diag[:, bass.ds(i * P, P)],
                              adj[bass.ds(i * P, P), bass.ds(i * P, P)]).then_inc(diag_loaded, 16)

            with eng.Fori(0, NC - 2) as k:
                eng.wait_ge(b_summed, CT * (k + 1))
                for m in range(CT):
                    eng.wait_ge(mask_ready, PAIRS * k + 2 * (m + 1) + 2)
                    eng.wait_ge(adjt_loaded[m], 16 * (k + 2))
                    apart(eng)
                    load_adjt(k + 2, m)
                eng.wait_ge(x1_ready, k + 2)
                apart(eng)
                load_x(k + 1)
            eng.wait_ge(x1_ready, NC)
            load_x(NC - 1)

            def turn(at):
                if at(-2):
                    i, half, q = at(-2)
                    eng.wait_ge(o_ready, i + 1)
                    eng.dma_start(out[bass.ds(i * P, P), :], o_sb[:, q, :]).then_inc(o_stored[q], 16)

            turns(eng, turn)
            for q in range(2):
                eng.wait_ge(o_stored[q], 16 * (NT // 2))
            with if_general(eng):
                with eng.Fori(0, NT) as i:
                    eng.dma_start(adj_row, adj[bass.ds(i * P, P), :]).then_inc(row_loaded, 16)
                    eng.wait_ge(row_o_ready, i + 1)
                    eng.dma_start(out[bass.ds(i * P, P), :], o_sb[:, 0, :]).then_inc(row_stored, 16)
                    eng.wait_ge(row_stored, 16 * (i + 1))
                    apart(eng)

        @block.gpsimd
        def _(eng):
            eng.memset(ident[:, :], 0.0).then_inc(consts_made, 1)
            eng.memset(ones[:, :], 1.0).then_inc(consts_made, 1)
            eng.memset(ones_b[:, :], 1.0).then_inc(consts_made, 1)
            eng.memset(half_neg[:, :], -0.5).then_inc(consts_made, 1)
            eng.wait_ge(consts_made, 4)
            eng.affine_select(out=ident[:, :], in_=ident[:, :], compare_op=ALU.not_equal, fill=1.0, base=0,
                              pattern=[[-1, P]], channel_multiplier=1).then_inc(consts_made, 1)
            eng.iota(iota_n, pattern=[[1, N]], base=0, channel_multiplier=0,
                     allow_small_or_imprecise_dtypes=True).then_inc(iota_made, 1)

            def inv_deviation(g):
                eng.wait_ge(var_made, g + 1)
                eng.tensor_tensor(rstd[:, CT * g:CT * g + CT], var_e[:, CT * g:CT * g + CT],
                                  half_neg[:, CT * g:CT * g + CT], ALU.pow).then_inc(rstd_made, 1)

            inv_deviation(0)
            eng.wait_ge(norm_made, 1)
            eng.tensor_tensor(norm_inv[:, :], norm_sq[:, :], half_neg[:, 0:3], ALU.pow).then_inc(inv_made, 1)
            for g in range(1, CT):
                inv_deviation(g)
                if g == 1:
                    eng.wait_ge(iota_made, 1)
                    eng.wait_ge(ptr_made, 1)
                    eng.tensor_scalar(cmp_ptr, iota_n, ptr_f[:, :], None, ALU.is_ge).then_inc(cmp_made, 1)
            eng.memset(hb16[:, :, 0, D + 2], 1.0).then_inc(consts_made, 1)

            def add_half(k):
                eng.wait_ge(x_read, 16 * (k + 1))
                apart(eng)
                eng.tensor_scalar(x_in[:, :, :], x_in[:, :, :], 0.5, None, ALU.add).then_inc(half_ready, 1)

            def inv_deviations(k):
                eng.wait_ge(mvb_ready, CT * (k + 1))
                apart(eng)
                eng.tensor_scalar(veb[:, :], mvb[:, :, 1], LN_EPS, None, ALU.add).then_inc(ve_ready, 1)
                eng.wait_ge(ve_ready, k + 1)
                eng.tensor_tensor(rs_all[:, bass.ds(CT * k, CT)], veb[:, :], half_neg[:, 0:CT], ALU.pow) \
                   .then_inc(rs_ready, 1)

            with eng.Fori(0, NC) as k:
                add_half(k)
                inv_deviations(k)

        @block.scalar
        def _(eng):
            eng.preload_act_table(ACT.Exp)
            eng.dma_start(w_sa[:, :, :], W_sa.rearrange("(k p) d -> p k d", p=P)).then_inc(norms_loaded, 16)
            eng.dma_start(w_b[:, :, D:D + 2], gate_w[:, :, 0:2]).then_inc(norms_loaded, 16)
            eng.dma_start(ptr_i[:, :], ptr.rearrange("(g a) -> g a", a=1)).then_inc(ptr_loaded, 16)
            eng.dma_start(bqk_col[:, :, :], bq_bk).then_inc(ptr_loaded, 16)
            eng.dma_start(a_row[:, :, :].rearrange("p a d -> p (a d)"), a_sa.broadcast_to([P, 2 * D])) \
               .then_inc(layer0_loaded, 16)
            eng.dma_start(w_b[:, :, D + 4:D + 6], gate_w[:, :, 2:4]).then_inc(layer0_loaded, 16)
            eng.sem_inc(hi_ready, 2)
            eng.sem_inc(t_kept, CT)

            def h_pair(g):
                eng.wait_ge(lnb_made, g // 2 + 1)
                for t in (2 * g, 2 * g + 1):
                    eng.activation(h[:, t, :], xs[:, t, :], ACT.Relu, scale=rstd[:, t:t + 1],
                                   bias=ln_b[:, t:t + 1]).then_inc(h_made, 1)

            def keep_hT(g):
                eng.wait_ge(h_turned, g + 1)
                eng.activation(hT[:, :, 2 * P * g:2 * P * (g + 1)],
                               bank[g % 2][:, :].rearrange("p (k n) -> p k n", k=KT), ACT.Copy) \
                   .then_inc(hT_kept_a, 1)

            def hb_high(t):
                eng.wait_ge(hb_summed, t + 1)
                eng.activation(hb16[:, t, 0, 0:D + 2], bank[2 + t % 4][:, 0:D + 2], ACT.Copy, scale=H_SCALE) \
                   .then_inc(hb_hi_made, 1)

            def keep_s(c):
                eng.wait_ge(rows_summed, CT * (c + 1))
                if c == 0:
                    eng.wait_ge(cmp_made, 1)
                eng.activation(s_row[:, c * CW:(c + 1) * CW], bank[6 + c % 2][:, :], ACT.Copy) \
                   .then_inc(rows_kept, 1)

            eng.wait_ge(norms_loaded, 16 * 3)
            for side, weights in enumerate((w_sa[:, :, :], w_b[:, :, 0:D], w_b[:, :, D:D + 2])):
                n = weights.shape[2]
                eng.activation(junk[:, side, :, 0:n], weights, ACT.Square, accum_out=sq[:, side:side + 1]) \
                   .then_inc(sq_made, 1)
            eng.wait_ge(x_loaded[0], 16)
            eng.wait_ge(x_loaded[1], 16)
            h_pair(0)
            h_pair(1)
            keep_hT(0)
            for g in range(NT // 2):
                if g % 2 == 1 and g + 1 < NT // 2:
                    keep_hT(g + 1)
                if g == 0:
                    for later in range(2, CT):
                        eng.wait_ge(x_loaded[later], 16)
                if g + 2 < NT // 2:
                    h_pair(g + 2)
                hb_high(2 * g)
                hb_high(2 * g + 1)
                if g % 2 == 1 and g > 1:
                    keep_s(g // 2 - 1)
            eng.wait_ge(cols_kept, NT)
            eng.activation(nbias[:, :], hc[:, :, 1], ACT.Copy, scale=SLOPE - 1.0).then_inc(bias_made, 1)
            keep_s(CT - 1)
            eng.wait_ge(rmin_v, 4)
            eng.activation(dp[:, :], hc[:, :, 1], ACT.Exp, scale=-SLOPE, bias=rm[:, 3:4]) \
               .then_inc(factors_made, 1)
            eng.wait_ge(dp_scaled, 1)
            for t in range(NT):
                eng.wait_ge(hd_summed, t + 1)
                eng.activation(hd16[:, t, 0, 0:D], bank[2 + t % 4][:, 0:D], ACT.Copy,
                               scale=dp_s[:, t:t + 1]).then_inc(hd_hi_made, 1)
            eng.activation(hd16[:, :, 0, D], dp_s[:, :], ACT.Copy).then_inc(hd_hi_made, 1)
            eng.activation(es[:, :], hc[:, :, 0], ACT.Exp, scale=SLOPE, bias=rm[:, 3:4]) \
               .then_inc(factors_made, 1)

            eng.wait_ge(rows_kept, 4)
            eng.wait_ge(bias_made, 1)
            eng.wait_ge(w_made, 2 * KT)
            eng.wait_ge(sq_made, 3)
            eng.wait_ge(gid_summed, CT)
            eng.wait_ge(rows_summed, NT)

            def raw(k, m):
                for q in range(2):
                    eng.wait_ge(mask_ready, PAIRS * k + 2 * m + q + 1)
                    apart(eng)
                    for n in range(2):
                        j = CT * m + 2 * q + n
                        ins = eng.activation(e_raw[:, q * PW + n * CW:q * PW + (n + 1) * CW],
                                             s_row[:, bass.ds(k * CW, CW)], ACT.Exp,
                                             scale=SLOPE - 1.0, bias=nbias[:, j:j + 1])
                    ins.then_inc(raw_ready, 1)

            def high(k, m):
                for q in range(2):
                    slot = (2 * m + q) % RING
                    eng.wait_ge(mask_ready, PAIRS * k + 2 * m + q + 3)
                    eng.wait_ge(slot_free, PAIRS * k + 2 * m + q + 1)
                    eng.activation(e_hi[:, slot * PW:(slot + 1) * PW], e_mask[:, q * PW:(q + 1) * PW],
                                   ACT.Copy, scale=E_SCALE).then_inc(hi_ready, 1)

            def keep_a(p):
                eng.wait_ge(ga_ready, p + 1)
                eng.wait_ge(x1_ready, p + 1)
                for r in range(CT):
                    eng.activation(xa[:, r, :], bank[r][:, 0:D], ACT.Copy, scale=ga[:, r:r + 1]) \
                       .then_inc(t_kept, 1)

            def tanh_mix(p):
                eng.wait_ge(u_ready, p + 1)
                eng.activation(xa[:, :, :], xa[:, :, :], ACT.Tanh, scale=0.5).then_inc(th_ready, 1)

            def turn(k, p):
                raw(k, 0)
                high(k, 0)
                raw(k, 1)
                if p is not None:
                    keep_a(p)
                high(k, 1)
                raw(k, 2)
                if p is not None:
                    tanh_mix(p)
                high(k, 2)
                raw(k, 3)
                high(k, 3)
                eng.wait_ge(z_ready, k + 1)
                eng.wait_ge(gates_ready, k + 1)
                eng.activation(gt[:, :, :], gz[:, :, :], ACT.Tanh, scale=0.5).then_inc(tz_ready, 1)

            chunks(eng, turn)

            eng.wait_ge(off_ready, 1)
            eng.activation(eo[:, :], mn_b[:, :], ACT.Exp, bias=off_score[:, 0:1]).then_inc(off_exp, 1)

            def turn(at):
                if at(1):
                    i, half, q = at(1)
                    eng.wait_ge(h1_turned, i + 1)
                    wait(eng, s_summed, i - 1)
                    eng.activation(h1T[:, q, :], H_T[:, 0:D], ACT.Copy).then_inc(h1T_kept, 1)
                if at(-2):
                    i, half, q = at(-2)
                    eng.wait_ge(p_turned, i + 1)
                    wait(eng, pv_summed, i - 1)
                    eng.activation(pT[:, q, :], P_T[:, 0:P], ACT.Copy).then_inc(pT_kept, 1)
                if at(0):
                    i, half, q = at(0)
                    eng.wait_ge(g_summed, i + 1)
                    wait(eng, s_summed, i - 1)
                    for c in range(KT):
                        eng.activation(gT[:, q, c * P:(c + 1) * P], G_T[:, c * P:(c + 1) * P],
                                       ACT.Identity, scale=QK_SCALE, bias=u_col[:, c:c + 1]) \
                           .then_inc(g_kept, 1)
                if at(2):
                    i, half, q = at(2)
                    eng.wait_ge(nb_ready, i // CT + 1)
                    wait(eng, h1_turned, i - 1)
                    apart(eng)
                    eng.activation(h1[:, q, :], x1_all[:, bass.ds(i * D, D)], ACT.Relu,
                                   scale=rs_all[:, bass.ds(i, 1)], bias=nb_all[:, bass.ds(i, 1)]) \
                       .then_inc(h1_ready, 1)
                if at(-1):
                    i, half, q = at(-1)
                    eng.wait_ge(m_ready, i + 1)
                    wait(eng, pm_ready, i)
                    eng.activation(prob[:, :], sc3[:, q, :], ACT.Exp, bias=neg_m[:, q:q + 1],
                                   accum_out=zw[:, q:q + 1]).then_inc(p_ready, 1)
                    wait(eng, z_sum, i)
                    eng.activation(fo[:, :], mn[:, bass.ds(i, 1)], ACT.Exp, scale=2.0 * OFF,
                                   bias=neg_m[:, q:q + 1]).then_inc(fo_ready, 1)

            eng.wait_ge(lo_ready, PAIRS * NC)
            turns(eng, turn, {0: lambda: keep_a(NC - 1), 1: lambda: tanh_mix(NC - 1)})
            with if_general(eng):
                eng.sem_inc(all_v_summed, 1)
                with eng.Fori(0, NT) as i:
                    eng.activation(h1[:, 0, :], x1_all[:, bass.ds(i * D, D)], ACT.Relu,
                                   scale=rs_all[:, bass.ds(i, 1)], bias=nb_all[:, bass.ds(i, 1)]) \
                       .then_inc(all_h1, 1)
                    eng.wait_ge(all_h1_turned, i + 1)
                    eng.wait_ge(all_v_summed, i + 1)
                    apart(eng)
                    eng.activation(h1T[:, 0, :], H_T[:, 0:D], ACT.Copy).then_inc(all_h1T_kept, 1)
                    eng.activation(h1T_all[:, :, bass.ds(i * P, P)],
                                   H_T[:, 0:D].rearrange("p (k n) -> p k n", k=KT), ACT.Copy) \
                       .then_inc(all_h1T_kept, 1)
                with eng.Fori(0, NT) as i:
                    eng.wait_ge(row_g_summed, i + 1)
                    apart(eng)
                    for c in range(KT):
                        eng.activation(gT[:, 0, c * P:(c + 1) * P], G_T[:, c * P:(c + 1) * P], ACT.Identity,
                                       scale=QK_SCALE, bias=u_col[:, c:c + 1]).then_inc(row_g_kept, 1)
                    eng.wait_ge(row_m_ready, i + 1)
                    apart(eng)
                    eng.activation(prob_row, score_row, ACT.Exp, bias=neg_m[:, 0:1], accum_out=zw[:, 0:1]) \
                       .then_inc(row_p_ready, 1)
                    for g in range(NT // CT):
                        eng.wait_ge(row_p_turned, CT * i + g + 1)
                        apart(eng)
                        eng.activation(probT_row[:, g * 512:(g + 1) * 512], bank[4 + g][:, :], ACT.Copy) \
                           .then_inc(row_pT_kept, 1)

        @block.tensor
        def _(eng):
            def turn_h(g):
                eng.wait_ge(h_made, 2 * g + 2)
                if g >= 2:
                    if g % 2 == 0:
                        eng.wait_ge(hT_kept_a, g // 2)
                    else:
                        eng.wait_ge(hT_kept_v, g // 2)
                for c in range(KT):
                    for n in range(2):
                        mm = eng.transpose(bank[g % 2][:, (2 * c + n) * P:(2 * c + n + 1) * P],
                                           h[:, 2 * g + n, c * P:(c + 1) * P], ident[:, :])
                mm.then_inc(h_turned, 1)

            def times_weights(g):
                if g % 2 == 0:
                    eng.wait_ge(hT_kept_a, g // 2 + 1)
                else:
                    eng.wait_ge(hT_kept_v, g // 2 + 1)
                for t in range(2 * g, 2 * g + 2):
                    if t >= 4:
                        eng.wait_ge(hb_lo_made, t - 3)
                    for kk in range(KT):
                        mm = eng.matmul(bank[2 + t % 4][:, 0:D + 6], hT[:, kk, t * P:(t + 1) * P], w_b[:, kk, :],
                                        start=(kk == 0), stop=(kk == KT - 1))
                    mm.then_inc(hb_summed, 1)

            def spread_s(g):
                for t in range(2 * g, 2 * g + 2):
                    eng.wait_ge(s_diag_made, t + 1)
                    if t == 0:
                        eng.wait_ge(qk_kept, 1)
                    if t % CT == 0 and t >= 2 * CT:
                        eng.wait_ge(rows_kept, t // CT - 1)
                    eng.matmul(bank[6 + t // CT % 2][:, (t % CT) * P:(t % CT + 1) * P], ones[:, :],
                               s_diag[:, t % CT, :], start=True, stop=True).then_inc(rows_summed, 1)

            eng.wait_ge(consts_made, 5)
            eng.wait_ge(sq_made, 3)
            eng.matmul(bank[7][:, 0:3], ones[:, :], sq[:, :], start=True, stop=True).then_inc(norm_summed, 1)
            turn_h(0)
            turn_h(1)
            eng.wait_ge(layer1_loaded, 16 * 2)
            for c in range(KT):
                for kk in range(KT):
                    mm = eng.matmul(bank[6][:, c * D:(c + 1) * D], wq[:, kk, c * P:(c + 1) * P],
                                    wk[:, kk, :], start=(kk == 0), stop=(kk == KT - 1))
            mm.then_inc(qk_summed, 1)
            eng.wait_ge(w_scaled, 3)
            eng.wait_ge(w_made, 2 * KT)
            eng.wait_ge(layer0_loaded, 16 * 2)
            for g in range(NT // 2):
                if g == 0:
                    times_weights(0)
                else:
                    if g + 1 < NT // 2:
                        turn_h(g + 1)
                    times_weights(g)
                    spread_s(g - 1)
            def times_w_sa(t):
                eng.wait_ge(hb_lo_made if t < CT else hd_lo_made, NT - 3 + t if t < CT else t - 3)
                for kk in range(KT):
                    mm = eng.matmul(bank[2 + t % 4][:, 0:D], hT[:, kk, t * P:(t + 1) * P], w_sa[:, kk, :],
                                    start=(kk == 0), stop=(kk == KT - 1))
                mm.then_inc(hd_summed, 1)

            def bias_product(n):
                side, c = divmod(n, KT)
                for kk in range(KT):
                    weights = (wk, wq)[side][:, kk, c * P:(c + 1) * P] if side < 2 else bq_wide[:, kk, :]
                    other = min(side, 1)
                    mm = eng.matmul(bank[0][:, n:n + 1], weights, bqk_col[:, kk, other:other + 1],
                                    start=(kk == 0), stop=(kk == KT - 1))
                return mm

            times_w_sa(0)
            eng.wait_ge(rmin_v, 1)
            eng.wait_ge(hT_kept_a, NT // 4)
            eng.transpose(bank[0][0:1, 0:P], rm[:, 0:1], ident[:, :]).then_inc(rmin_t, 1)
            spread_s(NT // 2 - 1)
            times_w_sa(1)
            eng.wait_ge(rmin_v, 2)
            eng.matmul(bank[0][:, 2 * P:2 * P + 1], ones[0:1, :], rm[0:1, 1:2], start=True, stop=True) \
               .then_inc(rmin_t, 1)
            for t in range(2, NT):
                times_w_sa(t)
                if t == 2:
                    eng.wait_ge(rmin_v, 4)
                    eng.wait_ge(wide_made, KT)
                if 3 <= t <= 3 + 2 * KT:
                    mm = bias_product(t - 3)
                if t == 3 + 2 * KT:
                    eng.wait_ge(cmp_made, 1)
                    for n in range(NT):
                        mm = eng.matmul(bank[0][:, P + n:P + n + 1], cmp_ptr[:, n * P:(n + 1) * P],
                                        ones_b[0:NP, 0:1], start=True, stop=True)
                    mm.then_inc(bias_summed, 1)
            eng.wait_ge(hT_kept_v, NT // 4)
            eng.wait_ge(rows_kept, CT)
            for c in range(N // CW):
                if c == 3:
                    eng.wait_ge(hd_lo_made, NT - 3)
                eng.matmul(bank[(1, 6, 7, 2)[c]][:, :], ones_b[0:NP, :], cmp_ptr[:, c * CW:(c + 1) * CW],
                           start=True, stop=True) \
                   .then_inc(gid_summed, 1)

            adjt_b = adjt[:, :].bitcast(BF16)

            def adj_group(place, r):
                for j in range(NT):
                    word = place * CHUNK + j * CW + r * P
                    for part in range(2):
                        cols = D + 3 - part
                        mm = eng.matmul(bank[4 + r][:, 0:cols], adjt_b[:, bass.ds(2 * word + 1, P, 2)],
                                        hb16[:, j, part, 0:cols], start=(j == 0 and part == 0),
                                        stop=(j == NT - 1 and part == 1), skip_group_check=True)
                mm.then_inc(b_summed, 1)

            def e_group(k, m):
                for q in range(2):
                    base = ((2 * m + q) % RING) * PW
                    eng.wait_ge(lo_ready, PAIRS * k + 2 * m + q + 1)
                    for n in range(2):
                        j = CT * m + 2 * q + n
                        for r in range(CT):
                            at = base + n * CW + r * P
                            high, low = e_hi[:, at:at + P], e_lo[:, at:at + P]
                            eng.matmul(bank[r][:, 0:D + 1], high, hd16[:, j, 0, 0:D + 1],
                                       start=(j == 0), stop=False, skip_group_check=True)
                            eng.matmul(bank[r][:, 0:D + 1], high, hd16[:, j, 1, 0:D + 1],
                                       start=False, stop=False, skip_group_check=True)
                            mm = eng.matmul(bank[r][:, 0:D + 1], low, hd16[:, j, 0, 0:D + 1],
                                            start=False, stop=(j == NT - 1), skip_group_check=True)
                    mm.then_inc(slot_free, 1)

            eng.wait_ge(hb_lo_made, NT)
            eng.wait_ge(consts_made, 6)
            eng.wait_ge(hd_lo_made, NT - 1)
            with eng.Fori(0, NC // 2) as pair:
                for place in range(2):
                    k = 2 * pair + place
                    for m in range(CT):
                        eng.wait_ge(adjt_loaded[m], 16 * (k + 1))
                    eng.wait_ge(b_kept, CT * k + 1)
                    adj_group(place, 0)
                    eng.wait_ge(b_kept, CT * k + 2)
                    if place == 0:
                        eng.wait_ge(hd_lo_made, NT)
                    adj_group(place, 1)
                    if place == 0:
                        eng.wait_ge(hd_lo_made, NT + 1)
                        eng.wait_ge(gid_kept, CT)
                        eng.wait_ge(qk_kept, 3 + KT)
                    eng.wait_ge(t_kept, CT * (k + 1))
                    e_group(k, 0)
                    eng.wait_ge(b_kept, CT * k + 3)
                    adj_group(place, 2)
                    e_group(k, 1)
                    eng.wait_ge(b_kept, CT * k + 4)
                    adj_group(place, 3)
                    e_group(k, 2)
                    e_group(k, 3)

            def turn(at):
                if at(1):
                    i, half, q = at(1)
                    eng.wait_ge(h1_ready, i + 1)
                    wait(eng, h1T_kept, i)
                    for c in range(KT):
                        mm = eng.transpose(H_T[:, c * P:(c + 1) * P], h1[:, q, c * P:(c + 1) * P], ident[:, :])
                    mm.then_inc(h1_turned, 1)
                if at(0):
                    i, half, q = at(0)
                    eng.wait_ge(h1T_kept, i + 1)
                    wait(eng, g_kept, KT * i)
                    for c in range(KT):
                        for kk in range(KT):
                            mm = eng.matmul(G_T[:, c * P:(c + 1) * P], w_qk[:, kk, c * P:(c + 1) * P],
                                            h1T[:, q, kk * P:(kk + 1) * P],
                                            start=(kk == 0), stop=(kk == KT - 1))
                    mm.then_inc(g_summed, 1)
                if at(-2):
                    i, half, q = at(-2)
                    eng.wait_ge(pm_ready, i + 1)
                    wait(eng, pT_kept, i)
                    eng.transpose(P_T[:, 0:P], probm[:, q, :], ident[:, :]).then_inc(p_turned, 1)
                if at(0):
                    i, half, q = at(0)
                    wait(eng, v_kept, i - 1)
                    for kk in range(KT):
                        mm = eng.matmul(V[q][:, 0:D + 1], h1T[:, q, kk * P:(kk + 1) * P], w_v[:, kk, :],
                                        start=(kk == 0), stop=(kk == KT - 1))
                    mm.then_inc(v_summed, 1)
                if at(-2):
                    i, half, q = at(-2)
                    eng.wait_ge(pT_kept, i + 1)
                    eng.wait_ge(v_kept, i + 1)
                    wait(eng, o_ready, i - 1)
                    eng.matmul(PV[q][:, 0:D], pT[:, q, :], v_sb[:, q, 0:D], start=True, stop=True) \
                       .then_inc(pv_summed, 1)
                if at(0):
                    i, half, q = at(0)
                    eng.wait_ge(g_kept, KT * (i + 1))
                    wait(eng, s1_ready, i)
                    eng.wait_ge(t_kept, CT * (NC + 1))
                    for kk in range(KT):
                        mm = eng.matmul(S_S[:, 0:P], gT[:, q, kk * P:(kk + 1) * P],
                                        h1T[:, q, kk * P:(kk + 1) * P], start=(kk == 0), stop=(kk == KT - 1))
                    mm.then_inc(s_summed, 1)

            eng.wait_ge(b_kept, CT * (NC + 1))
            eng.wait_ge(qk_kept, 3 + KT)
            turns(eng, turn)
            with if_general(eng):
                with eng.Fori(0, NT) as i:
                    eng.wait_ge(all_h1, i + 1)
                    apart(eng)
                    for c in range(KT):
                        mm = eng.transpose(H_T[:, c * P:(c + 1) * P], h1[:, 0, c * P:(c + 1) * P], ident[:, :])
                    mm.then_inc(all_h1_turned, 1)
                    eng.wait_ge(all_h1T_kept, 2 * i + 2)
                    eng.wait_ge(all_v_kept, 2 * i + 2)
                    apart(eng)
                    for kk in range(KT):
                        mm = eng.matmul(V_S[:, 0:D + 1], h1T[:, 0, kk * P:(kk + 1) * P], w_v[:, kk, :],
                                        start=(kk == 0), stop=(kk == KT - 1))
                    mm.then_inc(all_v_summed, 1)
                eng.wait_ge(all_v_kept, 2 * NT + 2)
                with eng.Fori(0, NT) as i:
                    for c in range(KT):
                        for kk in range(KT):
                            mm = eng.matmul(G_T[:, c * P:(c + 1) * P], w_qk[:, kk, c * P:(c + 1) * P],
                                            h1T_all[:, kk, bass.ds(i * P, P)],
                                            start=(kk == 0), stop=(kk == KT - 1))
                    mm.then_inc(row_g_summed, 1)
                    eng.wait_ge(row_g_kept, KT * (i + 1))
                    apart(eng)
                    for c in range(N // 512):
                        for kk in range(KT):
                            mm = eng.matmul(bank[c][:, :], gT[:, 0, kk * P:(kk + 1) * P],
                                            h1T_all[:, kk, c * 512:(c + 1) * 512],
                                            start=(kk == 0), stop=(kk == KT - 1))
                    mm.then_inc(row_s_summed, 1)
                    eng.wait_ge(row_pm_ready, i + 1)
                    apart(eng)
                    for g in range(NT // CT):
                        for n in range(CT):
                            mm = eng.transpose(bank[4 + g][:, n * P:(n + 1) * P],
                                               score_row[:, (CT * g + n) * P:(CT * g + n + 1) * P], ident[:, :])
                        mm.then_inc(row_p_turned, 1)
                    eng.wait_ge(row_pT_kept, CT * (i + 1))
                    apart(eng)
                    for j in range(NT):
                        mm = eng.matmul(bank[4][:, 0:D], probT_row[:, j * P:(j + 1) * P],
                                        v_all[:, j * D:(j + 1) * D], start=(j == 0), stop=(j == NT - 1))
                    mm.then_inc(row_pv_summed, 1)
                    eng.wait_ge(row_o_ready, i + 1)
                    apart(eng)

        @block.vector
        def _(eng):
            eng.sem_inc(mask_ready, 2)
            eng.sem_inc(slot_free, RING)
            eng.sem_inc(b_kept, CT)
            eng.sem_inc(x1_ready, 1)
            eng.sem_inc(gates_ready, 1)
            eng.memset(off_score[:, :], 2.0 * OFF).then_inc(score_made, 1)

            def moments(g):
                eng.wait_ge(x_loaded[g], 16)
                for t in range(CT * g, CT * g + CT):
                    eng.bn_stats(st6[:, t, :], xs[:, t, :]).then_inc(stats_made, 1)
                for t in range(CT * g, CT * g + CT):
                    eng.wait_ge(stats_made, t + 1)
                    eng.bn_aggr(mv[:, t, :], st6[:, t, :]).then_inc(moments_made, 1)
                eng.wait_ge(moments_made, CT * g + CT)
                eng.tensor_scalar(var_e[:, CT * g:CT * g + CT], mv[:, CT * g:CT * g + CT, 1], LN_EPS, None,
                                  ALU.add).then_inc(var_made, 1)

            def shift(g):
                eng.wait_ge(rstd_made, g + 1)
                eng.scalar_tensor_tensor(out=ln_b[:, CT * g:CT * g + CT], in0=mv[:, CT * g:CT * g + CT, 0],
                                         scalar=-1.0, in1=rstd[:, CT * g:CT * g + CT],
                                         op0=ALU.mult, op1=ALU.mult).then_inc(lnb_made, 1)

            def keep_hT(g):
                eng.wait_ge(h_turned, g + 1)
                eng.tensor_copy(hT[:, :, 2 * P * g:2 * P * (g + 1)],
                                bank[g % 2][:, :].rearrange("p (k n) -> p k n", k=KT)).then_inc(hT_kept_v, 1)

            def keep_tile(t):
                eng.wait_ge(hb_summed, t + 1)
                eng.wait_ge(hb_hi_made, t + 1)
                eng.tensor_copy(hc[:, t, :], bank[2 + t % 4][:, D + 2:D + 6]).then_inc(cols_kept, 1)
                eng.scalar_tensor_tensor(out=hb16[:, t, 1, 0:D + 2], in0=bank[2 + t % 4][:, 0:D + 2],
                                         scalar=H_SCALE, in1=hb16[:, t, 0, 0:D + 2],
                                         op0=ALU.mult, op1=ALU.subtract).then_inc(hb_lo_made, 1)
                eng.wait_ge(cols_kept, t + 1)
                if t >= CT:
                    eng.wait_ge(rows_summed, t - CT + 1)
                eng.tensor_scalar(s_diag[:, t % CT, :], ident[:, :], hc[:, t, 0:1], None, ALU.mult) \
                   .then_inc(s_diag_made, 1)

            moments(0)
            shift(0)
            eng.wait_ge(ptr_loaded, 16 * 2)
            eng.wait_ge(consts_made, 2)
            eng.tensor_copy(ptr_f[:, :], ptr_i[:, :]).then_inc(ptr_made, 1)
            for kk in range(KT):
                eng.tensor_scalar(bq_wide[:, kk, :], ones[:, :], bqk_col[:, kk, 0:1], None, ALU.mult) \
                   .then_inc(wide_made, 1)
            eng.wait_ge(norm_summed, 1)
            eng.tensor_scalar(norm_sq[:, :], bank[7][:, 0:3], TINY, None, ALU.add).then_inc(norm_made, 1)
            moments(1)
            eng.wait_ge(layer0_loaded, 16 * 2)
            for kk in range(KT):
                for side in range(2):
                    eng.tensor_tensor_reduce(prob_row[:, (2 * kk + side) * D:(2 * kk + side + 1) * D],
                                             w_sa[:, kk, :], a_row[:, side, :], 1.0, 0.0,
                                             ALU.mult, ALU.add, w4[:, kk, side:side + 1]).then_inc(w_made, 1)
            shift(1)
            eng.wait_ge(inv_made, 1)
            eng.wait_ge(w_made, 2 * KT)
            eng.wait_ge(sq_made, 3)
            for side, weights in ((1, w_b[:, :, 0:D]), (2, w_b[:, :, D:D + 2]), (0, w_sa[:, :, :])):
                eng.tensor_scalar(weights, weights, norm_inv[:, side:side + 1], None, ALU.mult) \
                   .then_inc(w_scaled, 1)
            keep_hT(1)
            eng.wait_ge(qk_summed, 1)
            eng.tensor_copy(w_qk[:, :, :].rearrange("p k d -> p (k d)"), bank[6][:, :]).then_inc(qk_kept, 1)
            for g in range(NT // 2):
                if g % 2 == 0 and g > 0:
                    keep_hT(g + 1)
                keep_tile(2 * g)
                if g == 1:
                    shift(2)
                keep_tile(2 * g + 1)
                if g == 2:
                    moments(3)
                if g == 3:
                    shift(3)
                if g == 0:
                    moments(2)
                    eng.wait_ge(norm_made, 1)
                    eng.tensor_tensor(norm[:, :], norm_sq[:, :], norm_inv[:, :], ALU.mult).then_inc(norm_made, 1)
                    eng.wait_ge(norm_made, 2)
                    eng.tensor_scalar(norm_h[:, :], norm[:, :], 1.0 / H_SCALE, None, ALU.mult).then_inc(norm_made, 1)
            eng.wait_ge(cols_kept, NT)
            eng.tensor_reduce(rm[:, 0:1], hc[:, :, 1], AX, ALU.min).then_inc(rmin_v, 1)
            eng.wait_ge(rest_loaded, 16 * 4)
            for c in range(2):
                eng.tensor_scalar(hc[:, :, 2 + c], hc[:, :, 2 + c], gate_bias[:, c:c + 1], None, ALU.add) \
                   .then_inc(cols_kept, 1)
            eng.wait_ge(rmin_t, 1)
            eng.tensor_reduce(rm[0:1, 1:2], bank[0][0:1, 0:P], AX, ALU.min).then_inc(rmin_v, 1)
            eng.wait_ge(rmin_t, 2)
            eng.tensor_copy(rm[:, 2:3], bank[0][:, 2 * P:2 * P + 1]).then_inc(rmin_v, 1)
            eng.wait_ge(rmin_v, 3)
            eng.tensor_scalar(rm[:, 3:4], rm[:, 2:3], SLOPE, None, ALU.mult).then_inc(rmin_v, 1)
            eng.wait_ge(factors_made, 1)
            eng.tensor_scalar(dp_s[:, :], dp[:, :], H_SCALE, None, ALU.mult).then_inc(dp_scaled, 1)
            for t in range(NT):
                eng.wait_ge(hd_hi_made, t + 1)
                if t == 0:
                    eng.wait_ge(dp_scaled, 1)
                eng.scalar_tensor_tensor(out=hd16[:, t, 1, 0:D], in0=bank[2 + t % 4][:, 0:D],
                                         scalar=dp_s[:, t:t + 1], in1=hd16[:, t, 0, 0:D],
                                         op0=ALU.mult, op1=ALU.subtract).then_inc(hd_lo_made, 1)
            eng.wait_ge(hd_hi_made, NT + 1)
            eng.tensor_tensor(hd16[:, :, 1, D], dp_s[:, :], hd16[:, :, 0, D], ALU.subtract) \
               .then_inc(hd_lo_made, 1)
            eng.wait_ge(bias_summed, 1)
            eng.tensor_copy(gid_col[:, :], bank[0][:, P:P + NT]).then_inc(gid_col_kept, 1)
            eng.tensor_scalar(u_col[:, :], bank[0][:, 0:KT], QK_SCALE, None, ALU.mult).then_inc(qk_kept, 1)
            for kk in range(KT):
                eng.tensor_scalar(w_v[:, kk, D:D + 1], bank[0][:, KT + kk:KT + kk + 1], QK_SCALE, None, ALU.mult) \
                   .then_inc(qk_kept, 1)
            eng.tensor_scalar(bv_row[:, D:D + 1], bank[0][:, 2 * KT:2 * KT + 1], QK_SCALE, None, ALU.mult) \
               .then_inc(qk_kept, 1)
            for c in range(N // CW):
                eng.wait_ge(gid_summed, c + 1)
                eng.tensor_copy(gid_row[:, c * CW:(c + 1) * CW], bank[(1, 6, 7, 2)[c]][:, :]).then_inc(gid_kept, 1)

            def pairs(k, m):
                eng.wait_ge(adjt_loaded[m], 16 * (k + 1))
                for q in range(2):
                    eng.wait_ge(raw_ready, PAIRS * k + 2 * m + q + 1)
                    eng.wait_ge(hi_ready, PAIRS * k + 2 * m + q + 1)
                    wait(eng, lo_ready, PAIRS * k + 2 * m + q - 1)
                    apart(eng)
                    eng.scalar_tensor_tensor(out=e_mask[:, q * PW:(q + 1) * PW],
                                             in0=e_raw[:, q * PW:(q + 1) * PW], scalar=1.0,
                                             in1=adjt[:, bass.ds((k % 2) * CHUNK + (CT * m + 2 * q) * CW, PW)],
                                             op0=ALU.min, op1=ALU.mult).then_inc(mask_ready, 1)
                for q in range(2):
                    slot = (2 * m + q) % RING
                    eng.wait_ge(hi_ready, PAIRS * k + 2 * m + q + 3)
                    eng.scalar_tensor_tensor(out=e_lo[:, slot * PW:(slot + 1) * PW],
                                             in0=e_mask[:, q * PW:(q + 1) * PW], scalar=E_SCALE,
                                             in1=e_hi[:, slot * PW:(slot + 1) * PW],
                                             op0=ALU.mult, op1=ALU.subtract).then_inc(lo_ready, 1)

            def keep_b(k, r):
                eng.wait_ge(b_summed, CT * k + r + 1)
                if r == 0:
                    wait(eng, u_ready, k)
                apart(eng)
                ins = eng.scalar_tensor_tensor(out=gz[:, r, :], in0=bank[4 + r][:, D:D + 2],
                                               scalar=norm_h[:, 2:3], in1=hc_f[:, bass.ds(4 * (CT * k + r) + 2, 2)],
                                               op0=ALU.mult, op1=ALU.add)
                if r == CT - 1:
                    ins.then_inc(z_ready, 1)
                eng.tensor_copy(deg[:, bass.ds(CT * k + r, 1)], bank[4 + r][:, D + 2:D + 3]).then_inc(deg_ready, 1)
                eng.scalar_tensor_tensor(out=xb[:, r, :], in0=bank[4 + r][:, 0:D], scalar=norm_h[:, 1:2],
                                         in1=bg_row[:, :], op0=ALU.mult, op1=ALU.add).then_inc(b_kept, 1)

            def gates_and_denominators(p):
                eng.wait_ge(tz_ready, p + 1)
                eng.tensor_scalar(gates[:, :, :], gt[:, :, :], 0.5, 0.5, ALU.mult, ALU.add) \
                   .then_inc(gates_ready, 1)
                eng.wait_ge(slot_free, RING + PAIRS * (p + 1))
                apart(eng)
                for r in range(CT):
                    ins = eng.scalar_tensor_tensor(out=den[:, r:r + 1], in0=es[:, bass.ds(CT * p + r, 1)],
                                                   scalar=ATTN_EPS * H_SCALE * E_SCALE,
                                                   in1=bank[r][:, D:D + 1], op0=ALU.mult, op1=ALU.add)
                ins.then_inc(den_ready, 1)
                eng.wait_ge(den_ready, p + 1)
                eng.reciprocal(rden[:, :], den[:, :]).then_inc(rden_ready, 1)
                eng.wait_ge(rden_ready, p + 1)
                eng.wait_ge(gates_ready, p + 2)
                eng.scalar_tensor_tensor(out=ga[:, :], in0=rden[:, :], scalar=norm[:, 0:1],
                                         in1=gates[:, :, 0], op0=ALU.mult, op1=ALU.mult).then_inc(ga_ready, 1)

            def mix(p):
                for r in range(CT):
                    eng.wait_ge(t_kept, CT * (p + 1) + r + 1)
                    eng.wait_ge(b_kept, CT * (p + 1) + r + 1)
                    ins = eng.scalar_tensor_tensor(out=xa[:, r, :], in0=xb[:, r, :], scalar=gates[:, r, 1:2],
                                                   in1=xa[:, r, :], op0=ALU.mult, op1=ALU.add)
                ins.then_inc(u_ready, 1)

            def add_mix(p):
                eng.wait_ge(th_ready, p + 1)
                eng.wait_ge(half_ready, p + 1)
                apart(eng)
                eng.scalar_tensor_tensor(out=x1_all[:, bass.ds(CT * D * p, CT * D)],
                                         in0=xa[:, :, :].rearrange("p t d -> p (t d)"), scalar=0.5,
                                         in1=x_in[:, :, :].rearrange("p t d -> p (t d)"),
                                         op0=ALU.mult, op1=ALU.add).then_inc(x1_ready, 1)

            def new_moments(p):
                eng.wait_ge(x1_ready, p + 2)
                apart(eng)
                for r in range(CT):
                    eng.bn_stats(st6b[:, r, :], x1_all[:, bass.ds(CT * D * p + r * D, D)]) \
                       .then_inc(stats_ready, 1)
                for r in range(CT):
                    eng.wait_ge(stats_ready, CT * p + r + 1)
                    apart(eng)
                    eng.bn_aggr(mvb[:, r, :], st6b[:, r, :]).then_inc(mvb_ready, 1)

            def shifts(p):
                eng.wait_ge(rs_ready, p + 1)
                apart(eng)
                eng.scalar_tensor_tensor(out=nb_all[:, bass.ds(CT * p, CT)], in0=mvb[:, :, 0], scalar=-1.0,
                                         in1=rs_all[:, bass.ds(CT * p, CT)],
                                         op0=ALU.mult, op1=ALU.mult).then_inc(nb_ready, 1)

            def window_masks(k):
                eng.wait_ge(diag_loaded, 16 * NT)
                for n in range(CT):
                    t = CT * k + n
                    ins = eng.tensor_scalar(mask[:, bass.ds(t * P, P)], gid_row[:, bass.ds(t * P, P)],
                                            gid_col[:, bass.ds(t, 1)], None, ALU.is_equal)
                ins.then_inc(msk_ready, 1)
                eng.tensor_reduce(deg_w[:, bass.ds(CT * k, CT)],
                                  diag[:, bass.ds(k * CW, CW)].rearrange("p (t n) -> p t n", n=P), AX, ALU.add) \
                   .then_inc(deg_w_ready, 1)

            def window_factors(k):
                eng.wait_ge(msk_ready, k + 1)
                wait(eng, adj_f_ready, k)
                apart(eng)
                eng.tensor_scalar(fac[:, :], mask[:, bass.ds(k * CW, CW)], 1.0 - OFF, OFF, ALU.mult, ALU.add) \
                   .then_inc(fac_ready, 1)

            def window_adj(k):
                eng.wait_ge(fac_ready, k + 1)
                eng.wait_ge(deg_w_ready, k + 1)
                apart(eng)
                eng.scalar_tensor_tensor(out=diag[:, bass.ds(k * CW, CW)], in0=diag[:, bass.ds(k * CW, CW)],
                                         scalar=2.0, in1=fac[:, :], op0=ALU.mult, op1=ALU.mult) \
                   .then_inc(adj_f_ready, 1)

            def turn(k, p):
                pairs(k, 0)
                if p is not None:
                    gates_and_denominators(p)
                pairs(k, 1)
                if p is not None:
                    mix(p)
                keep_b(k, 0)
                keep_b(k, 1)
                pairs(k, 2)
                keep_b(k, 2)
                window_masks(k)
                if p is not None:
                    add_mix(p)
                    new_moments(p)
                pairs(k, 3)
                window_factors(k)
                keep_b(k, 3)
                window_adj(k)
                if p is not None:
                    shifts(p)

            hc_f = hc[:, :, :].rearrange("p t c -> p (t c)")
            eng.wait_ge(cols_kept, NT + 2)
            eng.wait_ge(factors_made, 2)
            eng.wait_ge(norm_made, 3)
            eng.wait_ge(gid_col_kept, 1)
            chunks(eng, turn)

            eng.wait_ge(deg_ready, NT)
            eng.wait_ge(deg_w_ready, NC)
            eng.tensor_tensor(off_1[:, :], deg[:, :], deg_w[:, :], ALU.subtract).then_inc(off_made, 1)
            eng.wait_ge(off_made, 1)
            eng.tensor_scalar(off_0[:, :], off_1[:, :], -1.0, float(N - P), ALU.mult, ALU.add) \
               .then_inc(off_made, 1)
            eng.wait_ge(off_made, 2)
            eng.tensor_scalar(mn[:, :], off_0[:, :], 0.0, None, ALU.is_equal).then_inc(off_made, 1)
            eng.wait_ge(off_made, 3)
            eng.wait_ge(score_made, 1)
            eng.tensor_scalar(mn_b[:, :], mn[:, :], -2.0 * OFF, None, ALU.mult).then_inc(off_ready, 1)
            eng.wait_ge(off_exp, 1)
            eng.tensor_tensor(z_one[:, :], off_1[:, :], eo[:, :], ALU.mult).then_inc(off_made, 1)
            eng.wait_ge(off_made, 4)
            eng.tensor_tensor(z_off[:, :], z_one[:, :], off_0[:, :], ALU.add).then_inc(off_made, 1)
            eng.wait_ge(gid_kept, CT)
            eng.tensor_tensor(diff[0:1, 1:NT], gid_row[0:1, P - 1:N - P:P], gid_row[0:1, P:N:P], ALU.is_equal) \
               .then_inc(flag_made, 1)
            eng.wait_ge(flag_made, 1)
            eng.tensor_reduce(diff[0:1, 0:1], diff[0:1, 1:NT], AX, ALU.max).then_inc(flag_made, 1)
            eng.wait_ge(flag_made, 2)
            eng.tensor_copy(general[0:1, 0:1], diff[0:1, 0:1]).then_inc(flag_made, 1)

            def turn(at):
                if at(0):
                    i, half, q = at(0)
                    eng.wait_ge(v_summed, i + 1)
                    wait(eng, pv_summed, i - 1)
                    eng.tensor_tensor(v_sb[:, q, 0:D + 1], V[q][:, 0:D + 1], bv_row[:, :], ALU.add) \
                       .then_inc(v_kept, 1)
                if at(-1):
                    i, half, q = at(-1)
                    eng.wait_ge(p_ready, i + 1)
                    wait(eng, p_turned, i - 1)
                    apart(eng)
                    eng.tensor_tensor(probm[:, q, :], prob[:, :], mask[:, bass.ds(i * P, P)], ALU.mult) \
                       .then_inc(pm_ready, 1)
                if at(0):
                    i, half, q = at(0)
                    eng.wait_ge(s_summed, i + 1)
                    eng.wait_ge(v_kept, i + 1)
                    wait(eng, s3_ready, i)
                    apart(eng)
                    eng.scalar_tensor_tensor(out=sc1[:, :], in0=S_S[:, 0:P],
                                             scalar=v_sb[:, q, D:D + 1], in1=mask[:, bass.ds(i * P, P)],
                                             op0=ALU.add, op1=ALU.mult).then_inc(s1_ready, 1)
                if at(-1):
                    i, half, q = at(-1)
                    eng.wait_ge(fo_ready, i + 1)
                    wait(eng, rz_ready, i)
                    eng.scalar_tensor_tensor(out=zs[:, :], in0=z_off[:, bass.ds(i, 1)], scalar=fo[:, :],
                                             in1=zw[:, q:q + 1], op0=ALU.mult, op1=ALU.add).then_inc(z_sum, 1)
                if at(0):
                    i, half, q = at(0)
                    eng.wait_ge(s1_ready, i + 1)
                    wait(eng, p_ready, i - 1)
                    apart(eng)
                    eng.tensor_tensor(sc3[:, q, :], sc1[:, :], diag[:, bass.ds(i * P, P)], ALU.add) \
                       .then_inc(s3_ready, 1)
                if at(-1):
                    i, half, q = at(-1)
                    eng.wait_ge(z_sum, i + 1)
                    wait(eng, o_ready, i - 1)
                    eng.reciprocal(rz[:, q:q + 1], zs[:, :]).then_inc(rz_ready, 1)
                if at(0):
                    i, half, q = at(0)
                    eng.wait_ge(s3_ready, i + 1)
                    wait(eng, m_ready, i)
                    eng.tensor_reduce(neg_mw[:, :], sc3[:, q, :], AX, ALU.max, negate=True).then_inc(mw_ready, 1)
                if at(0):
                    i, half, q = at(0)
                    eng.wait_ge(mw_ready, i + 1)
                    wait(eng, fo_ready, i - 1)
                    eng.tensor_tensor(neg_m[:, q:q + 1], neg_mw[:, :], mn_b[:, bass.ds(i, 1)], ALU.min) \
                       .then_inc(m_ready, 1)
                if at(-2):
                    i, half, q = at(-2)
                    eng.wait_ge(pv_summed, i + 1)
                    eng.wait_ge(rz_ready, i + 1)
                    wait(eng, o_stored[q], 16 * half)
                    eng.scalar_tensor_tensor(out=o_sb[:, q, :], in0=PV[q][:, 0:D], scalar=rz[:, q:q + 1],
                                             in1=x1_all[:, bass.ds(i * D, D)], op0=ALU.mult, op1=ALU.add) \
                       .then_inc(o_ready, 1)

            eng.wait_ge(adj_f_ready, NC)
            eng.wait_ge(off_made, 5)
            turns(eng, turn, {-1: lambda: gates_and_denominators(NC - 1), 0: lambda: mix(NC - 1),
                              1: lambda: add_mix(NC - 1), 2: lambda: new_moments(NC - 1),
                              3: lambda: shifts(NC - 1)})
            with if_general(eng):
                eng.sem_inc(all_v_kept, 2)
                with eng.Fori(0, NT) as i:
                    eng.wait_ge(all_v_summed, i + 2)
                    apart(eng)
                    eng.tensor_tensor(v_all[:, bass.ds(i * D, D)], V_S[:, 0:D], bv_row[:, 0:D], ALU.add) \
                       .then_inc(all_v_kept, 1)
                    eng.tensor_tensor(c_all[:, bass.ds(i, 1)], V_S[:, D:D + 1], bv_row[:, D:D + 1], ALU.add) \
                       .then_inc(all_v_kept, 1)
                with eng.Fori(0, NT) as i:
                    eng.wait_ge(row_loaded, 16 * (i + 1))
                    apart(eng)
                    eng.tensor_scalar(mask_row[:, :], gid_row[:, :], gid_col[:, bass.ds(i, 1)], None,
                                      ALU.is_equal).then_inc(row_masked, 1)
                    eng.wait_ge(row_masked, 2 * i + 1)
                    apart(eng)
                    eng.tensor_scalar(fac_row, mask_row[:, :], 1.0 - OFF, OFF, ALU.mult, ALU.add) \
                       .then_inc(row_masked, 1)
                    eng.wait_ge(row_s_summed, i + 1)
                    apart(eng)
                    for c in range(N // 512):
                        ins = eng.scalar_tensor_tensor(out=score_row[:, c * 512:(c + 1) * 512],
                                                       in0=bank[c][:, :], scalar=c_all[:, bass.ds(i, 1)],
                                                       in1=mask_row[:, c * 512:(c + 1) * 512],
                                                       op0=ALU.add, op1=ALU.mult)
                    ins.then_inc(row_scored, 1)
                    eng.wait_ge(row_scored, 3 * i + 1)
                    apart(eng)
                    eng.scalar_tensor_tensor(out=score_row, in0=adj_row, scalar=2.0, in1=score_row,
                                             op0=ALU.mult, op1=ALU.add).then_inc(row_scored, 1)
                    eng.wait_ge(row_masked, 2 * i + 2)
                    eng.wait_ge(row_scored, 3 * i + 2)
                    apart(eng)
                    eng.tensor_tensor(score_row, score_row, fac_row, ALU.mult).then_inc(row_scored, 1)
                    eng.wait_ge(row_scored, 3 * i + 3)
                    apart(eng)
                    eng.tensor_reduce(neg_m[:, 0:1], score_row, AX, ALU.max, negate=True) \
                       .then_inc(row_m_ready, 1)
                    eng.wait_ge(row_p_ready, i + 1)
                    apart(eng)
                    eng.reciprocal(rz[:, 0:1], zw[:, 0:1])
                    eng.tensor_tensor(score_row, prob_row, mask_row[:, :], ALU.mult).then_inc(row_pm_ready, 1)
                    eng.wait_ge(row_pv_summed, i + 1)
                    apart(eng)
                    eng.scalar_tensor_tensor(out=o_sb[:, 0, :], in0=bank[4][:, 0:D], scalar=rz[:, 0:1],
                                             in1=x1_all[:, bass.ds(i * D, D)], op0=ALU.mult, op1=ALU.add) \
                       .then_inc(row_o_ready, 1)


_INPUTS = ["x", "adj", "adj_t", "L0_gnn_W_sa", "L0_gnn_a_sa", "L0_gnn_W_gcnb", "L0_gnn_b_gcnb", "gate_w",
           "gate_b", "L1_gnn_ptr", "L1_gnn_Wq", "L1_gnn_Wk", "WvT", "bq_bk", "L1_gnn_bv"]


def kernel(**inputs):
    import numpy as np
    import concourse.bacc as bacc
    from concourse.bass_utils import run_bass_kernel_spmd

    given = {name: np.ascontiguousarray(a) for name, a in inputs.items()}
    given["adj_t"] = np.ascontiguousarray(given["adj"].T)
    given["WvT"] = np.ascontiguousarray(given["L1_gnn_Wv"].T)
    both = np.stack([given["L0_gnn_Wa"].reshape(2, -1, P), given["L0_gnn_Wb"].reshape(2, -1, P)], axis=1)
    given["gate_w"] = np.ascontiguousarray(both.transpose(3, 2, 0, 1).reshape(P, -1, 4))
    given["gate_b"] = np.concatenate([given["L0_gnn_ba"], given["L0_gnn_bb"]])
    biases = np.stack([given["L1_gnn_bq"].reshape(-1, P), given["L1_gnn_bk"].reshape(-1, P)])
    given["bq_bk"] = np.ascontiguousarray(biases.transpose(2, 1, 0))

    nc = bacc.Bacc("TRN2", target_bir_lowering=False, num_devices=1)
    arrays, args = {}, []
    for name in _INPUTS:
        arrays[f"in_{name}"] = given[name]
        args.append(nc.dram_tensor(f"in_{name}", given[name].shape, mybir.dt.from_np(given[name].dtype),
                                   kind="ExternalInput").ap())
    args.append(nc.dram_tensor("out", given["x"].shape, F32, kind="ExternalOutput").ap())
    two_graph_layers(nc, *args)
    return run_bass_kernel_spmd(nc, [arrays], core_ids=[0]).results[0]["out"]
```
